# Optimizing a Trainium2 kernel written in Bass

```python
import numpy as np
import jax
import jax.numpy as jnp

def _softmax(x, axis=-1):
    return jax.nn.softmax(x, axis=axis)

def _gelu(x):
    return jax.nn.gelu(x, approximate=True)

def _silu(x):
    return jax.nn.silu(x)

def _sigmoid(x):
    return jax.nn.sigmoid(x)

def _layernorm(x, axis=-1, eps=1e-05):
    m = jnp.mean(x, axis=axis, keepdims=True)
    v = jnp.var(x, axis=axis, keepdims=True)
    return (x - m) / jnp.sqrt(v + eps)

def _scatter_add(tgt, idx, src, axis=0):
    return tgt.at[idx].add(src)

def _segment_sum(src, seg, n):
    return jax.ops.segment_sum(src, seg, n)
kernel_name = 'mk_xattn_seq_d2_seqx_r8_81db83'

def setup_inputs(seed: int=0):
    np.random.seed(seed)
    _w = jnp.asarray

    def _rec_inputs():
        import jax
        import jax.numpy as jnp
        _rk = jax.random.key(seed)
        x = -0.0002928 + 1 * jax.random.normal(jax.random.fold_in(_rk, 1), (64, 64, 256), jnp.float32)
        _lenS = 64 - jax.random.randint(jax.random.fold_in(_rk, 7), (64,), 0, max(1, 64 // 4) + 1, jnp.int32)
        _lenS2 = 64 - jax.random.randint(jax.random.fold_in(_rk, 8), (64,), 0, max(1, 64 // 4) + 1, jnp.int32)
        _ctx_2048P = jax.random.normal(jax.random.fold_in(_rk, 11), (64, 16, 256), jnp.float32)
        _ctx_2048c = jax.random.dirichlet(jax.random.fold_in(_rk, 511), 0.3 * jnp.ones((16,), jnp.float32), (64, 64))
        _ctx_2048t = jnp.einsum('bsk,bkd->bsd', _ctx_2048c, _ctx_2048P)
        _ctx_2048t = _ctx_2048t * jax.lax.rsqrt(jnp.mean(jnp.square(_ctx_2048t)) + 1e-12) * 0.953939
        ctx_2048 = -1.39393e-06 + 0.999914 * (_ctx_2048t + 0.3 * jax.random.normal(jax.random.fold_in(_rk, 611), (64, 64, 256), jnp.float32))
        _validS = jnp.arange(64)[None, :] < _lenS[:, None]
        _validS2 = jnp.arange(64)[None, :] < _lenS2[:, None]
        _causal = jnp.tril(jnp.ones((64, 64), dtype=bool))
        mask_1x1xSxS2_fc1 = jnp.where(jnp.broadcast_to(_validS2[0:1, None, None, :], (1, 1, 64, 64)), 1.0, 0.0).astype(jnp.float32)
        mask_Bx1xSxS2_ff1 = jnp.where(jnp.ones((64, 1, 64, 64), dtype=bool), 1.0, 0.0).astype(jnp.float32)
        return (x, ctx_2048, mask_1x1xSxS2_fc1, mask_Bx1xSxS2_ff1)
    x, ctx_2048, mask_1x1xSxS2_fc1, mask_Bx1xSxS2_ff1 = _rec_inputs()

    def _L0_xattn_setup():
        import jax, jax.numpy as jnp
        import numpy as np
        H = 256
        NH = 16
        HD = H // NH
        EPS = 1e-05

        def gelu(x):
            return 0.5 * x * (1.0 + jnp.tanh(0.7978845608028654 * x * (1.0 + 0.044715 * x * x)))

        def layernorm(x, scale, bias):
            m = jnp.mean(x, axis=-1, keepdims=True)
            v = jnp.mean(jnp.square(x - m), axis=-1, keepdims=True)
            return (x - m) * jax.lax.rsqrt(v + EPS) * scale + bias

        def split_heads(x):
            b, s, _ = x.shape
            return x.reshape(b, s, NH, HD).transpose(0, 2, 1, 3)

        def merge_heads(x):
            b, nh, s, hd = x.shape
            return x.transpose(0, 2, 1, 3).reshape(b, s, nh * hd)

        def attention(q, k, v, mask):
            scores = jnp.einsum('bhqd,bhkd->bhqk', q, k) / jnp.sqrt(jnp.float32(HD))
            scores = scores * mask - 10000.0 * (1.0 - mask)
            probs = jax.nn.softmax(scores, axis=-1)
            return jnp.einsum('bhqk,bhkd->bhqd', probs, v)
        key = jax.random.key(seed)
        ks = jax.random.split(key, 16)
        b, s, t = (2, 128, 128)
        w = lambda k, i, o: jax.random.normal(k, (i, o), jnp.float32) * 0.02
        inp = {'hidden_states': jax.random.normal(ks[0], (b, s, H), jnp.float32), 'encoder_states': jax.random.normal(ks[1], (b, t, H), jnp.float32), 'ltor_mask': jnp.tril(jnp.ones((1, 1, s, s), jnp.float32)), 'cross_mask': jnp.ones((b, 1, s, t), jnp.float32), 'ln1_s': jnp.ones((H,), jnp.float32), 'ln1_b': jnp.zeros((H,), jnp.float32), 'w_qkv': w(ks[2], H, 3 * H), 'b_qkv': jnp.zeros((3 * H,), jnp.float32), 'w_ao': w(ks[3], H, H), 'b_ao': jnp.zeros((H,), jnp.float32), 'ln2_s': jnp.ones((H,), jnp.float32), 'ln2_b': jnp.zeros((H,), jnp.float32), 'w_q': w(ks[4], H, H), 'b_q': jnp.zeros((H,), jnp.float32), 'w_kv': w(ks[5], H, 2 * H), 'b_kv': jnp.zeros((2 * H,), jnp.float32), 'w_co': w(ks[6], H, H), 'b_co': jnp.zeros((H,), jnp.float32), 'ln3_s': jnp.ones((H,), jnp.float32), 'ln3_b': jnp.zeros((H,), jnp.float32), 'w1': w(ks[7], H, 4 * H), 'b1': jnp.zeros((4 * H,), jnp.float32), 'w2': w(ks[8], 4 * H, H), 'b2': jnp.zeros((H,), jnp.float32)}
        return inp
    _L0_xattn_all = _L0_xattn_setup()
    _L0_xattn_in = {k: v for k, v in _L0_xattn_all.items() if k in ('ln1_s', 'ln1_b', 'w_qkv', 'b_qkv', 'w_ao', 'b_ao', 'ln2_s', 'ln2_b', 'w_q', 'b_q', 'w_kv', 'b_kv', 'w_co', 'b_co', 'ln3_s', 'ln3_b', 'w1', 'b1', 'w2', 'b2')}
    del _L0_xattn_all

    def _L1_xattn_setup():
        import jax, jax.numpy as jnp
        import numpy as np
        E, H, L, B = (256, 32, 128, 4)
        S = E // H
        DM, DD = (32, 64)

        def _ln(x, w, b, eps=1e-05):
            m = x.mean(-1, keepdims=True)
            v = ((x - m) ** 2).mean(-1, keepdims=True)
            return (x - m) / jnp.sqrt(v + eps) * w + b

        def _block(x, state, ln1_w, ln1_b, ln2_w, ln2_b, maa_x, maa_w1, maa_w2, maa_stack, time_decay, td_w1, td_w2, u, Wr, Wk, Wv, Wg, Wo, gn_w, gn_b, ffn_maa_k, ffn_maa_r, Wfk, Wfr, Wfv):
            b, l, e = x.shape
            h = u.shape[0]
            s_ = e // h
            xa = _ln(x, ln1_w, ln1_b)
            sx = jnp.concatenate([state[:, 1:2] - xa[:, :1], xa[:, :-1] - xa[:, 1:]], axis=1)
            xxx = jnp.tanh((xa + sx * maa_x) @ maa_w1).reshape(b, l, 5, DM)
            xxx = jnp.einsum('blfd,fde->blfe', xxx, maa_w2)
            xm = xa[:, :, None] + sx[:, :, None] * (maa_stack + xxx)
            xk, xw, xv, xr, xg = (xm[:, :, j] for j in range(5))
            w = jnp.exp(-jnp.exp(time_decay + jnp.tanh(xw @ td_w1) @ td_w2)).reshape(b, l, h, s_)
            r = (xr @ Wr.T).reshape(b, l, h, s_)
            k = (xk @ Wk.T).reshape(b, l, h, s_)
            v = (xv @ Wv.T).reshape(b, l, h, s_)
            g = jax.nn.silu(xg @ Wg.T)
            s0 = state[:, 2:2 + s_].reshape(b, h, s_, s_)

            def step(s, rkvw):
                r_t, k_t, v_t, w_t = rkvw
                a = k_t[..., :, None] * v_t[..., None, :]
                out = jnp.einsum('bhi,bhij->bhj', r_t, u * a + s)
                s = a + w_t[..., :, None] * s
                return (s, out)
            rkvw = tuple((jnp.moveaxis(t, 1, 0) for t in (r, k, v, w)))
            _, out = jax.lax.scan(step, s0, rkvw)
            out = jnp.moveaxis(out, 0, 1).reshape(b, l, e)
            og = out.reshape(b, l, h, s_)
            m = og.mean(-1, keepdims=True)
            va = ((og - m) ** 2).mean(-1, keepdims=True)
            og = ((og - m) / jnp.sqrt(va + 1e-05)).reshape(b, l, e) * gn_w + gn_b
            x1 = x + og * g @ Wo.T
            xc = _ln(x1, ln2_w, ln2_b)
            sx2 = jnp.concatenate([state[:, 0:1] - xc[:, :1], xc[:, :-1] - xc[:, 1:]], axis=1)
            xk2 = xc + sx2 * ffn_maa_k
            xr2 = xc + sx2 * ffn_maa_r
            rr = jax.nn.sigmoid(xr2 @ Wfr.T)
            kk = jnp.square(jax.nn.relu(xk2 @ Wfk.T))
            return x1 + rr * (kk @ Wfv.T)
        key = jax.random.key(seed)
        ks = jax.random.split(key, 24)
        sc = 0.02
        d = {'x': jax.random.normal(ks[0], (B, L, E), jnp.float32), 'state': jax.random.normal(ks[1], (B, 2 + S, E), jnp.float32) * 0.1, 'ln1_w': jnp.ones((E,), jnp.float32), 'ln1_b': jnp.zeros((E,), jnp.float32), 'ln2_w': jnp.ones((E,), jnp.float32), 'ln2_b': jnp.zeros((E,), jnp.float32), 'maa_x': jax.random.normal(ks[2], (E,), jnp.float32) * 0.1, 'maa_w1': jax.random.normal(ks[3], (E, 5 * DM), jnp.float32) * sc, 'maa_w2': jax.random.normal(ks[4], (5, DM, E), jnp.float32) * sc, 'maa_stack': jax.random.normal(ks[5], (1, 5, E), jnp.float32) * 0.1, 'time_decay': jax.random.normal(ks[6], (E,), jnp.float32) * 0.5, 'td_w1': jax.random.normal(ks[7], (E, DD), jnp.float32) * sc, 'td_w2': jax.random.normal(ks[8], (DD, E), jnp.float32) * sc, 'u': jax.random.normal(ks[9], (H, S, 1), jnp.float32) * 0.1, 'Wr': jax.random.normal(ks[10], (E, E), jnp.float32) * sc, 'Wk': jax.random.normal(ks[11], (E, E), jnp.float32) * sc, 'Wv': jax.random.normal(ks[12], (E, E), jnp.float32) * sc, 'Wg': jax.random.normal(ks[13], (E, E), jnp.float32) * sc, 'Wo': jax.random.normal(ks[14], (E, E), jnp.float32) * sc, 'gn_w': jnp.ones((E,), jnp.float32), 'gn_b': jnp.zeros((E,), jnp.float32), 'ffn_maa_k': jax.random.normal(ks[15], (E,), jnp.float32) * 0.1, 'ffn_maa_r': jax.random.normal(ks[16], (E,), jnp.float32) * 0.1, 'Wfk': jax.random.normal(ks[17], (E, E), jnp.float32) * sc, 'Wfr': jax.random.normal(ks[18], (E, E), jnp.float32) * sc, 'Wfv': jax.random.normal(ks[19], (E, E), jnp.float32) * sc}
        return d
    _L1_xattn_all = _L1_xattn_setup()
    _L1_xattn_in = {k: v for k, v in _L1_xattn_all.items() if k in ('ln1_w', 'ln1_b', 'ln2_w', 'ln2_b', 'maa_x', 'maa_w1', 'maa_w2', 'maa_stack', 'time_decay', 'td_w1', 'td_w2', 'u', 'Wr', 'Wk', 'Wv', 'Wg', 'Wo', 'gn_w', 'gn_b', 'ffn_maa_k', 'ffn_maa_r', 'Wfk', 'Wfr', 'Wfv')}
    del _L1_xattn_all
    return {'x': x, 'ctx_2048': ctx_2048, 'mask_1x1xSxS2_fc1': mask_1x1xSxS2_fc1, 'mask_Bx1xSxS2_ff1': mask_Bx1xSxS2_ff1, 'L0_xattn_ln1_s': _L0_xattn_in['ln1_s'], 'L0_xattn_ln1_b': _L0_xattn_in['ln1_b'], 'L0_xattn_w_qkv': _L0_xattn_in['w_qkv'], 'L0_xattn_b_qkv': _L0_xattn_in['b_qkv'], 'L0_xattn_w_ao': _L0_xattn_in['w_ao'], 'L0_xattn_b_ao': _L0_xattn_in['b_ao'], 'L0_xattn_ln2_s': _L0_xattn_in['ln2_s'], 'L0_xattn_ln2_b': _L0_xattn_in['ln2_b'], 'L0_xattn_w_q': _L0_xattn_in['w_q'], 'L0_xattn_b_q': _L0_xattn_in['b_q'], 'L0_xattn_w_kv': _L0_xattn_in['w_kv'], 'L0_xattn_b_kv': _L0_xattn_in['b_kv'], 'L0_xattn_w_co': _L0_xattn_in['w_co'], 'L0_xattn_b_co': _L0_xattn_in['b_co'], 'L0_xattn_ln3_s': _L0_xattn_in['ln3_s'], 'L0_xattn_ln3_b': _L0_xattn_in['ln3_b'], 'L0_xattn_w1': _L0_xattn_in['w1'], 'L0_xattn_b1': _L0_xattn_in['b1'], 'L0_xattn_w2': _L0_xattn_in['w2'], 'L0_xattn_b2': _L0_xattn_in['b2'], 'L1_xattn_ln1_w': _L1_xattn_in['ln1_w'], 'L1_xattn_ln1_b': _L1_xattn_in['ln1_b'], 'L1_xattn_ln2_w': _L1_xattn_in['ln2_w'], 'L1_xattn_ln2_b': _L1_xattn_in['ln2_b'], 'L1_xattn_maa_x': _L1_xattn_in['maa_x'], 'L1_xattn_maa_w1': _L1_xattn_in['maa_w1'], 'L1_xattn_maa_w2': _L1_xattn_in['maa_w2'], 'L1_xattn_maa_stack': _L1_xattn_in['maa_stack'], 'L1_xattn_time_decay': _L1_xattn_in['time_decay'], 'L1_xattn_td_w1': _L1_xattn_in['td_w1'], 'L1_xattn_td_w2': _L1_xattn_in['td_w2'], 'L1_xattn_u': _L1_xattn_in['u'], 'L1_xattn_Wr': _L1_xattn_in['Wr'], 'L1_xattn_Wk': _L1_xattn_in['Wk'], 'L1_xattn_Wv': _L1_xattn_in['Wv'], 'L1_xattn_Wg': _L1_xattn_in['Wg'], 'L1_xattn_Wo': _L1_xattn_in['Wo'], 'L1_xattn_gn_w': _L1_xattn_in['gn_w'], 'L1_xattn_gn_b': _L1_xattn_in['gn_b'], 'L1_xattn_ffn_maa_k': _L1_xattn_in['ffn_maa_k'], 'L1_xattn_ffn_maa_r': _L1_xattn_in['ffn_maa_r'], 'L1_xattn_Wfk': _L1_xattn_in['Wfk'], 'L1_xattn_Wfr': _L1_xattn_in['Wfr'], 'L1_xattn_Wfv': _L1_xattn_in['Wfv']}

def reference(x, ctx_2048, mask_1x1xSxS2_fc1, mask_Bx1xSxS2_ff1, L0_xattn_ln1_s, L0_xattn_ln1_b, L0_xattn_w_qkv, L0_xattn_b_qkv, L0_xattn_w_ao, L0_xattn_b_ao, L0_xattn_ln2_s, L0_xattn_ln2_b, L0_xattn_w_q, L0_xattn_b_q, L0_xattn_w_kv, L0_xattn_b_kv, L0_xattn_w_co, L0_xattn_b_co, L0_xattn_ln3_s, L0_xattn_ln3_b, L0_xattn_w1, L0_xattn_b1, L0_xattn_w2, L0_xattn_b2, L1_xattn_ln1_w, L1_xattn_ln1_b, L1_xattn_ln2_w, L1_xattn_ln2_b, L1_xattn_maa_x, L1_xattn_maa_w1, L1_xattn_maa_w2, L1_xattn_maa_stack, L1_xattn_time_decay, L1_xattn_td_w1, L1_xattn_td_w2, L1_xattn_u, L1_xattn_Wr, L1_xattn_Wk, L1_xattn_Wv, L1_xattn_Wg, L1_xattn_Wo, L1_xattn_gn_w, L1_xattn_gn_b, L1_xattn_ffn_maa_k, L1_xattn_ffn_maa_r, L1_xattn_Wfk, L1_xattn_Wfr, L1_xattn_Wfv):
    import jax
    import jax.numpy as jnp

    def _L0_xattn_ref(hidden_states, encoder_states, ltor_mask, cross_mask, ln1_s, ln1_b, w_qkv, b_qkv, w_ao, b_ao, ln2_s, ln2_b, w_q, b_q, w_kv, b_kv, w_co, b_co, ln3_s, ln3_b, w1, b1, w2, b2):
        import jax, jax.numpy as jnp
        import numpy as np
        H = 256
        NH = 16
        HD = H // NH
        EPS = 1e-05

        def gelu(x):
            return 0.5 * x * (1.0 + jnp.tanh(0.7978845608028654 * x * (1.0 + 0.044715 * x * x)))

        def layernorm(x, scale, bias):
            m = jnp.mean(x, axis=-1, keepdims=True)
            v = jnp.mean(jnp.square(x - m), axis=-1, keepdims=True)
            return (x - m) * jax.lax.rsqrt(v + EPS) * scale + bias

        def split_heads(x):
            b, s, _ = x.shape
            return x.reshape(b, s, NH, HD).transpose(0, 2, 1, 3)

        def merge_heads(x):
            b, nh, s, hd = x.shape
            return x.transpose(0, 2, 1, 3).reshape(b, s, nh * hd)

        def attention(q, k, v, mask):
            scores = jnp.einsum('bhqd,bhkd->bhqk', q, k) / jnp.sqrt(jnp.float32(HD))
            scores = scores * mask - 10000.0 * (1.0 - mask)
            probs = jax.nn.softmax(scores, axis=-1)
            return jnp.einsum('bhqk,bhkd->bhqd', probs, v)
        ln_out = layernorm(hidden_states, ln1_s, ln1_b)
        qkv = ln_out @ w_qkv + b_qkv
        q, k, v = jnp.split(qkv, 3, axis=-1)
        ctx = merge_heads(attention(split_heads(q), split_heads(k), split_heads(v), ltor_mask))
        attn_out = ctx @ w_ao + b_ao
        x = hidden_states + attn_out
        ln_out = layernorm(x, ln2_s, ln2_b)
        q = ln_out @ w_q + b_q
        kv = encoder_states @ w_kv + b_kv
        k, v = jnp.split(kv, 2, axis=-1)
        ctx = merge_heads(attention(split_heads(q), split_heads(k), split_heads(v), cross_mask))
        cross_out = ctx @ w_co + b_co
        x = x + cross_out
        ln_out = layernorm(x, ln3_s, ln3_b)
        mlp_out = gelu(ln_out @ w1 + b1) @ w2 + b2
        return x + mlp_out

    def _L1_xattn_ref(x, state, ln1_w, ln1_b, ln2_w, ln2_b, maa_x, maa_w1, maa_w2, maa_stack, time_decay, td_w1, td_w2, u, Wr, Wk, Wv, Wg, Wo, gn_w, gn_b, ffn_maa_k, ffn_maa_r, Wfk, Wfr, Wfv):
        import jax, jax.numpy as jnp
        import numpy as np
        E, H, L, B = (256, 32, 128, 4)
        S = E // H
        DM, DD = (32, 64)

        def _ln(x, w, b, eps=1e-05):
            m = x.mean(-1, keepdims=True)
            v = ((x - m) ** 2).mean(-1, keepdims=True)
            return (x - m) / jnp.sqrt(v + eps) * w + b

        def _block(x, state, ln1_w, ln1_b, ln2_w, ln2_b, maa_x, maa_w1, maa_w2, maa_stack, time_decay, td_w1, td_w2, u, Wr, Wk, Wv, Wg, Wo, gn_w, gn_b, ffn_maa_k, ffn_maa_r, Wfk, Wfr, Wfv):
            b, l, e = x.shape
            h = u.shape[0]
            s_ = e // h
            xa = _ln(x, ln1_w, ln1_b)
            sx = jnp.concatenate([state[:, 1:2] - xa[:, :1], xa[:, :-1] - xa[:, 1:]], axis=1)
            xxx = jnp.tanh((xa + sx * maa_x) @ maa_w1).reshape(b, l, 5, DM)
            xxx = jnp.einsum('blfd,fde->blfe', xxx, maa_w2)
            xm = xa[:, :, None] + sx[:, :, None] * (maa_stack + xxx)
            xk, xw, xv, xr, xg = (xm[:, :, j] for j in range(5))
            w = jnp.exp(-jnp.exp(time_decay + jnp.tanh(xw @ td_w1) @ td_w2)).reshape(b, l, h, s_)
            r = (xr @ Wr.T).reshape(b, l, h, s_)
            k = (xk @ Wk.T).reshape(b, l, h, s_)
            v = (xv @ Wv.T).reshape(b, l, h, s_)
            g = jax.nn.silu(xg @ Wg.T)
            s0 = state[:, 2:2 + s_].reshape(b, h, s_, s_)

            def step(s, rkvw):
                r_t, k_t, v_t, w_t = rkvw
                a = k_t[..., :, None] * v_t[..., None, :]
                out = jnp.einsum('bhi,bhij->bhj', r_t, u * a + s)
                s = a + w_t[..., :, None] * s
                return (s, out)
            rkvw = tuple((jnp.moveaxis(t, 1, 0) for t in (r, k, v, w)))
            _, out = jax.lax.scan(step, s0, rkvw)
            out = jnp.moveaxis(out, 0, 1).reshape(b, l, e)
            og = out.reshape(b, l, h, s_)
            m = og.mean(-1, keepdims=True)
            va = ((og - m) ** 2).mean(-1, keepdims=True)
            og = ((og - m) / jnp.sqrt(va + 1e-05)).reshape(b, l, e) * gn_w + gn_b
            x1 = x + og * g @ Wo.T
            xc = _ln(x1, ln2_w, ln2_b)
            sx2 = jnp.concatenate([state[:, 0:1] - xc[:, :1], xc[:, :-1] - xc[:, 1:]], axis=1)
            xk2 = xc + sx2 * ffn_maa_k
            xr2 = xc + sx2 * ffn_maa_r
            rr = jax.nn.sigmoid(xr2 @ Wfr.T)
            kk = jnp.square(jax.nn.relu(xk2 @ Wfk.T))
            return x1 + rr * (kk @ Wfv.T)
        return _block(x, state, ln1_w, ln1_b, ln2_w, ln2_b, maa_x, maa_w1, maa_w2, maa_stack, time_decay, td_w1, td_w2, u, Wr, Wk, Wv, Wg, Wo, gn_w, gn_b, ffn_maa_k, ffn_maa_r, Wfk, Wfr, Wfv)
    x = _L0_xattn_ref(x, ctx_2048, mask_1x1xSxS2_fc1, mask_Bx1xSxS2_ff1, L0_xattn_ln1_s, L0_xattn_ln1_b, L0_xattn_w_qkv, L0_xattn_b_qkv, L0_xattn_w_ao, L0_xattn_b_ao, L0_xattn_ln2_s, L0_xattn_ln2_b, L0_xattn_w_q, L0_xattn_b_q, L0_xattn_w_kv, L0_xattn_b_kv, L0_xattn_w_co, L0_xattn_b_co, L0_xattn_ln3_s, L0_xattn_ln3_b, L0_xattn_w1, L0_xattn_b1, L0_xattn_w2, L0_xattn_b2)
    x = _L1_xattn_ref(x, ctx_2048, L1_xattn_ln1_w, L1_xattn_ln1_b, L1_xattn_ln2_w, L1_xattn_ln2_b, L1_xattn_maa_x, L1_xattn_maa_w1, L1_xattn_maa_w2, L1_xattn_maa_stack, L1_xattn_time_decay, L1_xattn_td_w1, L1_xattn_td_w2, L1_xattn_u, L1_xattn_Wr, L1_xattn_Wk, L1_xattn_Wv, L1_xattn_Wg, L1_xattn_Wo, L1_xattn_gn_w, L1_xattn_gn_b, L1_xattn_ffn_maa_k, L1_xattn_ffn_maa_r, L1_xattn_Wfk, L1_xattn_Wfr, L1_xattn_Wfv)
    return x

_drawn_inputs = setup_inputs


def setup_inputs(seed=0):
    import zlib

    import numpy as np

    out = dict(_drawn_inputs(seed))
    spreads = {'L0_xattn_ln1_s': (1.0, 0.6),
     'L0_xattn_ln1_b': (0.0, 0.758),
     'L0_xattn_b_qkv': (0.0, 0.269),
     'L0_xattn_b_ao': (0.0, 0.1),
     'L0_xattn_ln2_s': (1.0, 0.6),
     'L0_xattn_ln2_b': (0.0, 2.0),
     'L0_xattn_b_q': (0.0, 2.0),
     'L0_xattn_b_kv': (0.0, 0.28),
     'L0_xattn_b_co': (0.0, 0.1),
     'L0_xattn_ln3_s': (1.0, 0.6),
     'L0_xattn_ln3_b': (0.0, 0.649),
     'L0_xattn_b1': (0.0, 0.1),
     'L0_xattn_b2': (0.0, 0.1),
     'L1_xattn_ln1_w': (1.0, 0.6),
     'L1_xattn_ln1_b': (0.0, 0.572),
     'L1_xattn_ln2_w': (1.0, 0.6),
     'L1_xattn_ln2_b': (0.0, 0.8),
     'L1_xattn_gn_w': (1.0, 0.6),
     'L1_xattn_gn_b': (0.0, 0.8)}
    factors = {'L0_xattn_w_qkv': 3.092,
     'L0_xattn_w_q': 8.0,
     'L1_xattn_maa_x': 8.0,
     'L1_xattn_maa_w1': 7.909,
     'L1_xattn_maa_w2': 7.928,
     'L1_xattn_maa_stack': 2.904,
     'L1_xattn_time_decay': 2.806,
     'L1_xattn_td_w1': 8.0,
     'L1_xattn_td_w2': 8.0,
     'L1_xattn_u': 5.943,
     'L1_xattn_ffn_maa_k': 8.0,
     'L1_xattn_ffn_maa_r': 8.0,
     'L1_xattn_Wfk': 2.888,
     'L1_xattn_Wfr': 8.0,
     'L1_xattn_Wfv': 2.696}
    for name, (base, spread) in spreads.items():
        noise = np.random.default_rng([zlib.crc32(name.encode()), seed]).standard_normal(out[name].shape)
        drawn = base * np.exp(spread * noise) if base else spread * noise
        out[name] = jnp.asarray(drawn.astype(out[name].dtype))
    for name, factor in factors.items():
        out[name] = (out[name] * factor).astype(out[name].dtype)
    return out
```

```python
import concourse.bass as bass
from concourse import mybir
from contextlib import ExitStack
import numpy as np

FP32 = mybir.dt.float32
ALU = mybir.AluOpType
ACT = mybir.ActivationFunctionType
AX = mybir.AxisListType

B, S, C = 64, 64, 256
P = 128
HALVES = C // P
TILES = B * S // P
BPT = P // S
NH, HD = 16, 16
PAIRS = NH // 2
GROUPS = P // 32
PW = 2 * HD + 2
F1 = 4 * C
EPS = 1e-5
MASKED = 10000.0
RH, RS = 32, 8
HPH = RH // HALVES
DM, DD, NMIX = 32, 64, 5

COLS = {}
for _name, _n in (("ln1_s", 2), ("ln1_b", 2), ("b_q_self", 2), ("b_k_self", 2), ("b_v_self", 2),
                  ("ln2_s", 2), ("ln2_b", 2), ("b_q_cross", 2), ("b_k_cross", 2), ("b_v_cross", 2),
                  ("ln3_s", 2), ("ln3_b", 2), ("b1", 8), ("r_ln1_w", 2), ("r_ln1_b", 2),
                  ("r_ln2_w", 2), ("r_ln2_b", 2), ("maa_x", 2), ("maa_stack", 2 * NMIX),
                  ("time_decay", 2), ("u", 2), ("gn_w", 2), ("gn_b", 2), ("ffn_maa_k", 2),
                  ("ffn_maa_r", 2)):
    COLS[_name] = (sum(n for _, n in COLS.values()), _n)
NCOLS = sum(n for _, n in COLS.values())


def ds(t, n):
    return bass.ds(t * n, n)


def later(n):
    return not isinstance(n, int) or n > 0


class Core:
    pass


def semaphores(nc, ctx, *names):
    return [ctx.enter_context(nc.semaphore(n)) for n in names]


def col(core, name, i):
    return core.cols[:, COLS[name][0] + i:COLS[name][0] + i + 1]


def load_phase(core, dram):
    nc = core.nc
    with ExitStack() as ctx:
        loaded, prepared = semaphores(nc, ctx, "loaded", "prepared")
        block = ctx.enter_context(nc.Block())
        loads = [(core.x[:, :], dram["x"]), (core.cols[:, :], dram["cols"]), (core.ident[:, :], dram["ident"]),
                 (core.parity[:, :], dram["parity"]),
                 (core.self_mask[:, :], dram["self_mask"]), (core.cross_mask[:, :], dram["cross_mask"])]
        for name in FIRST_WEIGHTS:
            loads.append((core.weights[name][:, :], dram[name]))
        for n in range(3):
            loads.append((core.rows[:, n, :], dram["rows"][n:n + 1, :].partition_broadcast(P)))
        split = len(loads) // 2

        @block.sync
        def _(sp):
            for dst, src in loads[:split]:
                sp.dma_start(dst, src).then_inc(loaded, 16)
            sp.wait_ge(loaded, 16 * len(loads))

        @block.gpsimd
        def _(pool):
            nc.gpsimd.memset(core.vpad[:, :, :, :], 0.0).then_inc(prepared, 1)
            nc.gpsimd.memset(core.eps[:, :], EPS).then_inc(prepared, 1)
            pool.wait_ge(prepared, 2)
            nc.gpsimd.memset(core.vpad[0:S, :, :, 2 * HD:2 * HD + 1], 1.0).then_inc(prepared, 1)
            nc.gpsimd.memset(core.vpad[S:P, :, :, 2 * HD + 1:PW], 1.0).then_inc(prepared, 1)
            pool.wait_ge(prepared, 4)

        @block.scalar
        def _(act):
            for dst, src in loads[split:]:
                act.dma_start(dst, src).then_inc(loaded, 16)


        @block.vector
        def _(dve):
            dve.wait_ge(loaded, 16 * len(loads))
            for n, (q, k) in enumerate((("b_q_self", "b_k_self"), ("b_q_cross", "b_k_cross"))):
                a = COLS[q][0]
                nc.vector.tensor_scalar_mul(core.q_bias[:, n, :], core.cols[:, a:a + 2], HD ** -0.5)
                for half in range(HALVES):
                    nc.vector.tensor_scalar(core.k_bias[:, n, half, :], core.parity[:, :], col(core, k, half),
                                            None, ALU.mult)
            for bias, mask in ((core.self_bias, core.self_mask), (core.cross_bias, core.cross_mask)):
                nc.vector.tensor_scalar(bias[:, :], mask[:, :], -1.0, MASKED, ALU.add, ALU.mult)

    with ExitStack() as ctx:
        [stats_of] = semaphores(nc, ctx, "first_stats")
        block = ctx.enter_context(nc.Block())

        @block.vector
        def _(dve):
            with dve.Fori(0, TILES) as t:
                nc.vector.bn_stats(core.stats[:, ds(t, 6)], core.x[:, ds(t, C)])


def load_second_phase(core, dram):
    nc = core.nc
    with ExitStack() as ctx:
        [loaded] = semaphores(nc, ctx, "second_loaded")
        block = ctx.enter_context(nc.Block())
        loads = [(core.head_sum[:, :], dram["head_sum"]), (core.spread[:, :, :], dram["spread"]),
                 (core.maa_w2a[:, :], dram["maa_w2"][0:P, :]), (core.maa_w2b[:, :], dram["maa_w2"][P:P + DM, :]),
                 (core.td_w2[:, :], dram["td_w2"]), (core.state_rows[:, :, :, :], dram["state_rows"]),
                 (core.state0[:, :, :], dram["state0"])]
        loads += [(core.weights[name][:, :], dram[name]) for name in SECOND_WEIGHTS]

        @block.sync
        def _(sp):
            for dst, src in loads[0::2]:
                sp.dma_start(dst, src).then_inc(loaded, 16)
            sp.wait_ge(loaded, 16 * len(loads))

        @block.scalar
        def _(act):
            for dst, src in loads[1::2]:
                act.dma_start(dst, src).then_inc(loaded, 16)


def norm_phase(core, name):
    nc = core.nc
    with ExitStack() as ctx:
        step, var_ready, std_ready = semaphores(nc, ctx, f"{name}_step", f"{name}_var_ready", f"{name}_std_ready")
        block = ctx.enter_context(nc.Block())
        st = core.stats[:, :].rearrange("p (t s) -> p t s", s=6)
        mean_even, m2_even, mean_odd, m2_odd = (st[:, :, i] for i in (1, 2, 4, 5))
        a, b, c = (core.norm_tmp[:, i, :] for i in range(3))

        @block.vector
        def _(dve):
            nc.vector.tensor_tensor(a, m2_even, m2_odd, ALU.add)
            nc.vector.tensor_tensor(b, mean_even, mean_odd, ALU.subtract)
            nc.vector.tensor_tensor(core.neg_mean[:, :], mean_even, mean_odd, ALU.add).then_inc(step, 1)
            dve.wait_ge(step, 1)
            nc.vector.tensor_tensor(b, b, b, ALU.mult).then_inc(step, 1)
            dve.wait_ge(step, 2)
            nc.vector.tensor_scalar(b, b, 0.25, None, ALU.mult).then_inc(step, 1)
            dve.wait_ge(step, 3)
            nc.vector.scalar_tensor_tensor(out=c, in0=a, scalar=1.0 / C, in1=b, op0=ALU.mult,
                                           op1=ALU.add).then_inc(var_ready, 1)
            dve.wait_ge(std_ready, 1)
            nc.vector.reciprocal(core.rstd[:, :], a).then_inc(step, 1)
            dve.wait_ge(step, 4)
            nc.vector.scalar_tensor_tensor(out=core.neg_mean[:, :], in0=core.neg_mean[:, :], scalar=-0.5,
                                           in1=core.rstd[:, :], op0=ALU.mult, op1=ALU.mult)

        @block.scalar
        def _(act):
            act.wait_ge(var_ready, 1)
            nc.scalar.activation(a, c, ACT.Sqrt, bias=core.eps[:, :]).then_inc(std_ready, 1)


def attention_phase(core, cross):
    nc = core.nc
    kind = "cross" if cross else "self"
    n = int(cross)
    ln_s, ln_b = ("ln2_s", "ln2_b") if cross else ("ln1_s", "ln1_b")
    wq, q0 = (core.w["w_q"], 0) if cross else (core.w["w_qkv"], 0)
    wk, k0 = (core.w["w_kv"], 0) if cross else (core.w["w_qkv"], C)
    wv, v0 = (core.w["w_kv"], C) if cross else (core.w["w_qkv"], 2 * C)
    wo = core.w["w_co"] if cross else core.w["w_ao"]
    with ExitStack() as ctx:
        def sb(name, shape):
            return ctx.enter_context(nc.sbuf_tensor(f"{kind}_{name}", shape, FP32))

        xn = sb("xn", [P, C])
        lnT = sb("lnT", [P, HALVES, 3 * S])
        qT = sb("qT", [P, HALVES, P])
        kT = sb("kT", [P, HALVES, 2, P])
        z = sb("z", [P, PAIRS, P])
        zT = sb("zT", [P, PAIRS, P])
        row_max = sb("row_max", [P, NH])
        recip = sb("recip", [P, NH])
        heads = sb("heads", [P, C])
        headsT = sb("headsT", [P, HALVES, P])
        if cross:
            encT = sb("encT", [P, HALVES, 3 * S])
        kvT = encT if cross else lnT

        tr, qk, vv, oo = (core.banks[i] for i in (0, 1, 2, 7))
        scores = core.psum[:, 3 * 512:7 * 512].rearrange("p (g n) -> p g n", n=512)
        pT = core.psum[:, 5 * 512:7 * 512]

        (xn_ready, xnT_ready, ln_ready, qk_ready, v_ready, q_copied, v_copied, scores_ready,
         masked, biased, max_ready, shifted, probs_ready, probsT_ready, probsT_copied, out_ready,
         recip_ready, heads_ready, headsT_ready, headsT_copied, proj_ready, x_ready, bias_added,
         ln_repeated, enc_loaded) = semaphores(
            nc, ctx, *(f"{kind}_{s}" for s in (
                "xn_ready", "xnT_ready", "ln_ready", "qk_ready", "v_ready", "q_copied", "v_copied",
                "scores_ready", "masked", "biased", "max_ready", "shifted", "probs_ready",
                "probsT_ready", "probsT_copied", "out_ready", "recip_ready", "heads_ready",
                "headsT_ready", "headsT_copied", "proj_ready", "x_ready", "bias_added",
                "ln_repeated", "enc_loaded")))
        block = ctx.enter_context(nc.Block())

        if cross:
            @block.sync
            def _(sp):
                def load(t):
                    sp.dma_start(encT[:, :, 0:P], core.dram["enc"][:, :, ds(t, P)]).then_inc(enc_loaded, 16)
                    sp.dma_start(encT[:, :, P:3 * S], core.dram["enc"][:, :, bass.ds(t * P, S)]).then_inc(enc_loaded, 16)

                load(0)
                with sp.Fori(1, TILES) as t:
                    sp.wait_ge(v_ready, t)
                    load(t)

        @block.gpsimd
        def _(pool):
            with pool.Fori(0, TILES) as t:
                pool.wait_ge(xn_ready, t + 1)
                xt = core.x[:, ds(t, C)]
                nc.gpsimd.tensor_tensor(xt, xt, core.rows[:, n, :], ALU.add).then_inc(bias_added, 1)

        @block.tensor
        def _(pe):
            def project_in(t):
                pe.wait_ge(xn_ready, t + 1)
                if later(t - 1):
                    pe.wait_ge(headsT_copied, t - 1)
                for half in range(HALVES):
                    last = nc.tensor.transpose(tr[:, half * P:(half + 1) * P], xn[:, half * P:(half + 1) * P],
                                               core.ident[:, :])
                last.then_inc(xnT_ready, 1)
                pe.wait_ge(ln_ready, t + 1)
                if cross:
                    pe.wait_ge(enc_loaded, 32 * t + 32)
                for dst, w, c0, src in ((0, wq, q0, lnT), (HALVES, wk, k0, kvT)):
                    for half in range(HALVES):
                        for kb in range(HALVES):
                            last = nc.tensor.matmul(
                                qk[:, (dst + half) * P:(dst + half + 1) * P],
                                w[:, kb, c0 + half * P:c0 + (half + 1) * P], src[:, kb, 0:P],
                                start=(kb == 0), stop=(kb == HALVES - 1))
                last.then_inc(qk_ready, 1)
                if later(t):
                    pe.wait_ge(v_copied, t)
                if not cross:
                    pe.wait_ge(ln_repeated, t + 1)
                for j in range(2):
                    for kb in range(HALVES):
                        last = nc.tensor.matmul(vv[:, j * C:(j + 1) * C], kvT[:, kb, j * S:j * S + P],
                                                wv[:, kb, v0:v0 + C], start=(kb == 0), stop=(kb == HALVES - 1))
                last.then_inc(v_ready, 1)

            def score(t):
                pe.wait_ge(q_copied, t + 1)
                if later(t):
                    pe.wait_ge(probsT_copied, t)
                for half in range(HALVES):
                    for g in range(GROUPS):
                        rows = slice(32 * g, 32 * (g + 1))
                        for b in range(BPT):
                            last = nc.tensor.matmul(
                                scores[b * S:(b + 1) * S, g, half * P:(half + 1) * P],
                                qT[rows, half, b * S:(b + 1) * S],
                                kT[rows, half, :, b * S:(b + 1) * S], start=True, stop=True)
                last.then_inc(scores_ready, 1)

            def attend(t):
                pe.wait_ge(probs_ready, t + 1)
                for pair in range(PAIRS):
                    last = nc.tensor.transpose(pT[:, pair * P:(pair + 1) * P], z[:, pair, :], core.ident[:, :])
                last.then_inc(probsT_ready, 1)
                pe.wait_ge(probsT_copied, t + 1)
                pe.wait_ge(v_copied, t + 1)
                if later(t):
                    pe.wait_ge(x_ready, t)
                for pair in range(PAIRS):
                    for b in range(BPT):
                        last = nc.tensor.matmul(oo[b * S:(b + 1) * S, pair * PW:(pair + 1) * PW],
                                                zT[:, pair, b * S:(b + 1) * S], core.vpad[:, b, pair, :],
                                                start=True, stop=True)
                last.then_inc(out_ready, 1)

            def project_out(t):
                pe.wait_ge(heads_ready, t + 1)
                for half in range(HALVES):
                    last = nc.tensor.transpose(tr[:, half * P:(half + 1) * P], heads[:, half * P:(half + 1) * P],
                                               core.ident[:, :])
                last.then_inc(headsT_ready, 1)
                pe.wait_ge(headsT_copied, t + 1)
                for kb in range(HALVES):
                    last = nc.tensor.matmul(oo[:, 0:C], headsT[:, kb, :], wo[:, kb, :],
                                            start=(kb == 0), stop=(kb == HALVES - 1))
                last.then_inc(proj_ready, 1)

            project_in(0)
            score(0)
            def body(t):
                project_in(t + 1)
                attend(t)
                score(t + 1)
                project_out(t)

            body(0)
            with pe.Fori(1, TILES - 1) as t:
                body(t)
            attend(TILES - 1)
            project_out(TILES - 1)

        @block.scalar
        def _(act):
            def normalise(t):
                if later(t):
                    act.wait_ge(xnT_ready, t)
                nc.scalar.activation(xn[:, :], core.x[:, ds(t, C)], ACT.Identity, scale=core.rstd[:, ds(t, 1)],
                                     bias=core.neg_mean[:, ds(t, 1)]).then_inc(xn_ready, 1)

            def copy_in(t):
                act.wait_ge(xnT_ready, t + 1)
                for half in range(HALVES):
                    last = nc.scalar.activation(lnT[:, half, 0:P], tr[:, half * P:(half + 1) * P], ACT.Identity,
                                                scale=col(core, ln_s, half), bias=col(core, ln_b, half))
                last.then_inc(ln_ready, 1)
                act.wait_ge(qk_ready, t + 1)
                for half in range(HALVES):
                    nc.scalar.activation(qT[:, half, :], qk[:, half * P:(half + 1) * P], ACT.Identity,
                                         scale=HD ** -0.5, bias=core.q_bias[:, n, half:half + 1])
                    for e in range(2):
                        last = nc.scalar.activation(
                            kT[:, half, e, :], qk[:, (HALVES + half) * P:(HALVES + half + 1) * P], ACT.Identity,
                            scale=core.parity[:, e:e + 1], bias=core.k_bias[:, n, half, e:e + 1])
                last.then_inc(q_copied, 1)

            def copy_values(t):
                act.wait_ge(v_ready, t + 1)
                if later(t):
                    act.wait_ge(out_ready, t)
                for e in range(2):
                    rows = slice(e * S, (e + 1) * S)
                    for b in range(BPT):
                        j = (b + e) % 2
                        last = nc.scalar.activation(
                            core.vpad[rows, b, :, e * HD:(e + 1) * HD],
                            vv[rows, j * C:(j + 1) * C].rearrange("p (r e d) -> p r e d", r=PAIRS, e=2)[:, :, e, :],
                            ACT.Copy)
                last.then_inc(v_copied, 1)

            def exps(t):
                act.wait_ge(shifted, t + 1)
                nc.scalar.activation(z[:, :, :], z[:, :, :], ACT.Exp).then_inc(probs_ready, 1)

            def copy_probs(t):
                act.wait_ge(probsT_ready, t + 1)
                for j in range(2):
                    last = nc.scalar.activation(zT[:, j * PAIRS // 2:(j + 1) * PAIRS // 2, :],
                                                pT[:, j * 512:(j + 1) * 512], ACT.Copy)
                last.then_inc(probsT_copied, 1)

            def copy_heads(t):
                act.wait_ge(headsT_ready, t + 1)
                for half in range(HALVES):
                    last = nc.scalar.activation(headsT[:, half, :], tr[:, half * P:(half + 1) * P], ACT.Identity,
                                                bias=col(core, f"b_v_{kind}", half))
                last.then_inc(headsT_copied, 1)

            def body(t, more):
                copy_in(t + 1)
                copy_probs(t)
                if more:
                    normalise(t + 2)
                copy_values(t + 1)
                copy_heads(t)
                exps(t + 1)

            normalise(0)
            copy_in(0)
            copy_values(0)
            normalise(1)
            exps(0)
            body(0, True)
            with act.Fori(1, TILES - 2) as t:
                body(t, True)
            body(TILES - 2, False)
            copy_probs(TILES - 1)
            copy_heads(TILES - 1)

        @block.vector
        def _(dve):
            def softmax_shift(t):
                mask, bias = ((m[:, ds(t, S)] for m in (core.cross_mask, core.cross_bias)) if cross
                              else (core.self_mask[:, :], core.self_bias[:, :]))
                dve.wait_ge(scores_ready, t + 1)
                for half in range(HALVES):
                    last = nc.vector.tensor_tensor(
                        z[:, half * GROUPS:(half + 1) * GROUPS, :].rearrange("p g (e k) -> p g e k", e=2),
                        scores[:, :, half * P:(half + 1) * P].rearrange("p g (e k) -> p g e k", e=2),
                        mask.unsqueeze(1).unsqueeze(1).to_broadcast([P, GROUPS, 2, S]), ALU.mult)
                last.then_inc(masked, 1)
                dve.wait_ge(masked, t + 1)
                by_head = z[:, :, :].rearrange("p r (e k) -> p (r e) k", e=2)
                nc.vector.tensor_tensor(by_head, by_head, bias.unsqueeze(1).to_broadcast([P, NH, S]),
                                        ALU.add).then_inc(biased, 1)
                dve.wait_ge(biased, t + 1)
                nc.vector.tensor_reduce(out=row_max[:, :], in_=by_head, op=ALU.max, axis=AX.X).then_inc(max_ready, 1)
                dve.wait_ge(max_ready, t + 1)
                nc.vector.tensor_tensor(by_head, by_head, row_max[:, :].unsqueeze(2).to_broadcast([P, NH, S]),
                                        ALU.subtract).then_inc(shifted, 1)

            def repeat(t):
                if not cross:
                    dve.wait_ge(ln_ready, t + 1)
                    if later(t):
                        dve.wait_ge(v_ready, t)
                    nc.vector.tensor_copy(lnT[:, :, P:3 * S], lnT[:, :, 0:S]).then_inc(ln_repeated, 1)

            def divide(t):
                dve.wait_ge(out_ready, t + 1)
                pairs = oo[:, 0:PAIRS * PW].rearrange("p (r n) -> p r n", n=PW)
                nc.vector.reciprocal(recip[:, :].rearrange("p (r e) -> p r e", e=2),
                                     pairs[:, :, 2 * HD:PW]).then_inc(recip_ready, 1)
                dve.wait_ge(recip_ready, t + 1)
                if later(t):
                    dve.wait_ge(headsT_ready, t)
                nc.vector.tensor_tensor(
                    heads[:, :].rearrange("p (r e d) -> p r e d", e=2, d=HD),
                    pairs[:, :, 0:2 * HD].rearrange("p r (e d) -> p r e d", e=2),
                    recip[:, :].rearrange("p (r e) -> p r e", e=2).unsqueeze(3).to_broadcast([P, PAIRS, 2, HD]),
                    ALU.mult).then_inc(heads_ready, 1)

            def add_residual(t):
                xt = core.x[:, ds(t, C)]
                dve.wait_ge(proj_ready, t + 1)
                dve.wait_ge(bias_added, t + 1)
                nc.vector.tensor_tensor(xt, oo[:, 0:C], xt, ALU.add).then_inc(x_ready, 1)
                dve.wait_ge(x_ready, t + 1)
                nc.vector.bn_stats(core.stats[:, ds(t, 6)], xt)

            repeat(0)
            softmax_shift(0)
            def body(t):
                repeat(t + 1)
                divide(t)
                softmax_shift(t + 1)
                add_residual(t)

            body(0)
            with dve.Fori(1, TILES - 1) as t:
                body(t)
            divide(TILES - 1)
            add_residual(TILES - 1)


def gelu_phase(core):
    nc = core.nc
    n4 = 4
    runs, hidden = TILES // n4, F1 // P
    w1, w2 = core.w["w1"], core.w["w2"]
    with ExitStack() as ctx:
        def sb(name, shape):
            return ctx.enter_context(nc.sbuf_tensor(f"gelu_{name}", shape, FP32))

        xn = sb("xn", [P, n4, C])
        lnT = sb("lnT", [P, HALVES, n4 * P])
        hT = sb("hT", [P, hidden, n4 * P])
        tr = core.banks[0:2]
        up_banks = core.banks[2:5]
        down_banks = core.banks[5:7]
        names = ("xn_ready", "xnT_ready", "ln_ready", "up_ready", "gelu_ready", "down_ready", "x_ready", "bias_added")
        (xn_ready, xnT_ready, ln_ready, up_ready, gelu_ready, down_ready, x_ready,
         bias_added) = semaphores(nc, ctx, *(f"gelu_{s}" for s in names))
        block = ctx.enter_context(nc.Block())

        @block.gpsimd
        def _(pool):
            with pool.Fori(0, runs) as s:
                pool.wait_ge(xn_ready, s + 1)
                xs = core.x[:, ds(s, n4 * C)].rearrange("p (j c) -> p j c", j=n4)
                nc.gpsimd.tensor_tensor(xs, xs, core.rows[:, 2, :].unsqueeze(1).to_broadcast([P, n4, C]),
                                        ALU.add).then_inc(bias_added, 1)

        @block.tensor
        def _(pe):
            def transpose(s):
                pe.wait_ge(xn_ready, s + 1)
                if later(s):
                    pe.wait_ge(ln_ready, s)
                for half in range(HALVES):
                    for j in range(n4):
                        last = nc.tensor.transpose(tr[half][:, j * P:(j + 1) * P],
                                                   xn[:, j, half * P:(half + 1) * P], core.ident[:, :])
                last.then_inc(xnT_ready, 1)

            def up(s):
                pe.wait_ge(ln_ready, s + 1)
                for h in range(hidden):
                    if h >= len(up_banks) or later(s):
                        pe.wait_ge(gelu_ready, s * hidden + h + 1 - len(up_banks))
                    for kb in range(HALVES):
                        last = nc.tensor.matmul(up_banks[h % len(up_banks)], w1[:, kb, h * P:(h + 1) * P],
                                                lnT[:, kb, :], start=(kb == 0), stop=(kb == HALVES - 1))
                    last.then_inc(up_ready, 1)

            def down(s):
                pe.wait_ge(gelu_ready, s * hidden + hidden)
                if later(s):
                    pe.wait_ge(x_ready, s * n4)
                for j in range(n4):
                    for h in range(hidden):
                        last = nc.tensor.matmul(down_banks[j // 2][:, (j % 2) * C:(j % 2 + 1) * C],
                                                hT[:, h, j * P:(j + 1) * P], w2[:, h, :],
                                                start=(h == 0), stop=(h == hidden - 1))
                    if j % 2:
                        last.then_inc(down_ready, 1)

            transpose(0)
            up(0)
            transpose(1)
            down(0)
            with pe.Fori(1, runs - 1) as s:
                up(s)
                transpose(s + 1)
                down(s)
            up(runs - 1)
            down(runs - 1)

        @block.scalar
        def _(act):
            def copy_in(s):
                act.wait_ge(xnT_ready, s + 1)
                for half in range(HALVES):
                    last = nc.scalar.activation(lnT[:, half, :], tr[half], ACT.Identity,
                                                scale=col(core, "ln3_s", half), bias=col(core, "ln3_b", half))
                last.then_inc(ln_ready, 1)

            def gelus(s):
                if later(s):
                    act.wait_ge(down_ready, 2 * s)
                for h in range(hidden):
                    act.wait_ge(up_ready, s * hidden + h + 1)
                    nc.scalar.activation(hT[:, h, :], up_banks[h % len(up_banks)], ACT.Gelu_apprx_tanh,
                                         bias=col(core, "b1", h)).then_inc(gelu_ready, 1)

            copy_in(0)
            gelus(0)
            copy_in(1)
            with act.Fori(1, runs - 1) as s:
                gelus(s)
                copy_in(s + 1)
            gelus(runs - 1)

        @block.vector
        def _(dve):
            def normalise(s):
                if later(s):
                    dve.wait_ge(xnT_ready, s)
                for j in range(n4):
                    t = s * n4 + j
                    last = nc.vector.tensor_scalar(xn[:, j, :], core.x[:, ds(t, C)], core.rstd[:, ds(t, 1)],
                                                   core.neg_mean[:, ds(t, 1)], ALU.mult, ALU.add)
                last.then_inc(xn_ready, 1)

            def add_residual(s):
                for j in range(n4):
                    t = s * n4 + j
                    if j % 2 == 0:
                        dve.wait_ge(down_ready, 2 * s + j // 2 + 1)
                    if j == 0:
                        dve.wait_ge(bias_added, s + 1)
                    xt = core.x[:, ds(t, C)]
                    nc.vector.tensor_tensor(xt, down_banks[j // 2][:, (j % 2) * C:(j % 2 + 1) * C], xt,
                                            ALU.add).then_inc(x_ready, 1)
                for j in range(n4):
                    t = s * n4 + j
                    dve.wait_ge(x_ready, t + 1)
                    nc.vector.bn_stats(core.stats[:, ds(t, 6)], core.x[:, ds(t, C)])

            normalise(0)
            normalise(1)
            add_residual(0)
            with dve.Fori(1, runs - 1) as s:
                normalise(s + 1)
                add_residual(s)
            add_residual(runs - 1)


MIX = (1, 0, 3, 2, 4)
NW, NK, NR, NV, NG = range(NMIX)
CH = 2
RT = CH * P
RB = RT // S
RUNS = B * S // RT
JG = 2
GROUPS_R = HALVES * RS // JG


def recurrence_phase(core):
    nc = core.nc
    w = core.w
    with ExitStack() as ctx:
        def sb(name, shape):
            return ctx.enter_context(nc.sbuf_tensor(f"rec_{name}", shape, FP32))

        xn = sb("xn", [P, CH, C])
        xa = sb("xa", [P, HALVES, RB, S + 1])
        sx = sb("sx", [P, HALVES, RB, S])
        xin = sb("xin", [P, HALVES, RT])
        mixer_a, mixer_b = sb("mixer_a", [P, RT]), sb("mixer_b", [DM, RT])
        mixed = sb("mixed", [P, 2, HALVES, RT])
        xm = sb("xm", [P, 2, HALVES, RT])
        decay_in = sb("decay_in", [DD, RT])
        decay_exp = sb("decay_exp", [P, HALVES * RB, S])
        gate_tanh = sb("gate_tanh", [P, HALVES * RT])
        kT = sb("kT", [P, 2, HALVES, RB, S])
        rT = sb("rT", [P, 2, HALVES, RT])
        vT = sb("vT", [P, 2, HALVES, RT])
        wT = sb("wT", [P, 2, HALVES * RB, S])
        bonus = sb("bonus", [P, HALVES, RT])
        v_tok = sb("v_tok", [P, CH * C])
        bonus_sum = sb("bonus_sum", [P, CH * RH])
        st = sb("st", [P, GROUPS_R, JG, RB, S])
        o = sb("o", [P, CH * C])
        o_sq = sb("o_sq", [P, CH * C])
        mean = sb("mean", [P, CH * RH])

        tr, small = core.banks[0], core.banks[1]
        mix_banks, proj_banks = core.banks[2:4], core.banks[4:6]
        v_bank, o_bank = core.banks[6], core.banks[7]

        names = ("xn_ready xnT_ready xa_ready first_slot sx_ready xin_ready mixer_ready mixer_tanh mix_ready mixed_ready "
                 "xm_ready decay_ready decay_tanh proj_ready copied gate_ready gate_done decay_expd w_ready v_tok_ready v_tok_copied "
                 "bonus_ready bonus_sum_ready bonus_sum_copied vj_ready kv_ready slot_ready scanned read_ready summed "
                 "o_bonus o_ready mean_ready mean_scaled o_stored sq_ready var_stored").split()
        sem = dict(zip(names, semaphores(nc, ctx, *(f"rec_{n}" for n in names))))
        (xn_ready, xnT_ready, xa_ready, first_slot, sx_ready, xin_ready, mixer_ready, mixer_tanh, mix_ready, mixed_ready,
         xm_ready, decay_ready, decay_tanh, proj_ready, copied, gate_ready, gate_done, decay_expd, w_ready, v_tok_ready, v_tok_copied,
         bonus_ready, bonus_sum_ready, bonus_sum_copied, vj_ready, kv_ready, slot_ready, scanned, read_ready, summed,
         o_bonus, o_ready, mean_ready, mean_scaled, o_stored, sq_ready, var_stored) = (sem[n] for n in names)
        block = ctx.enter_context(nc.Block())

        def bodies(eng, body):
            body(0, 0, True, True)
            body(1, 1, True, True)
            with eng.Fori(1, RUNS // 2 - 1) as i:
                body(2 * i, 0, True, True)
                body(2 * i + 1, 1, True, True)
            body(RUNS - 2, 0, True, False)
            body(RUNS - 1, 1, False, False)

        @block.gpsimd
        def _(pool):
            with pool.Fori(0, RUNS) as s:
                for m in range(NMIX):
                    pool.wait_ge(mixed_ready, s * NMIX + m + 1)
                    if m >= 2:
                        pool.wait_ge(proj_ready, s * NMIX + m - 1)
                    nc.gpsimd.tensor_tensor(
                        xm[:, m % 2, :, :].rearrange("p h (b t) -> p (h b) t", t=S),
                        mixed[:, m % 2, :, :].rearrange("p h (b t) -> p (h b) t", t=S),
                        xa[:, :, :, 1:S + 1].rearrange("p h b t -> p (h b) t"), ALU.add).then_inc(xm_ready, 1)

        @block.tensor
        def _(pe):
            def transpose(s):
                pe.wait_ge(xn_ready, s + 1)
                if later(s):
                    pe.wait_ge(bonus_sum_copied, s)
                for half in range(HALVES):
                    for c in range(CH):
                        a = half * RT + c * P
                        last = nc.tensor.transpose(tr[:, a:a + P], xn[:, c, half * P:(half + 1) * P], core.ident[:, :])
                last.then_inc(xnT_ready, 1)

            def mixer(s):
                pe.wait_ge(xin_ready, s + 1)
                if later(s):
                    pe.wait_ge(v_tok_copied, s)
                for kb in range(HALVES):
                    nc.tensor.matmul(small[:, 0:RT], w["maa_w1"][:, kb, 0:P], xin[:, kb, :],
                                     start=(kb == 0), stop=(kb == HALVES - 1))
                for kb in range(HALVES):
                    last = nc.tensor.matmul(small[0:DM, RT:2 * RT], w["maa_w1"][:, kb, P:P + DM], xin[:, kb, :],
                                            start=(kb == 0), stop=(kb == HALVES - 1))
                last.then_inc(mixer_ready, 1)

            def mix(s, m):
                if m == 0:
                    pe.wait_ge(mixer_tanh, s + 1)
                if later(s) or m >= 2:
                    pe.wait_ge(mixed_ready, s * NMIX + m - 1)
                f = MIX[m]
                rows = slice(f * DM, (f + 1) * DM) if f < 4 else slice(0, DM)
                w2, x = (core.maa_w2a, mixer_a) if f < 4 else (core.maa_w2b, mixer_b)
                for half in range(HALVES):
                    last = nc.tensor.matmul(mix_banks[m % 2][:, half * RT:(half + 1) * RT],
                                            w2[rows, half * P:(half + 1) * P], x[rows, :], start=True, stop=True)
                last.then_inc(mix_ready, 1)

            def project(s, m):
                pe.wait_ge(xm_ready, s * NMIX + m + 1)
                if m == NW:
                    pe.wait_ge(xa_ready, s + 1)
                    for kb in range(HALVES):
                        last = nc.tensor.matmul(tr[0:DD, 0:RT], w["td_w1"][:, kb, :], xm[:, m % 2, kb, :],
                                                start=(kb == 0), stop=(kb == HALVES - 1))
                    last.then_inc(proj_ready, 1)
                    return
                name = {NK: "WkT", NR: "WrT", NV: "WvT", NG: "WgT"}[m]
                bank = proj_banks[m % 2]
                if later(s) and m == NK:
                    pe.wait_ge(w_ready, s)
                if later(s) and m == NR:
                    pe.wait_ge(gate_done, s)
                if m >= 3:
                    pe.wait_ge(copied, s * 3 + m - 2)
                for half in range(HALVES):
                    for kb in range(HALVES):
                        last = nc.tensor.matmul(bank[:, half * RT:(half + 1) * RT], w[name][:, kb, half * P:(half + 1) * P],
                                                xm[:, m % 2, kb, :], start=(kb == 0), stop=(kb == HALVES - 1))
                last.then_inc(proj_ready, 1)

            def decay(s):
                pe.wait_ge(decay_tanh, s + 1)
                pe.wait_ge(copied, s * 3 + 3)
                for half in range(HALVES):
                    last = nc.tensor.matmul(proj_banks[NV % 2][:, half * RT:(half + 1) * RT],
                                            core.td_w2[:, half * P:(half + 1) * P], decay_in[:, :], start=True, stop=True)
                last.then_inc(decay_ready, 1)

            def tokens(s, u):
                for c in range(CH):
                    for half in range(HALVES):
                        a = c * C + half * P
                        last = nc.tensor.transpose(small[:, a:a + P], vT[:, u, half, c * P:(c + 1) * P], core.ident[:, :])
                last.then_inc(v_tok_ready, 1)
                pe.wait_ge(bonus_ready, s + 1)
                for c in range(CH):
                    for half in range(HALVES):
                        a = c * RH + half * HPH
                        last = nc.tensor.matmul(tr[:, a:a + HPH], bonus[:, half, c * P:(c + 1) * P],
                                                core.head_sum[:, :], start=True, stop=True)
                last.then_inc(bonus_sum_ready, 1)

            def spread(s, u, n):
                half, j0 = n // (RS // JG), n % (RS // JG) * JG
                if later(s) or n:
                    pe.wait_ge(kv_ready, s * GROUPS_R + n)
                for jj in range(JG):
                    last = nc.tensor.matmul(v_bank[:, jj * RT:(jj + 1) * RT], core.spread[:, j0 + jj, :],
                                            vT[:, u, half, :], start=True, stop=True)
                last.then_inc(vj_ready, 1)

            def sum_heads(s, n):
                half, j0 = n // (RS // JG), n % (RS // JG) * JG
                pe.wait_ge(read_ready, s * GROUPS_R + n + 1)
                if n == 0 and later(s):
                    pe.wait_ge(o_ready, s)
                for c in range(CH):
                    for jj in range(JG):
                        a = c * C + (half * RS + j0 + jj) * HPH
                        rows = st[:, n, jj, :, :].rearrange("p b t -> p (b t)")[:, c * P:(c + 1) * P]
                        last = nc.tensor.matmul(o_bank[:, a:a + HPH], rows, core.head_sum[:, :], start=True, stop=True)
                last.then_inc(summed, 1)

            def front(s, u):
                return [lambda: transpose(s), lambda: mixer(s), lambda: mix(s, 0),
                        lambda: (mix(s, 1), project(s, 0)), lambda: (mix(s, 2), project(s, 1)),
                        lambda: (mix(s, 3), project(s, 2)), lambda: (mix(s, 4), project(s, 3)),
                        lambda: (project(s, 4), decay(s)), lambda: tokens(s, u)]

            def body(s, u, more, _):
                pieces = front(s + 1, 1 - u) if more else [lambda: None] * 9
                for n in range(GROUPS_R):
                    spread(s, u, n)
                    if n:
                        sum_heads(s, n - 1)
                    pieces[n]()
                sum_heads(s, GROUPS_R - 1)
                pieces[8]()

            for piece in front(0, 0):
                piece()
            bodies(pe, body)

        @block.scalar
        def _(act):
            def copy_in(s):
                act.wait_ge(xnT_ready, s + 1)
                if later(s):
                    act.wait_ge(xm_ready, s * NMIX)
                for half in range(HALVES):
                    last = nc.scalar.activation(xa[:, half, :, 1:S + 1],
                                                tr[:, half * RT:(half + 1) * RT].rearrange("p (b t) -> p b t", t=S),
                                                ACT.Identity, scale=col(core, "r_ln1_w", half),
                                                bias=col(core, "r_ln1_b", half))
                last.then_inc(xa_ready, 1)

            def mixer(s):
                act.wait_ge(mixer_ready, s + 1)
                nc.scalar.activation(mixer_a[:, :], small[:, 0:RT], ACT.Tanh)
                nc.scalar.activation(mixer_b[:, :], small[0:DM, RT:2 * RT], ACT.Tanh).then_inc(mixer_tanh, 1)

            def copy(s, u, m):
                act.wait_ge(proj_ready, s * NMIX + m + 1)
                bank = proj_banks[m % 2]
                if m == NW:
                    nc.scalar.activation(decay_in[:, :], tr[0:DD, 0:RT], ACT.Tanh).then_inc(decay_tanh, 1)
                elif m == NG:
                    nc.scalar.activation(gate_tanh[:, :], bank, ACT.Tanh, scale=0.5).then_inc(gate_ready, 1)
                elif m == NK:
                    nc.scalar.activation(kT[:, u, :, :, :].rearrange("p h b t -> p (h b t)"), bank,
                                         ACT.Copy).then_inc(copied, 1)
                else:
                    dst = rT if m == NR else vT
                    nc.scalar.activation(dst[:, u, :, :].rearrange("p h t -> p (h t)"), bank, ACT.Copy).then_inc(copied, 1)

            def decay(s, u):
                act.wait_ge(decay_ready, s + 1)
                for half in range(HALVES):
                    last = nc.scalar.activation(decay_exp[:, half * RB:(half + 1) * RB, :].rearrange("p b t -> p (b t)"),
                                                proj_banks[NV % 2][:, half * RT:(half + 1) * RT], ACT.Exp,
                                                bias=col(core, "time_decay", half))
                last.then_inc(decay_expd, 1)
                act.wait_ge(decay_expd, s + 1)
                nc.scalar.activation(wT[:, u, :, 1:S], decay_exp[:, :, 0:S - 1], ACT.Exp, scale=-1.0).then_inc(w_ready, 1)

            def tokens(s):
                act.wait_ge(v_tok_ready, s + 1)
                if later(s):
                    act.wait_ge(o_bonus, s)
                nc.scalar.activation(v_tok[:, :], small, ACT.Copy).then_inc(v_tok_copied, 1)
                act.wait_ge(bonus_sum_ready, s + 1)
                nc.scalar.activation(bonus_sum[:, :], tr[:, 0:CH * RH], ACT.Copy).then_inc(bonus_sum_copied, 1)

            def square(s):
                act.wait_ge(o_stored, s + 1)
                if later(s):
                    act.wait_ge(var_stored, s)
                nc.scalar.activation(o_sq[:, :], core.o[:, ds(s, CH * C)], ACT.Square).then_inc(sq_ready, 1)

            def front(s, u):
                copy_in(s)
                mixer(s)
                for m in range(NMIX):
                    copy(s, u, m)
                decay(s, u)

            def body(s, u, more, _):
                if more:
                    front(s + 1, 1 - u)
                square(s)
                if more:
                    tokens(s + 1)

            front(0, 0)
            tokens(0)
            bodies(act, body)

        @block.vector
        def _(dve):
            def normalise(s):
                if later(s):
                    dve.wait_ge(xnT_ready, s)
                for c in range(CH):
                    t = s * CH + c
                    last = nc.vector.tensor_scalar(xn[:, c, :], core.x[:, ds(t, C)], core.rstd[:, ds(t, 1)],
                                                   core.neg_mean[:, ds(t, 1)], ALU.mult, ALU.add)
                last.then_inc(xn_ready, 1)

            def shift(s):
                if later(s):
                    dve.wait_ge(xm_ready, s * NMIX)
                nc.vector.tensor_copy(xa[:, :, :, 0], core.state_rows[:, 1, :, ds(s, RB)]).then_inc(first_slot, 1)
                dve.wait_ge(xa_ready, s + 1)
                dve.wait_ge(first_slot, s + 1)
                nc.vector.tensor_tensor(sx[:, :, :, :].rearrange("p h b t -> p (h b) t"),
                                        xa[:, :, :, 0:S].rearrange("p h b t -> p (h b) t"),
                                        xa[:, :, :, 1:S + 1].rearrange("p h b t -> p (h b) t"),
                                        ALU.subtract).then_inc(sx_ready, 1)
                dve.wait_ge(sx_ready, s + 1)
                if later(s):
                    dve.wait_ge(mixer_ready, s)
                for half in range(HALVES):
                    last = nc.vector.scalar_tensor_tensor(
                        out=xin[:, half, :].rearrange("p (b t) -> p b t", t=S), in0=sx[:, half, :, :],
                        scalar=col(core, "maa_x", half), in1=xa[:, half, :, 1:S + 1], op0=ALU.mult, op1=ALU.add)
                last.then_inc(xin_ready, 1)

            def mix(s, m):
                dve.wait_ge(mix_ready, s * NMIX + m + 1)
                if later(s) or m >= 2:
                    dve.wait_ge(xm_ready, s * NMIX + m - 1)
                for half in range(HALVES):
                    last = nc.vector.scalar_tensor_tensor(
                        out=mixed[:, m % 2, half, :], in0=mix_banks[m % 2][:, half * RT:(half + 1) * RT],
                        scalar=col(core, "maa_stack", MIX[m] * HALVES + half),
                        in1=sx[:, half, :, :].rearrange("p b t -> p (b t)"), op0=ALU.add, op1=ALU.mult)
                last.then_inc(mixed_ready, 1)

            def gate(s):
                dve.wait_ge(gate_ready, s + 1)
                nc.vector.scalar_tensor_tensor(out=core.gate[:, ds(s, HALVES * RT)], in0=gate_tanh[:, :], scalar=1.0,
                                               in1=proj_banks[NG % 2], op0=ALU.add, op1=ALU.mult).then_inc(gate_done, 1)

            def make_bonus(s, u):
                dve.wait_ge(copied, s * 3 + 2)
                if later(s):
                    dve.wait_ge(bonus_sum_ready, s)
                for half in range(HALVES):
                    last = nc.vector.scalar_tensor_tensor(
                        out=bonus[:, half, :], in0=rT[:, u, half, :], scalar=col(core, "u", half),
                        in1=kT[:, u, half, :, :].rearrange("p b t -> p (b t)"), op0=ALU.mult, op1=ALU.mult)
                last.then_inc(bonus_ready, 1)

            def recur(s, u, n):
                half, j0 = n // (RS // JG), n % (RS // JG) * JG
                g = s * GROUPS_R + n
                dve.wait_ge(vj_ready, g + 1)
                if later(s):
                    dve.wait_ge(summed, g + 1 - GROUPS_R)
                if n == 0:
                    dve.wait_ge(copied, s * 3 + 3)
                    dve.wait_ge(w_ready, s + 1)
                nc.vector.tensor_copy(st[:, n, :, :, 0], core.state0[:, half * RS + j0:half * RS + j0 + JG, ds(s, RB)])
                nc.vector.tensor_tensor(
                    st[:, n, :, :, 1:S], v_bank.rearrange("p (j b t) -> p j b t", j=JG, t=S)[:, :, :, 0:S - 1],
                    kT[:, u, half, :, 0:S - 1].unsqueeze(1).to_broadcast([P, JG, RB, S - 1]),
                    ALU.mult).then_inc(kv_ready, 1)
                dve.wait_ge(kv_ready, g + 1)
                for jj in range(JG):
                    states = st[:, n, jj, :, :].rearrange("p b t -> p (b t)")
                    last = nc.vector.tensor_tensor_scan(
                        states, wT[:, u, half * RB:(half + 1) * RB, :].rearrange("p b t -> p (b t)"), states, 0.0,
                        ALU.mult, ALU.add)
                last.then_inc(scanned, 1)
                dve.wait_ge(scanned, g + 1)
                states = st[:, n, :, :, :].rearrange("p j b t -> p j (b t)")
                nc.vector.tensor_tensor(states, states, rT[:, u, half, :].unsqueeze(1).to_broadcast([P, JG, RT]),
                                        ALU.mult).then_inc(read_ready, 1)

            def finish(s):
                dve.wait_ge(v_tok_copied, s + 1)
                dve.wait_ge(bonus_sum_copied, s + 1)
                heads = o[:, :].rearrange("p (h j) -> p h j", j=RS)
                nc.vector.tensor_tensor(heads, v_tok[:, :].rearrange("p (h j) -> p h j", j=RS),
                                        bonus_sum[:, :].unsqueeze(2).to_broadcast([P, CH * RH, RS]),
                                        ALU.mult).then_inc(o_bonus, 1)
                dve.wait_ge(o_bonus, s + 1)
                dve.wait_ge(summed, s * GROUPS_R + GROUPS_R)
                by_half = o[:, :].rearrange("p (q h j) -> p q h j", q=CH * HALVES, j=RS)
                nc.vector.tensor_tensor(by_half, o_bank.rearrange("p (q j h) -> p q h j", q=CH * HALVES, j=RS), by_half,
                                        ALU.add).then_inc(o_ready, 1)
                dve.wait_ge(o_ready, s + 1)
                nc.vector.tensor_reduce(out=mean[:, :], in_=heads, op=ALU.add, axis=AX.X).then_inc(mean_ready, 1)
                dve.wait_ge(mean_ready, s + 1)
                nc.vector.tensor_scalar(mean[:, :], mean[:, :], 1.0 / RS, None, ALU.mult).then_inc(mean_scaled, 1)
                dve.wait_ge(mean_scaled, s + 1)
                nc.vector.tensor_tensor(core.o[:, ds(s, CH * C)].rearrange("p (h j) -> p h j", j=RS), heads,
                                        mean[:, :].unsqueeze(2).to_broadcast([P, CH * RH, RS]),
                                        ALU.subtract).then_inc(o_stored, 1)

            def sum_squares(s):
                dve.wait_ge(sq_ready, s + 1)
                nc.vector.tensor_reduce(out=core.var[:, ds(s, CH * RH)], in_=o_sq[:, :].rearrange("p (h j) -> p h j", j=RS),
                                        op=ALU.add, axis=AX.X).then_inc(var_stored, 1)

            def body(s, u, more, norm):
                for n in range(GROUPS_R):
                    recur(s, u, n)
                    if more and n == 0:
                        shift(s + 1)
                    if more and n >= 2 and n < 7:
                        mix(s + 1, n - 2)
                    if n == 1 and later(s):
                        sum_squares(s - 1)
                    if norm and n == 7:
                        normalise(s + 2)
                if more:
                    make_bonus(s + 1, 1 - u)
                finish(s)
                if more:
                    gate(s + 1)

            nc.vector.memset(wT[:, :, :, 0], 0.0)
            normalise(0)
            shift(0)
            for m in range(NMIX):
                mix(0, m)
            make_bonus(0, 0)
            gate(0)
            normalise(1)
            bodies(dve, body)
            sum_squares(RUNS - 1)


def gate_phase(core):
    nc = core.nc
    with ExitStack() as ctx:
        def sb(name, shape):
            return ctx.enter_context(nc.sbuf_tensor(f"gate_{name}", shape, FP32))

        rstd = sb("rstd", [P, TILES * RH])
        on = sb("on", [P, CH * C])
        onT = sb("onT", [P, HALVES * RT])
        yT = sb("yT", [P, HALVES * RT])
        tr, proj = core.banks[0], core.banks[1]
        (std_ready, rstd_ready, on_ready, onT_ready, onT_copied, y_ready, proj_ready, x_ready) = semaphores(
            nc, ctx, *(f"gate_{s}" for s in ("std_ready", "rstd_ready", "on_ready", "onT_ready", "onT_copied",
                                             "y_ready", "proj_ready", "x_ready")))
        block = ctx.enter_context(nc.Block())

        @block.tensor
        def _(pe):
            def transpose(s):
                pe.wait_ge(on_ready, s + 1)
                if later(s):
                    pe.wait_ge(onT_copied, s)
                for half in range(HALVES):
                    for c in range(CH):
                        a = half * RT + c * P
                        last = nc.tensor.transpose(tr[:, a:a + P], on[:, c * C + half * P:c * C + (half + 1) * P],
                                                   core.ident[:, :])
                last.then_inc(onT_ready, 1)

            def project(s):
                pe.wait_ge(y_ready, s + 1)
                if later(s):
                    pe.wait_ge(x_ready, s)
                for c in range(CH):
                    for kb in range(HALVES):
                        a = kb * RT + c * P
                        last = nc.tensor.matmul(proj[:, c * C:(c + 1) * C], yT[:, a:a + P], core.w["WoT"][:, kb, :],
                                                start=(kb == 0), stop=(kb == HALVES - 1))
                last.then_inc(proj_ready, 1)

            transpose(0)
            transpose(1)
            project(0)
            with pe.Fori(1, RUNS - 1) as s:
                transpose(s + 1)
                project(s)
            project(RUNS - 1)

        @block.scalar
        def _(act):
            nc.scalar.activation(rstd[:, :], core.var[:, :], ACT.Sqrt, scale=1.0 / RS,
                                 bias=core.eps[:, :]).then_inc(std_ready, 1)

            def copy(s):
                act.wait_ge(onT_ready, s + 1)
                if later(s):
                    act.wait_ge(y_ready, s)
                for half in range(HALVES):
                    last = nc.scalar.activation(onT[:, half * RT:(half + 1) * RT], tr[:, half * RT:(half + 1) * RT],
                                                ACT.Identity, scale=col(core, "gn_w", half), bias=col(core, "gn_b", half))
                last.then_inc(onT_copied, 1)

            copy(0)
            with act.Fori(1, RUNS) as s:
                copy(s)

        @block.vector
        def _(dve):
            def scale(s):
                if later(s):
                    dve.wait_ge(onT_ready, s)
                nc.vector.tensor_tensor(on[:, :].rearrange("p (h j) -> p h j", j=RS),
                                        core.o[:, ds(s, CH * C)].rearrange("p (h j) -> p h j", j=RS),
                                        rstd[:, ds(s, CH * RH)].unsqueeze(2).to_broadcast([P, CH * RH, RS]),
                                        ALU.mult).then_inc(on_ready, 1)

            def gate(s):
                dve.wait_ge(onT_copied, s + 1)
                if later(s):
                    dve.wait_ge(proj_ready, s)
                nc.vector.scalar_tensor_tensor(out=yT[:, :], in0=onT[:, :], scalar=0.5,
                                               in1=core.gate[:, ds(s, HALVES * RT)], op0=ALU.mult,
                                               op1=ALU.mult).then_inc(y_ready, 1)

            def add_residual(s):
                dve.wait_ge(proj_ready, s + 1)
                xs = core.x[:, ds(s, CH * C)]
                nc.vector.tensor_tensor(xs, proj, xs, ALU.add).then_inc(x_ready, 1)
                dve.wait_ge(x_ready, s + 1)
                for c in range(CH):
                    t = s * CH + c
                    nc.vector.bn_stats(core.stats[:, ds(t, 6)], core.x[:, ds(t, C)])

            dve.wait_ge(std_ready, 1)
            nc.vector.reciprocal(rstd[:, :], rstd[:, :]).then_inc(rstd_ready, 1)
            dve.wait_ge(rstd_ready, 1)
            scale(0)
            scale(1)
            gate(0)
            scale(2)
            add_residual(0)
            with dve.Fori(1, RUNS - 2) as s:
                gate(s)
                scale(s + 2)
                add_residual(s)
            for s in (RUNS - 2, RUNS - 1):
                gate(s)
                add_residual(s)


def channel_phase(core, out):
    nc = core.nc
    w = core.w
    with ExitStack() as ctx:
        def sb(name, shape):
            return ctx.enter_context(nc.sbuf_tensor(f"ch_{name}", shape, FP32))

        xn = sb("xn", [P, CH, C])
        xc = sb("xc", [P, HALVES, RB, S + 1])
        sx = sb("sx", [P, HALVES, RB, S])
        xk, xr = sb("xk", [P, HALVES, RT]), sb("xr", [P, HALVES, RT])
        relu = sb("relu", [P, HALVES * RT])
        kk = sb("kk", [P, HALVES * RT])
        rr = sb("rr", [P, CH * C])
        tr, key, recept, value = (core.banks[i] for i in range(4))
        names = ("xn_ready xnT_ready xc_ready first_slot sx_ready mixed_ready key_ready relu_ready kk_ready recept_ready "
                 "rr_ready value_ready rv_ready out_ready stored").split()
        (xn_ready, xnT_ready, xc_ready, first_slot, sx_ready, mixed_ready, key_ready, relu_ready, kk_ready, recept_ready,
         rr_ready, value_ready, rv_ready, out_ready, stored) = semaphores(nc, ctx, *(f"ch_{n}" for n in names))
        block = ctx.enter_context(nc.Block())

        @block.sync
        def _(sp):
            with sp.Fori(0, RUNS) as s:
                sp.wait_ge(out_ready, s + 1)
                sp.dma_start(out[:, ds(s, CH * C)], core.x[:, ds(s, CH * C)]).then_inc(stored, 16)
            sp.wait_ge(stored, 16 * RUNS)

        @block.gpsimd
        def _(pool):
            def square(s):
                pool.wait_ge(relu_ready, s + 1)
                if later(s):
                    pool.wait_ge(value_ready, s)
                nc.gpsimd.tensor_tensor(kk[:, :], relu[:, :], relu[:, :], ALU.mult).then_inc(kk_ready, 1)

            square(0)
            with pool.Fori(1, RUNS) as s:
                square(s)

        @block.tensor
        def _(pe):
            def front(s):
                pe.wait_ge(xn_ready, s + 1)
                if later(s):
                    pe.wait_ge(xc_ready, s)
                for half in range(HALVES):
                    for c in range(CH):
                        a = half * RT + c * P
                        last = nc.tensor.transpose(tr[:, a:a + P], xn[:, c, half * P:(half + 1) * P], core.ident[:, :])
                last.then_inc(xnT_ready, 1)

            def keys(s):
                pe.wait_ge(mixed_ready, s + 1)
                if later(s):
                    pe.wait_ge(relu_ready, s)
                    pe.wait_ge(rr_ready, s)
                for half in range(HALVES):
                    for kb in range(HALVES):
                        last = nc.tensor.matmul(key[:, half * RT:(half + 1) * RT], w["WfkT"][:, kb, half * P:(half + 1) * P],
                                                xk[:, kb, :], start=(kb == 0), stop=(kb == HALVES - 1))
                last.then_inc(key_ready, 1)
                for c in range(CH):
                    for kb in range(HALVES):
                        last = nc.tensor.matmul(recept[:, c * C:(c + 1) * C], xr[:, kb, c * P:(c + 1) * P],
                                                w["WfrT"][:, kb, :], start=(kb == 0), stop=(kb == HALVES - 1))
                last.then_inc(recept_ready, 1)

            def values(s):
                pe.wait_ge(kk_ready, s + 1)
                if later(s):
                    pe.wait_ge(rv_ready, s)
                for c in range(CH):
                    for kb in range(HALVES):
                        a = kb * RT + c * P
                        last = nc.tensor.matmul(value[:, c * C:(c + 1) * C], kk[:, a:a + P],
                                                w["WfvT"][:, kb, :], start=(kb == 0), stop=(kb == HALVES - 1))
                last.then_inc(value_ready, 1)

            front(0)
            front(1)
            keys(0)
            front(2)
            keys(1)
            values(0)
            with pe.Fori(1, RUNS - 2) as s:
                front(s + 2)
                keys(s + 1)
                values(s)
            keys(RUNS - 1)
            values(RUNS - 2)
            values(RUNS - 1)

        @block.scalar
        def _(act):
            def copy_in(s):
                act.wait_ge(xnT_ready, s + 1)
                if later(s):
                    act.wait_ge(mixed_ready, s)
                for half in range(HALVES):
                    last = nc.scalar.activation(xc[:, half, :, 1:S + 1],
                                                tr[:, half * RT:(half + 1) * RT].rearrange("p (b t) -> p b t", t=S),
                                                ACT.Identity, scale=col(core, "r_ln2_w", half),
                                                bias=col(core, "r_ln2_b", half))
                last.then_inc(xc_ready, 1)

            def nonlinear(s):
                act.wait_ge(key_ready, s + 1)
                if later(s):
                    act.wait_ge(kk_ready, s)
                nc.scalar.activation(relu[:, :], key, ACT.Relu).then_inc(relu_ready, 1)
                act.wait_ge(recept_ready, s + 1)
                if later(s):
                    act.wait_ge(out_ready, s)
                nc.scalar.activation(rr[:, :], recept, ACT.Sigmoid).then_inc(rr_ready, 1)

            copy_in(0)
            copy_in(1)
            nonlinear(0)
            with act.Fori(1, RUNS - 1) as s:
                copy_in(s + 1)
                nonlinear(s)
            nonlinear(RUNS - 1)

        @block.vector
        def _(dve):
            def normalise(s):
                if later(s):
                    dve.wait_ge(xnT_ready, s)
                for c in range(CH):
                    t = s * CH + c
                    last = nc.vector.tensor_scalar(xn[:, c, :], core.x[:, ds(t, C)], core.rstd[:, ds(t, 1)],
                                                   core.neg_mean[:, ds(t, 1)], ALU.mult, ALU.add)
                last.then_inc(xn_ready, 1)

            def shift(s):
                nc.vector.tensor_copy(xc[:, :, :, 0], core.state_rows[:, 0, :, ds(s, RB)]).then_inc(first_slot, 1)
                dve.wait_ge(xc_ready, s + 1)
                dve.wait_ge(first_slot, s + 1)
                nc.vector.tensor_tensor(sx[:, :, :, :].rearrange("p h b t -> p (h b) t"),
                                        xc[:, :, :, 0:S].rearrange("p h b t -> p (h b) t"),
                                        xc[:, :, :, 1:S + 1].rearrange("p h b t -> p (h b) t"),
                                        ALU.subtract).then_inc(sx_ready, 1)
                dve.wait_ge(sx_ready, s + 1)
                if later(s):
                    dve.wait_ge(recept_ready, s)
                for half in range(HALVES):
                    for dst, name in ((xk, "ffn_maa_k"), (xr, "ffn_maa_r")):
                        last = nc.vector.scalar_tensor_tensor(
                            out=dst[:, half, :].rearrange("p (b t) -> p b t", t=S), in0=sx[:, half, :, :],
                            scalar=col(core, name, half), in1=xc[:, half, :, 1:S + 1], op0=ALU.mult, op1=ALU.add)
                last.then_inc(mixed_ready, 1)

            def finish(s):
                dve.wait_ge(value_ready, s + 1)
                dve.wait_ge(rr_ready, s + 1)
                nc.vector.tensor_tensor(rr[:, :], value, rr[:, :], ALU.mult).then_inc(rv_ready, 1)
                dve.wait_ge(rv_ready, s + 1)
                xs = core.x[:, ds(s, CH * C)]
                nc.vector.tensor_tensor(xs, rr[:, :], xs, ALU.add).then_inc(out_ready, 1)

            normalise(0)
            normalise(1)
            shift(0)
            normalise(2)
            shift(1)
            finish(0)
            with dve.Fori(1, RUNS - 2) as s:
                normalise(s + 2)
                shift(s + 1)
                finish(s)
            shift(RUNS - 1)
            finish(RUNS - 2)
            finish(RUNS - 1)


FIRST_WEIGHTS = {"w_qkv": (2, 3 * C), "w_ao": (2, C), "w_q": (2, C), "w_kv": (2, 2 * C), "w_co": (2, C),
                 "w1": (2, F1), "w2": (8, C)}
SECOND_WEIGHTS = {"maa_w1": (2, NMIX * DM), "td_w1": (2, DD), "WrT": (2, C), "WkT": (2, C), "WvT": (2, C),
                  "WgT": (2, C), "WoT": (2, C), "WfkT": (2, C), "WfrT": (2, C), "WfvT": (2, C)}


def build(nc, dram, out):
    core = Core()
    core.nc, core.dram = nc, dram
    with ExitStack() as ctx:
        def sb(name, shape, scope=ctx):
            return scope.enter_context(nc.sbuf_tensor(name, shape, FP32))

        def weights(table, scope):
            for k, (kb, n) in table.items():
                core.weights[k] = sb(k, [P, kb * n], scope)
                core.w[k] = core.weights[k][:, :].rearrange("p (k n) -> p k n", k=kb)

        core.weights, core.w = {}, {}
        core.x = sb("x", [P, TILES * C])
        core.cols = sb("cols", [P, NCOLS])
        core.ident = sb("ident", [P, P])
        core.stats = sb("stats", [P, TILES * 6])
        core.norm_tmp = sb("norm_tmp", [P, 3, TILES])
        core.neg_mean = sb("neg_mean", [P, TILES])
        core.rstd = sb("rstd", [P, TILES])
        core.eps = sb("eps", [P, 1])
        core.psum = ctx.enter_context(nc.psum_tensor("psum", [P, 8 * 512], FP32))
        core.banks = [core.psum[:, i * 512:(i + 1) * 512] for i in range(8)]

        with ExitStack() as first:
            core.rows = sb("rows", [P, 3, C], first)
            core.parity = sb("parity", [P, 2], first)
            core.q_bias = sb("q_bias", [P, 2, HALVES], first)
            core.k_bias = sb("k_bias", [P, 2, HALVES, 2], first)
            core.self_mask = sb("self_mask", [P, S], first)
            core.self_bias = sb("self_bias", [P, S], first)
            core.cross_mask = sb("cross_mask", [P, TILES * S], first)
            core.cross_bias = sb("cross_bias", [P, TILES * S], first)
            core.vpad = sb("vpad", [P, BPT, PAIRS, PW], first)
            weights(FIRST_WEIGHTS, first)
            load_phase(core, dram)
            norm_phase(core, "norm1")
            attention_phase(core, False)
            norm_phase(core, "norm2")
            attention_phase(core, True)
            norm_phase(core, "norm3")
            gelu_phase(core)

        core.head_sum = sb("head_sum", [P, HPH])
        core.spread = sb("spread", [P, RS, P])
        core.maa_w2a, core.maa_w2b = sb("maa_w2a", [P, C]), sb("maa_w2b", [DM, C])
        core.td_w2 = sb("td_w2", [DD, C])
        core.state_rows = sb("state_rows", [P, 2, HALVES, B])
        core.state0 = sb("state0", [P, HALVES * RS, B])
        core.o = sb("o", [P, TILES * C])
        core.gate = sb("gate", [P, TILES * C])
        core.var = sb("var", [P, TILES * RH])
        weights(SECOND_WEIGHTS, ctx)
        load_second_phase(core, dram)
        norm_phase(core, "norm4")
        recurrence_phase(core)
        gate_phase(core)
        norm_phase(core, "norm5")
        channel_phase(core, out)


def lay_out(inputs):
    a = {k: np.asarray(v) for k, v in inputs.items()}
    L0, L1 = "L0_xattn_", "L1_xattn_"

    def per_channel(v):
        return v.reshape(-1, P).T

    def rows(w):
        return np.ascontiguousarray(w.reshape(-1, P, w.shape[1]).transpose(1, 0, 2).reshape(P, -1))

    b_qkv, b_kv = a[L0 + "b_qkv"], a[L0 + "b_kv"]
    vectors = {"ln1_s": a[L0 + "ln1_s"], "ln1_b": a[L0 + "ln1_b"], "b_q_self": b_qkv[:C], "b_k_self": b_qkv[C:2 * C],
               "b_v_self": b_qkv[2 * C:], "ln2_s": a[L0 + "ln2_s"], "ln2_b": a[L0 + "ln2_b"],
               "b_q_cross": a[L0 + "b_q"], "b_k_cross": b_kv[:C], "b_v_cross": b_kv[C:], "ln3_s": a[L0 + "ln3_s"],
               "ln3_b": a[L0 + "ln3_b"], "b1": a[L0 + "b1"], "r_ln1_w": a[L1 + "ln1_w"], "r_ln1_b": a[L1 + "ln1_b"],
               "r_ln2_w": a[L1 + "ln2_w"], "r_ln2_b": a[L1 + "ln2_b"], "maa_x": a[L1 + "maa_x"],
               "maa_stack": a[L1 + "maa_stack"].reshape(-1), "time_decay": a[L1 + "time_decay"],
               "u": a[L1 + "u"].reshape(-1), "gn_w": a[L1 + "gn_w"], "gn_b": a[L1 + "gn_b"],
               "ffn_maa_k": a[L1 + "ffn_maa_k"], "ffn_maa_r": a[L1 + "ffn_maa_r"]}
    ctx = a["ctx_2048"]
    p = np.arange(P)
    out = {
        "x": rows(a["x"].reshape(B * S, C)),
        "cols": np.ascontiguousarray(np.concatenate([per_channel(vectors[k]) for k in COLS], axis=1)),
        "rows": np.ascontiguousarray(np.stack([a[L0 + "b_ao"], a[L0 + "b_co"], a[L0 + "b2"]])),
        "enc": np.ascontiguousarray(ctx.reshape(B * S, HALVES, P).transpose(2, 1, 0)),
        "cross_mask": rows(a["mask_Bx1xSxS2_ff1"].reshape(B * S, S)),
        "self_mask": np.ascontiguousarray(np.concatenate([a["mask_1x1xSxS2_fc1"].reshape(S, S)] * 2)),
        "ident": np.eye(P, dtype=np.float32),
        "parity": np.ascontiguousarray(((p[:, None] // HD) % 2 == np.arange(2)[None, :]).astype(np.float32)),
        "head_sum": np.ascontiguousarray((p[:, None] // RS == np.arange(HPH)[None, :]).astype(np.float32)),
    }
    q = np.arange(P)
    same_head = (p[:, None] // RS == q[None, :] // RS)
    out["spread"] = np.ascontiguousarray(np.stack(
        [(same_head & (p[:, None] % RS == j)).astype(np.float32) for j in range(RS)], axis=1))
    out["maa_w2"] = np.ascontiguousarray(a[L1 + "maa_w2"].reshape(NMIX * DM, C))
    out["td_w2"] = np.ascontiguousarray(a[L1 + "td_w2"])
    out["state_rows"] = np.ascontiguousarray(ctx[:, 0:2, :].reshape(B, 2, HALVES, P).transpose(3, 1, 2, 0))
    out["state0"] = np.ascontiguousarray(
        ctx[:, 2:2 + RS, :].reshape(B, HALVES, P, RS).transpose(2, 1, 3, 0).reshape(P, HALVES * RS, B))
    for k in FIRST_WEIGHTS:
        out[k] = rows(a[L0 + k])
    for k in SECOND_WEIGHTS:
        out[k] = rows(a[L1 + k[:-1]].T) if k[0] == "W" else rows(a[L1 + k])
    return out


def kernel(**inputs):
    import concourse.bacc as bacc
    from concourse.bass_utils import run_bass_kernel_spmd

    nc = bacc.Bacc("TRN2", target_bir_lowering=False, num_devices=1)
    arrays = lay_out(inputs)
    dram = {k: nc.dram_tensor(f"in_{k}", v.shape, mybir.dt.from_np(v.dtype), kind="ExternalInput").ap()
            for k, v in arrays.items()}
    out = nc.dram_tensor("out", [P, TILES * C], FP32, kind="ExternalOutput").ap()
    build(nc, dram, out)
    result = run_bass_kernel_spmd(nc, [{f"in_{k}": v for k, v in arrays.items()}], core_ids=[0]).results[0]["out"]
    return np.ascontiguousarray(result.reshape(P, TILES, C).transpose(1, 0, 2).reshape(B, S, C))
```

```python
import concourse.bass as bass
from concourse import mybir
from contextlib import ExitStack
import numpy as np

FP32 = mybir.dt.float32
ALU = mybir.AluOpType
ACT = mybir.ActivationFunctionType
AX = mybir.AxisListType

B, S, C = 64, 64, 256
P = 128
HALVES = C // P
TILES = B * S // P
BPT = P // S
NH, HD = 16, 16
PAIRS = NH // 2
POOL_GROUPS, ACT_GROUPS = (0, 1), (2, 3)
PW = 2 * HD + 2
F1 = 4 * C
EPS = 1e-5
MASKED = 10000.0
RH, RS = 32, 8
HPH = RH // HALVES
DM, DD, NMIX = 32, 64, 5

COLS = {}
for _name, _n in (("ln1_s", 2), ("ln1_b", 2), ("b_q_self", 2), ("b_k_self", 2), ("b_v_self", 2),
                  ("ln2_s", 2), ("ln2_b", 2), ("b_q_cross", 2), ("b_k_cross", 2), ("b_v_cross", 2),
                  ("ln3_s", 2), ("ln3_b", 2), ("b1", 8), ("r_ln1_w", 2), ("r_ln1_b", 2),
                  ("r_ln2_w", 2), ("r_ln2_b", 2), ("maa_x", 2), ("maa_stack", 2 * NMIX),
                  ("time_decay", 2), ("u", 2), ("gn_w", 2), ("gn_b", 2), ("ffn_maa_k", 2),
                  ("ffn_maa_r", 2)):
    COLS[_name] = (sum(n for _, n in COLS.values()), _n)
NCOLS = sum(n for _, n in COLS.values())


def ds(t, n):
    return bass.ds(t * n, n)


def later(n):
    return not isinstance(n, int) or n > 0


class Core:
    pass


def semaphores(nc, ctx, *names):
    return [ctx.enter_context(nc.semaphore(n)) for n in names]


def col(core, name, i):
    return core.cols[:, COLS[name][0] + i:COLS[name][0] + i + 1]


def load_phase(core, dram):
    nc = core.nc
    with ExitStack() as ctx:
        loaded, prepared = semaphores(nc, ctx, "loaded", "prepared")
        block = ctx.enter_context(nc.Block())
        loads = [(core.x[:, :], dram["x"]), (core.cols[:, :], dram["cols"]), (core.ident[:, :], dram["ident"]),
                 (core.parity[:, :], dram["parity"]),
                 (core.self_mask[:, :], dram["self_mask"]), (core.cross_mask[:, :], dram["cross_mask"])]
        for name in FIRST_WEIGHTS:
            loads.append((core.weights[name][:, :], dram[name]))
        for n in range(3):
            loads.append((core.rows[:, n, :], dram["rows"][n:n + 1, :].partition_broadcast(P)))
        split = len(loads) // 2

        @block.sync
        def _(sp):
            for dst, src in loads[:split]:
                sp.dma_start(dst, src).then_inc(loaded, 16)
            sp.wait_ge(loaded, 16 * len(loads))

        @block.gpsimd
        def _(pool):
            nc.gpsimd.memset(core.vpad[:, :, :], 0.0).then_inc(prepared, 1)
            nc.gpsimd.memset(core.eps[:, :], EPS).then_inc(prepared, 1)
            nc.gpsimd.memset(core.k_heads[:, :, :, :], 0.0).then_inc(prepared, 1)
            pool.wait_ge(prepared, 3)
            for e in range(2):
                for b in range(BPT):
                    a = b * PW + 2 * HD + e
                    nc.gpsimd.memset(core.vpad[e * S:(e + 1) * S, :, a:a + 1], 1.0).then_inc(prepared, 1)
            pool.wait_ge(prepared, 7)

        @block.scalar
        def _(act):
            for dst, src in loads[split:]:
                act.dma_start(dst, src).then_inc(loaded, 16)


        @block.vector
        def _(dve):
            dve.wait_ge(loaded, 16 * len(loads))
            for n, q in enumerate(("b_q_self", "b_q_cross")):
                a = COLS[q][0]
                nc.vector.tensor_scalar_mul(core.q_bias[:, n, :], core.cols[:, a:a + 2], HD ** -0.5)
            for bias, mask in ((core.self_bias, core.self_mask), (core.cross_bias, core.cross_mask)):
                nc.vector.tensor_scalar(bias[:, :], mask[:, :], -1.0, MASKED, ALU.add, ALU.mult)

    with ExitStack() as ctx:
        [stats_of] = semaphores(nc, ctx, "first_stats")
        block = ctx.enter_context(nc.Block())

        @block.vector
        def _(dve):
            with dve.Fori(0, TILES) as t:
                nc.vector.bn_stats(core.stats[:, ds(t, 6)], core.x[:, ds(t, C)])


def load_second_phase(core, dram):
    nc = core.nc
    with ExitStack() as ctx:
        [loaded] = semaphores(nc, ctx, "second_loaded")
        block = ctx.enter_context(nc.Block())
        loads = [(core.head_sum[:, :, :], dram["head_sum"]), (core.spread[:, :, :], dram["spread"]),
                 (core.maa_w2a[:, :], dram["maa_w2"][0:P, :]), (core.maa_w2b[:, :], dram["maa_w2"][P:P + DM, :]),
                 (core.td_w2[:, :], dram["td_w2"]), (core.state_rows[:, :, :, :], dram["state_rows"]),
                 (core.state0[:, :, :], dram["state0"])]
        loads += [(core.weights[name][:, :], dram[name]) for name in SECOND_WEIGHTS]

        @block.sync
        def _(sp):
            for dst, src in loads[0::2]:
                sp.dma_start(dst, src).then_inc(loaded, 16)
            sp.wait_ge(loaded, 16 * len(loads))

        @block.scalar
        def _(act):
            for dst, src in loads[1::2]:
                act.dma_start(dst, src).then_inc(loaded, 16)


def norm_phase(core, name):
    nc = core.nc
    with ExitStack() as ctx:
        step, var_ready, std_ready = semaphores(nc, ctx, f"{name}_step", f"{name}_var_ready", f"{name}_std_ready")
        block = ctx.enter_context(nc.Block())
        st = core.stats[:, :].rearrange("p (t s) -> p t s", s=6)
        mean_even, m2_even, mean_odd, m2_odd = (st[:, :, i] for i in (1, 2, 4, 5))
        a, b, c = (core.norm_tmp[:, i, :] for i in range(3))

        @block.vector
        def _(dve):
            nc.vector.tensor_tensor(a, m2_even, m2_odd, ALU.add)
            nc.vector.tensor_tensor(b, mean_even, mean_odd, ALU.subtract)
            nc.vector.tensor_tensor(core.neg_mean[:, :], mean_even, mean_odd, ALU.add).then_inc(step, 1)
            dve.wait_ge(step, 1)
            nc.vector.tensor_tensor(b, b, b, ALU.mult).then_inc(step, 1)
            dve.wait_ge(step, 2)
            nc.vector.tensor_scalar(b, b, 0.25, None, ALU.mult).then_inc(step, 1)
            dve.wait_ge(step, 3)
            nc.vector.scalar_tensor_tensor(out=c, in0=a, scalar=1.0 / C, in1=b, op0=ALU.mult,
                                           op1=ALU.add).then_inc(var_ready, 1)
            dve.wait_ge(std_ready, 1)
            nc.vector.reciprocal(core.rstd[:, :], a).then_inc(step, 1)
            dve.wait_ge(step, 4)
            nc.vector.scalar_tensor_tensor(out=core.neg_mean[:, :], in0=core.neg_mean[:, :], scalar=-0.5,
                                           in1=core.rstd[:, :], op0=ALU.mult, op1=ALU.mult)

        @block.scalar
        def _(act):
            act.wait_ge(var_ready, 1)
            nc.scalar.activation(a, c, ACT.Sqrt, bias=core.eps[:, :]).then_inc(std_ready, 1)


def attention_phase(core, cross):
    nc = core.nc
    kind = "cross" if cross else "self"
    n = int(cross)
    ln_s, ln_b = ("ln2_s", "ln2_b") if cross else ("ln1_s", "ln1_b")
    wq, q0 = (core.w["w_q"], 0) if cross else (core.w["w_qkv"], 0)
    wk, k0 = (core.w["w_kv"], 0) if cross else (core.w["w_qkv"], C)
    wv, v0 = (core.w["w_kv"], C) if cross else (core.w["w_qkv"], 2 * C)
    wo = core.w["w_co"] if cross else core.w["w_ao"]
    with ExitStack() as ctx:
        def sb(name, shape):
            return ctx.enter_context(nc.sbuf_tensor(f"{kind}_{name}", shape, FP32))

        xn = sb("xn", [P, C])
        lnT = sb("lnT", [P, HALVES, P])
        qT = sb("qT", [P, HALVES, P])
        kT = sb("kT", [P, HALVES * BPT, S])
        k_heads = core.k_heads
        z = sb("z", [P, NH, S])
        probs = sb("probs", [P, NH * S])
        zT = sb("zT", [P, PAIRS, P])
        row_max = sb("row_max", [P, NH])
        recip = sb("recip", [P, NH])
        heads = sb("heads", [P, C])
        headsT = sb("headsT", [P, HALVES, P])
        encT = sb("encT", [P, HALVES, P]) if cross else None
        kvT = encT if cross else lnT

        tr, qk, vv, proj = (core.banks[i] for i in (0, 1, 2, 7))
        tr, trh = tr[:, 0:C], tr[:, C:2 * C]
        scores = core.psum[:, 3 * 512:5 * 512].rearrange("p (h k) -> p h k", k=S)
        outs = core.psum[:, 3 * 512:5 * 512].rearrange("p (r n) -> p r n", n=P)
        pT = core.psum[:, 5 * 512:7 * 512]

        names = ("xn_ready xnT_ready ln_ready qk_ready v_ready q_copied v_copied scores_ready masked biased max_ready "
                 "shifted probs_ready probsT_ready probsT_copied out_ready recip_ready heads_ready headsT_ready "
                 "headsT_copied proj_ready x_ready bias_added enc_loaded k_copied k_spread_pool k_spread_act").split()
        (xn_ready, xnT_ready, ln_ready, qk_ready, v_ready, q_copied, v_copied, scores_ready, masked, biased, max_ready,
         shifted, probs_ready, probsT_ready, probsT_copied, out_ready, recip_ready, heads_ready, headsT_ready,
         headsT_copied, proj_ready, x_ready, bias_added, enc_loaded, k_copied, k_spread_pool,
         k_spread_act) = semaphores(nc, ctx, *(f"{kind}_{s}" for s in names))
        block = ctx.enter_context(nc.Block())

        def there(t):
            return not isinstance(t, int) or t < TILES

        if cross:
            @block.sync
            def _(sp):
                def load(t):
                    sp.dma_start(encT[:, :, :], core.dram["enc"][:, :, ds(t, P)]).then_inc(enc_loaded, 16)

                load(0)
                with sp.Fori(1, TILES) as t:
                    sp.wait_ge(v_ready, t)
                    load(t)

        def spread_keys(eng, groups):
            for g in groups:
                rows = slice(32 * g, 32 * (g + 1))
                last = eng.tensor_tensor(
                    k_heads[rows, :, 2 * g:2 * g + 2, :],
                    kT[rows, :, :].unsqueeze(2).to_broadcast([32, HALVES * BPT, 2, S]),
                    core.parity[rows, :].unsqueeze(1).unsqueeze(3).to_broadcast([32, HALVES * BPT, 2, S]), ALU.mult)
            return last

        @block.gpsimd
        def _(pool):
            def add_bias(t):
                pool.wait_ge(xn_ready, t + 1)
                if later(t):
                    pool.wait_ge(k_spread_pool, t)
                xt = core.x[:, ds(t, C)]
                nc.gpsimd.tensor_tensor(xt, xt, core.rows[:, n, :], ALU.add).then_inc(bias_added, 1)

            def spread(t):
                pool.wait_ge(bias_added, t + 1)
                pool.wait_ge(k_copied, t + 1)
                spread_keys(nc.gpsimd, POOL_GROUPS).then_inc(k_spread_pool, 1)

            add_bias(0)
            spread(0)
            with pool.Fori(1, TILES) as t:
                add_bias(t)
                spread(t)

        @block.tensor
        def _(pe):
            def transpose_in(t):
                pe.wait_ge(xn_ready, t + 1)
                if later(t):
                    pe.wait_ge(ln_ready, t)
                if later(t - 3):
                    pe.wait_ge(headsT_copied, t - 3)
                for half in range(HALVES):
                    last = nc.tensor.transpose(tr[:, half * P:(half + 1) * P], xn[:, half * P:(half + 1) * P],
                                               core.ident[:, :])
                last.then_inc(xnT_ready, 1)

            def project_qk(t):
                pe.wait_ge(ln_ready, t + 1)
                if cross:
                    pe.wait_ge(enc_loaded, 16 * t + 16)
                for dst, w, c0, src in ((0, wq, q0, lnT), (HALVES, wk, k0, kvT)):
                    for half in range(HALVES):
                        for kb in range(HALVES):
                            last = nc.tensor.matmul(
                                qk[:, (dst + half) * P:(dst + half + 1) * P],
                                w[:, kb, c0 + half * P:c0 + (half + 1) * P], src[:, kb, :],
                                start=(kb == 0), stop=(kb == HALVES - 1))
                last.then_inc(qk_ready, 1)

            def project_v(t):
                if later(t):
                    pe.wait_ge(v_copied, t)
                for kb in range(HALVES):
                    last = nc.tensor.matmul(vv[:, 0:C], kvT[:, kb, :], wv[:, kb, v0:v0 + C],
                                            start=(kb == 0), stop=(kb == HALVES - 1))
                last.then_inc(v_ready, 1)

            def score(t):
                pe.wait_ge(q_copied, t + 1)
                pe.wait_ge(k_spread_pool, t + 1)
                pe.wait_ge(k_spread_act, t * len(ACT_GROUPS) + len(ACT_GROUPS))
                if later(t):
                    pe.wait_ge(masked, t)
                if later(t - 1):
                    pe.wait_ge(heads_ready, t - 1)
                for half in range(HALVES):
                    for b in range(BPT):
                        last = nc.tensor.matmul(
                            scores[b * S:(b + 1) * S, half * PAIRS:(half + 1) * PAIRS, :],
                            qT[:, half, b * S:(b + 1) * S], k_heads[:, half * BPT + b, :, :], start=True, stop=True)
                last.then_inc(scores_ready, 1)

            def transpose_probs(t):
                pe.wait_ge(probs_ready, t + 1)
                if later(t):
                    pe.wait_ge(probsT_copied, t)
                for pair in range(PAIRS):
                    last = nc.tensor.transpose(pT[:, pair * P:(pair + 1) * P], probs[:, pair * P:(pair + 1) * P],
                                               core.ident[:, :])
                last.then_inc(probsT_ready, 1)

            def attend(t):
                pe.wait_ge(probsT_copied, t + 1)
                pe.wait_ge(v_copied, t + 1)
                if there(t + 1):
                    pe.wait_ge(masked, t + 2)
                for pair in range(PAIRS):
                    last = nc.tensor.matmul(outs[:, pair, :], zT[:, pair, :], core.vpad[:, pair, :],
                                            start=True, stop=True)
                last.then_inc(out_ready, 1)

            def transpose_heads(t):
                pe.wait_ge(heads_ready, t + 1)
                if later(t):
                    pe.wait_ge(headsT_copied, t)
                for half in range(HALVES):
                    last = nc.tensor.transpose(trh[:, half * P:(half + 1) * P], heads[:, half * P:(half + 1) * P],
                                               core.ident[:, :])
                last.then_inc(headsT_ready, 1)

            def project_out(t):
                pe.wait_ge(headsT_copied, t + 1)
                if later(t):
                    pe.wait_ge(x_ready, t)
                for kb in range(HALVES):
                    last = nc.tensor.matmul(proj[:, 0:C], headsT[:, kb, :], wo[:, kb, :],
                                            start=(kb == 0), stop=(kb == HALVES - 1))
                last.then_inc(proj_ready, 1)

            def body(t):
                if there(t + 1):
                    score(t + 1)
                if there(t + 2):
                    project_qk(t + 2)
                attend(t)
                if later(t):
                    project_out(t - 1)
                if there(t + 2):
                    project_v(t + 2)
                if there(t + 1):
                    transpose_probs(t + 1)
                if there(t + 3):
                    transpose_in(t + 3)
                transpose_heads(t)

            transpose_in(0)
            project_qk(0)
            project_v(0)
            transpose_in(1)
            score(0)
            project_qk(1)
            project_v(1)
            transpose_in(2)
            transpose_probs(0)
            body(0)
            with pe.Fori(1, TILES - 3) as t:
                body(t)
            for t in range(TILES - 3, TILES):
                body(t)
            project_out(TILES - 1)

        @block.scalar
        def _(act):
            def normalise(t):
                if later(t):
                    act.wait_ge(xnT_ready, t)
                nc.scalar.activation(xn[:, :], core.x[:, ds(t, C)], ACT.Identity, scale=core.rstd[:, ds(t, 1)],
                                     bias=core.neg_mean[:, ds(t, 1)]).then_inc(xn_ready, 1)

            def copy_ln(t):
                act.wait_ge(xnT_ready, t + 1)
                if later(t):
                    act.wait_ge(v_ready, t)
                if later(t - 2):
                    act.wait_ge(headsT_ready, t - 2)
                for half in range(HALVES):
                    last = nc.scalar.activation(lnT[:, half, :], tr[:, half * P:(half + 1) * P], ACT.Identity,
                                                scale=col(core, ln_s, half), bias=col(core, ln_b, half))
                last.then_inc(ln_ready, 1)

            def copy_qk(t):
                act.wait_ge(qk_ready, t + 1)
                if later(t):
                    act.wait_ge(scores_ready, t)
                    act.wait_ge(k_spread_pool, t)
                for half in range(HALVES):
                    last = nc.scalar.activation(
                        kT[:, half * BPT:(half + 1) * BPT, :].rearrange("p b k -> p (b k)"),
                        qk[:, (HALVES + half) * P:(HALVES + half + 1) * P], ACT.Identity,
                        bias=col(core, f"b_k_{kind}", half))
                last.then_inc(k_copied, 1)
                for half in range(HALVES):
                    last = nc.scalar.activation(qT[:, half, :], qk[:, half * P:(half + 1) * P], ACT.Identity,
                                                scale=HD ** -0.5, bias=core.q_bias[:, n, half:half + 1])
                last.then_inc(q_copied, 1)

            def spread(t, g):
                act.wait_ge(k_copied, t + 1)
                rows = slice(32 * g, 32 * (g + 1))
                for e in range(2):
                    last = nc.scalar.activation(k_heads[rows, :, 2 * g + e, :], kT[rows, :, :], ACT.Copy,
                                                scale=core.parity[rows, e:e + 1])
                last.then_inc(k_spread_act, 1)

            def copy_values(t):
                act.wait_ge(v_ready, t + 1)
                if later(t):
                    act.wait_ge(out_ready, t)
                for e in range(2):
                    for b in range(BPT):
                        a = b * PW + e * HD
                        last = nc.scalar.activation(
                            core.vpad[e * S:(e + 1) * S, :, a:a + HD],
                            vv[b * S:(b + 1) * S, 0:C].rearrange("p (r e d) -> p r e d", r=PAIRS, e=2)[:, :, e, :],
                            ACT.Copy)
                last.then_inc(v_copied, 1)

            def exps(t):
                act.wait_ge(shifted, t + 1)
                if later(t):
                    act.wait_ge(probsT_ready, t)
                nc.scalar.activation(probs[:, :], z[:, :, :].rearrange("p h k -> p (h k)"),
                                     ACT.Exp).then_inc(probs_ready, 1)

            def copy_probs(t):
                act.wait_ge(probsT_ready, t + 1)
                if later(t):
                    act.wait_ge(out_ready, t)
                for j in range(2):
                    last = nc.scalar.activation(zT[:, j * PAIRS // 2:(j + 1) * PAIRS // 2, :],
                                                pT[:, j * 512:(j + 1) * 512], ACT.Copy)
                last.then_inc(probsT_copied, 1)

            def copy_heads(t):
                act.wait_ge(headsT_ready, t + 1)
                if later(t):
                    act.wait_ge(proj_ready, t)
                for half in range(HALVES):
                    last = nc.scalar.activation(headsT[:, half, :], trh[:, half * P:(half + 1) * P], ACT.Identity,
                                                bias=col(core, f"b_v_{kind}", half))
                last.then_inc(headsT_copied, 1)

            def body(t):
                copy_probs(t)
                if there(t + 2):
                    copy_ln(t + 2)
                if later(t):
                    copy_heads(t - 1)
                if there(t + 2):
                    copy_qk(t + 2)
                    spread(t + 2, ACT_GROUPS[0])
                if there(t + 1):
                    copy_values(t + 1)
                if there(t + 2):
                    spread(t + 2, ACT_GROUPS[1])
                if there(t + 1):
                    exps(t + 1)
                if there(t + 3):
                    normalise(t + 3)

            normalise(0)
            copy_ln(0)
            normalise(1)
            copy_qk(0)
            for g in ACT_GROUPS:
                spread(0, g)
            copy_values(0)
            copy_ln(1)
            normalise(2)
            copy_qk(1)
            for g in ACT_GROUPS:
                spread(1, g)
            exps(0)
            body(0)
            with act.Fori(1, TILES - 3) as t:
                body(t)
            for t in range(TILES - 3, TILES):
                body(t)
            copy_heads(TILES - 1)

        @block.vector
        def _(dve):
            def apply_mask(t):
                mask = core.cross_mask[:, ds(t, S)] if cross else core.self_mask[:, :]
                dve.wait_ge(scores_ready, t + 1)
                if later(t):
                    dve.wait_ge(probs_ready, t)
                nc.vector.tensor_tensor(z[:, :, :], scores, mask.unsqueeze(1).to_broadcast([P, NH, S]),
                                        ALU.mult).then_inc(masked, 1)

            def subtract_max(t):
                bias = core.cross_bias[:, ds(t, S)] if cross else core.self_bias[:, :]
                dve.wait_ge(masked, t + 1)
                nc.vector.tensor_tensor(z[:, :, :], z[:, :, :], bias.unsqueeze(1).to_broadcast([P, NH, S]),
                                        ALU.add).then_inc(biased, 1)
                dve.wait_ge(biased, t + 1)
                nc.vector.tensor_reduce(out=row_max[:, :], in_=z[:, :, :], op=ALU.max, axis=AX.X).then_inc(max_ready, 1)
                dve.wait_ge(max_ready, t + 1)
                nc.vector.tensor_tensor(z[:, :, :], z[:, :, :], row_max[:, :].unsqueeze(2).to_broadcast([P, NH, S]),
                                        ALU.subtract).then_inc(shifted, 1)

            def divide(t):
                dve.wait_ge(out_ready, t + 1)
                for b in range(BPT):
                    rows = slice(b * S, (b + 1) * S)
                    last = nc.vector.reciprocal(recip[rows, :].rearrange("p (r e) -> p r e", e=2),
                                                outs[rows, :, b * PW + 2 * HD:(b + 1) * PW])
                last.then_inc(recip_ready, 1)
                dve.wait_ge(recip_ready, t + 1)
                if later(t):
                    dve.wait_ge(headsT_ready, t)
                for b in range(BPT):
                    rows = slice(b * S, (b + 1) * S)
                    last = nc.vector.tensor_tensor(
                        heads[rows, :].rearrange("p (r e d) -> p r e d", e=2, d=HD),
                        outs[rows, :, b * PW:b * PW + 2 * HD].rearrange("p r (e d) -> p r e d", e=2),
                        recip[rows, :].rearrange("p (r e) -> p r e", e=2).unsqueeze(3).to_broadcast([S, PAIRS, 2, HD]),
                        ALU.mult)
                last.then_inc(heads_ready, 1)

            def add_residual(t):
                xt = core.x[:, ds(t, C)]
                dve.wait_ge(proj_ready, t + 1)
                dve.wait_ge(bias_added, t + 1)
                nc.vector.tensor_tensor(xt, proj[:, 0:C], xt, ALU.add).then_inc(x_ready, 1)
                dve.wait_ge(x_ready, t + 1)
                nc.vector.bn_stats(core.stats[:, ds(t, 6)], xt)

            def body(t):
                if there(t + 1):
                    apply_mask(t + 1)
                    subtract_max(t + 1)
                divide(t)
                if later(t):
                    add_residual(t - 1)

            apply_mask(0)
            subtract_max(0)
            body(0)
            with dve.Fori(1, TILES - 1) as t:
                body(t)
            body(TILES - 1)
            add_residual(TILES - 1)


def gelu_phase(core):
    nc = core.nc
    n4 = 4
    runs, hidden = TILES // n4, F1 // P
    w1, w2 = core.w["w1"], core.w["w2"]
    with ExitStack() as ctx:
        def sb(name, shape):
            return ctx.enter_context(nc.sbuf_tensor(f"gelu_{name}", shape, FP32))

        xn = sb("xn", [P, n4, C])
        lnT = sb("lnT", [P, HALVES, n4 * P])
        hT = sb("hT", [P, hidden, n4 * P])
        tr = core.banks[0:2]
        up_banks = core.banks[2:5]
        down_banks = core.banks[5:7]
        names = ("xn_ready", "xnT_ready", "ln_ready", "up_ready", "gelu_ready", "down_ready", "x_ready", "bias_added")
        (xn_ready, xnT_ready, ln_ready, up_ready, gelu_ready, down_ready, x_ready,
         bias_added) = semaphores(nc, ctx, *(f"gelu_{s}" for s in names))
        block = ctx.enter_context(nc.Block())

        @block.gpsimd
        def _(pool):
            with pool.Fori(0, runs) as s:
                pool.wait_ge(xn_ready, s + 1)
                xs = core.x[:, ds(s, n4 * C)].rearrange("p (j c) -> p j c", j=n4)
                nc.gpsimd.tensor_tensor(xs, xs, core.rows[:, 2, :].unsqueeze(1).to_broadcast([P, n4, C]),
                                        ALU.add).then_inc(bias_added, 1)

        @block.tensor
        def _(pe):
            def transpose(s):
                pe.wait_ge(xn_ready, s + 1)
                if later(s):
                    pe.wait_ge(ln_ready, s)
                for half in range(HALVES):
                    for j in range(n4):
                        last = nc.tensor.transpose(tr[half][:, j * P:(j + 1) * P],
                                                   xn[:, j, half * P:(half + 1) * P], core.ident[:, :])
                last.then_inc(xnT_ready, 1)

            def up(s):
                pe.wait_ge(ln_ready, s + 1)
                for h in range(hidden):
                    if h >= len(up_banks) or later(s):
                        pe.wait_ge(gelu_ready, s * hidden + h + 1 - len(up_banks))
                    for kb in range(HALVES):
                        last = nc.tensor.matmul(up_banks[h % len(up_banks)], w1[:, kb, h * P:(h + 1) * P],
                                                lnT[:, kb, :], start=(kb == 0), stop=(kb == HALVES - 1))
                    last.then_inc(up_ready, 1)

            def down(s):
                pe.wait_ge(gelu_ready, s * hidden + hidden)
                if later(s):
                    pe.wait_ge(x_ready, s * n4)
                for j in range(n4):
                    for h in range(hidden):
                        last = nc.tensor.matmul(down_banks[j // 2][:, (j % 2) * C:(j % 2 + 1) * C],
                                                hT[:, h, j * P:(j + 1) * P], w2[:, h, :],
                                                start=(h == 0), stop=(h == hidden - 1))
                    if j % 2:
                        last.then_inc(down_ready, 1)

            transpose(0)
            up(0)
            transpose(1)
            down(0)
            with pe.Fori(1, runs - 1) as s:
                up(s)
                transpose(s + 1)
                down(s)
            up(runs - 1)
            down(runs - 1)

        @block.scalar
        def _(act):
            def copy_in(s):
                act.wait_ge(xnT_ready, s + 1)
                for half in range(HALVES):
                    last = nc.scalar.activation(lnT[:, half, :], tr[half], ACT.Identity,
                                                scale=col(core, "ln3_s", half), bias=col(core, "ln3_b", half))
                last.then_inc(ln_ready, 1)

            def gelus(s):
                if later(s):
                    act.wait_ge(down_ready, 2 * s)
                for h in range(hidden):
                    act.wait_ge(up_ready, s * hidden + h + 1)
                    nc.scalar.activation(hT[:, h, :], up_banks[h % len(up_banks)], ACT.Gelu_apprx_tanh,
                                         bias=col(core, "b1", h)).then_inc(gelu_ready, 1)

            copy_in(0)
            gelus(0)
            copy_in(1)
            with act.Fori(1, runs - 1) as s:
                gelus(s)
                copy_in(s + 1)
            gelus(runs - 1)

        @block.vector
        def _(dve):
            def normalise(s):
                if later(s):
                    dve.wait_ge(xnT_ready, s)
                for j in range(n4):
                    t = s * n4 + j
                    last = nc.vector.tensor_scalar(xn[:, j, :], core.x[:, ds(t, C)], core.rstd[:, ds(t, 1)],
                                                   core.neg_mean[:, ds(t, 1)], ALU.mult, ALU.add)
                last.then_inc(xn_ready, 1)

            def add_residual(s):
                for j in range(n4):
                    t = s * n4 + j
                    if j % 2 == 0:
                        dve.wait_ge(down_ready, 2 * s + j // 2 + 1)
                    if j == 0:
                        dve.wait_ge(bias_added, s + 1)
                    xt = core.x[:, ds(t, C)]
                    nc.vector.tensor_tensor(xt, down_banks[j // 2][:, (j % 2) * C:(j % 2 + 1) * C], xt,
                                            ALU.add).then_inc(x_ready, 1)
                for j in range(n4):
                    t = s * n4 + j
                    dve.wait_ge(x_ready, t + 1)
                    nc.vector.bn_stats(core.stats[:, ds(t, 6)], core.x[:, ds(t, C)])

            normalise(0)
            normalise(1)
            add_residual(0)
            with dve.Fori(1, runs - 1) as s:
                normalise(s + 1)
                add_residual(s)
            add_residual(runs - 1)


MIX = (1, 0, 3, 2, 4)
NW, NK, NR, NV, NG = range(NMIX)
CH = 2
RT = CH * P
RB = RT // S
RUNS = B * S // RT
JG = 2
GROUPS_R = HALVES * RS // JG
JQ = P // RH
SUMS = GROUPS_R * JG // JQ


def group(n):
    q, part = divmod(n, JQ // JG)
    return q % HALVES, q // HALVES * JQ + part * JG


def recurrence_phase(core):
    nc = core.nc
    w = core.w
    with ExitStack() as ctx:
        def sb(name, shape):
            return ctx.enter_context(nc.sbuf_tensor(f"rec_{name}", shape, FP32))

        xn = sb("xn", [P, CH, C])
        xa = sb("xa", [P, HALVES, RB, S + 1])
        sx = sb("sx", [P, HALVES, RB, S])
        xin = sb("xin", [P, HALVES, RT])
        mixer_a, mixer_b = sb("mixer_a", [P, RT]), sb("mixer_b", [DM, RT])
        mixed = sb("mixed", [P, 2, HALVES, RT])
        xm = sb("xm", [P, 2, HALVES, RT])
        decay_in = sb("decay_in", [DD, RT])
        decay_exp = sb("decay_exp", [P, HALVES * RB, S])
        gate_tanh = sb("gate_tanh", [P, HALVES * RT])
        kT = sb("kT", [P, 2, HALVES, RB, S])
        rT = sb("rT", [P, 2, HALVES, RT])
        vT = sb("vT", [P, 2, HALVES, RT])
        wT = sb("wT", [P, 2, HALVES * RB, S])
        bonus = sb("bonus", [P, HALVES, RT])
        bonus_v = sb("bonus_v", [P, HALVES, RT])
        st = sb("st", [P, GROUPS_R, JG, RB, S])
        o = sb("o", [P, HALVES * RT])
        o_sq = sb("o_sq", [P, CH * C])
        mean = sb("mean", [P, CH * RH])

        tr, small = core.banks[0], core.banks[1]
        mix_banks, proj_banks = core.banks[2:4], core.banks[4:6]
        v_bank, o_bank = core.banks[6], core.banks[7]

        names = ("xn_ready xnT_ready xa_ready first_slot sx_ready xin_ready mixer_ready mixer_tanh mix_ready mixed_ready "
                 "xm_ready decay_ready decay_tanh proj_ready copied gate_ready gate_done decay_expd w_ready oT_ready "
                 "bonus_ready bonus_sum_ready vj_ready kv_ready slot_ready scanned read_ready summed "
                 "o_bonus o_ready mean_ready mean_scaled o_stored sq_ready var_stored").split()
        sem = dict(zip(names, semaphores(nc, ctx, *(f"rec_{n}" for n in names))))
        (xn_ready, xnT_ready, xa_ready, first_slot, sx_ready, xin_ready, mixer_ready, mixer_tanh, mix_ready, mixed_ready,
         xm_ready, decay_ready, decay_tanh, proj_ready, copied, gate_ready, gate_done, decay_expd, w_ready, oT_ready,
         bonus_ready, bonus_sum_ready, vj_ready, kv_ready, slot_ready, scanned, read_ready, summed,
         o_bonus, o_ready, mean_ready, mean_scaled, o_stored, sq_ready, var_stored) = (sem[n] for n in names)
        block = ctx.enter_context(nc.Block())

        def bodies(eng, body):
            body(0, 0, True, True)
            body(1, 1, True, True)
            with eng.Fori(1, RUNS // 2 - 1) as i:
                body(2 * i, 0, True, True)
                body(2 * i + 1, 1, True, True)
            body(RUNS - 2, 0, True, False)
            body(RUNS - 1, 1, False, False)

        @block.gpsimd
        def _(pool):
            with pool.Fori(0, RUNS) as s:
                for m in range(NMIX):
                    pool.wait_ge(mixed_ready, s * NMIX + m + 1)
                    if m >= 2:
                        pool.wait_ge(proj_ready, s * NMIX + m - 1)
                    nc.gpsimd.tensor_tensor(
                        xm[:, m % 2, :, :].rearrange("p h (b t) -> p (h b) t", t=S),
                        mixed[:, m % 2, :, :].rearrange("p h (b t) -> p (h b) t", t=S),
                        xa[:, :, :, 1:S + 1].rearrange("p h b t -> p (h b) t"), ALU.add).then_inc(xm_ready, 1)

        @block.tensor
        def _(pe):
            def transpose(s):
                pe.wait_ge(xn_ready, s + 1)
                if later(s):
                    pe.wait_ge(decay_expd, s)
                for half in range(HALVES):
                    for c in range(CH):
                        a = half * RT + c * P
                        last = nc.tensor.transpose(tr[:, a:a + P], xn[:, c, half * P:(half + 1) * P], core.ident[:, :])
                last.then_inc(xnT_ready, 1)

            def mixer(s):
                pe.wait_ge(xin_ready, s + 1)
                if later(s - 2):
                    pe.wait_ge(o_stored, s - 2)
                for kb in range(HALVES):
                    nc.tensor.matmul(small[:, 0:RT], w["maa_w1"][:, kb, 0:P], xin[:, kb, :],
                                     start=(kb == 0), stop=(kb == HALVES - 1))
                for kb in range(HALVES):
                    last = nc.tensor.matmul(small[0:DM, RT:2 * RT], w["maa_w1"][:, kb, P:P + DM], xin[:, kb, :],
                                            start=(kb == 0), stop=(kb == HALVES - 1))
                last.then_inc(mixer_ready, 1)

            def mix(s, m):
                if m == 0:
                    pe.wait_ge(mixer_tanh, s + 1)
                if later(s) or m >= 2:
                    pe.wait_ge(mixed_ready, s * NMIX + m - 1)
                f = MIX[m]
                rows = slice(f * DM, (f + 1) * DM) if f < 4 else slice(0, DM)
                w2, x = (core.maa_w2a, mixer_a) if f < 4 else (core.maa_w2b, mixer_b)
                for half in range(HALVES):
                    last = nc.tensor.matmul(mix_banks[m % 2][:, half * RT:(half + 1) * RT],
                                            w2[rows, half * P:(half + 1) * P], x[rows, :], start=True, stop=True)
                last.then_inc(mix_ready, 1)

            def project(s, m):
                pe.wait_ge(xm_ready, s * NMIX + m + 1)
                if m == NW:
                    pe.wait_ge(xa_ready, s + 1)
                    if later(s):
                        pe.wait_ge(o_bonus, s)
                    for kb in range(HALVES):
                        last = nc.tensor.matmul(tr[0:DD, 0:RT], w["td_w1"][:, kb, :], xm[:, m % 2, kb, :],
                                                start=(kb == 0), stop=(kb == HALVES - 1))
                    last.then_inc(proj_ready, 1)
                    return
                name = {NK: "WkT", NR: "WrT", NV: "WvT", NG: "WgT"}[m]
                bank = proj_banks[m % 2]
                if later(s) and m == NK:
                    pe.wait_ge(copied, s * 3)
                if later(s) and m == NR:
                    pe.wait_ge(gate_done, s)
                if m >= 3:
                    pe.wait_ge(copied, s * 3 + m - 2)
                for half in range(HALVES):
                    for kb in range(HALVES):
                        last = nc.tensor.matmul(bank[:, half * RT:(half + 1) * RT], w[name][:, kb, half * P:(half + 1) * P],
                                                xm[:, m % 2, kb, :], start=(kb == 0), stop=(kb == HALVES - 1))
                last.then_inc(proj_ready, 1)

            def decay(s):
                pe.wait_ge(decay_tanh, s + 1)
                for half in range(HALVES):
                    last = nc.tensor.matmul(tr[:, half * RT:(half + 1) * RT],
                                            core.td_w2[:, half * P:(half + 1) * P], decay_in[:, :], start=True, stop=True)
                last.then_inc(decay_ready, 1)

            def bonus_sums(s, more):
                pe.wait_ge(bonus_ready, s + 1)
                if more:
                    pe.wait_ge(xa_ready, s + 2)
                else:
                    pe.wait_ge(decay_expd, s + 1)
                for half in range(HALVES):
                    last = nc.tensor.matmul(tr[:, 0:RT], core.head_sum[:, half, :], bonus[:, half, :],
                                            start=(half == 0), stop=(half == HALVES - 1))
                last.then_inc(bonus_sum_ready, 1)

            def transpose_out(s, tanhs):
                pe.wait_ge(o_ready, s + 1)
                pe.wait_ge(mixer_tanh, tanhs)
                for c in range(CH):
                    for jq in range(HALVES):
                        a = c * C + jq * P
                        last = nc.tensor.transpose(small[:, a:a + P], o[:, jq * RT + c * P:jq * RT + (c + 1) * P],
                                                   core.ident[:, :])
                last.then_inc(oT_ready, 1)

            def spread(s, u, n):
                half, j0 = group(n)
                if n == 0:
                    pe.wait_ge(copied, s * 3 + 3)
                if later(s) or n:
                    pe.wait_ge(kv_ready, s * GROUPS_R + n)
                for jj in range(JG):
                    jq, jl = divmod(j0 + jj, JQ)
                    last = nc.tensor.matmul(v_bank[:, jj * RT:(jj + 1) * RT], core.spread[:, half * JQ + jl, :],
                                            vT[:, u, jq, :], start=True, stop=True)
                last.then_inc(vj_ready, 1)

            def sum_heads(s, q):
                half, jq = q % HALVES, q // HALVES
                pe.wait_ge(read_ready, s * GROUPS_R + (q + 1) * JQ // JG)
                if q == 0 and later(s):
                    pe.wait_ge(o_ready, s)
                for jl in range(JQ):
                    rows = slice(jl * RH, (jl + 1) * RH)
                    states = st[:, q * JQ // JG + jl // JG, jl % JG, :, :].rearrange("p b t -> p (b t)")
                    last = nc.tensor.matmul(o_bank[rows, jq * RT:(jq + 1) * RT], core.head_sum[:, half, 0:RH], states,
                                            start=(half == 0), stop=(half == HALVES - 1))
                last.then_inc(summed, 1)

            def body(s, u, more, more2):
                for n in range(GROUPS_R):
                    spread(s, u, n)
                    if n == 0:
                        project(s, NG)
                    if n == 1:
                        bonus_sums(s, more)
                        if more:
                            mixer(s + 1)
                    if n == 3 and later(s):
                        transpose_out(s - 1, s + 2 if more else s + 1)
                    if n in (2, 3) and more:
                        mix(s + 1, n - 2)
                    if n in (2, 4, 6):
                        sum_heads(s, n // 2 - 1)
                    if n in (4, 5, 6) and more:
                        mix(s + 1, n - 2)
                    if n >= 4 and more:
                        project(s + 1, n - 4)
                    if n == 6 and more:
                        decay(s + 1)
                    if n == 7 and more2:
                        transpose(s + 2)
                sum_heads(s, SUMS - 1)

            transpose(0)
            mixer(0)
            for m in range(NMIX):
                mix(0, m)
                if m:
                    project(0, m - 1)
                if m == NMIX - 1:
                    decay(0)
            transpose(1)
            bodies(pe, body)
            transpose_out(RUNS - 1, RUNS)

        @block.scalar
        def _(act):
            def copy_in(s):
                act.wait_ge(xnT_ready, s + 1)
                if later(s):
                    act.wait_ge(xm_ready, s * NMIX)
                for half in range(HALVES):
                    last = nc.scalar.activation(xa[:, half, :, 1:S + 1],
                                                tr[:, half * RT:(half + 1) * RT].rearrange("p (b t) -> p b t", t=S),
                                                ACT.Identity, scale=col(core, "r_ln1_w", half),
                                                bias=col(core, "r_ln1_b", half))
                last.then_inc(xa_ready, 1)

            def mixer(s):
                act.wait_ge(mixer_ready, s + 1)
                nc.scalar.activation(mixer_a[:, :], small[:, 0:RT], ACT.Tanh)
                nc.scalar.activation(mixer_b[:, :], small[0:DM, RT:2 * RT], ACT.Tanh).then_inc(mixer_tanh, 1)

            def copy(s, u, m):
                act.wait_ge(proj_ready, s * NMIX + m + 1)
                bank = proj_banks[m % 2]
                if m == NW:
                    nc.scalar.activation(decay_in[:, :], tr[0:DD, 0:RT], ACT.Tanh).then_inc(decay_tanh, 1)
                elif m == NG:
                    nc.scalar.activation(gate_tanh[:, :], bank, ACT.Tanh, scale=0.5).then_inc(gate_ready, 1)
                elif m == NK:
                    nc.scalar.activation(kT[:, u, :, :, :].rearrange("p h b t -> p (h b t)"), bank,
                                         ACT.Copy).then_inc(copied, 1)
                else:
                    dst = rT if m == NR else vT
                    nc.scalar.activation(dst[:, u, :, :].rearrange("p h t -> p (h t)"), bank, ACT.Copy).then_inc(copied, 1)

            def decay(s, u):
                act.wait_ge(decay_ready, s + 1)
                for half in range(HALVES):
                    last = nc.scalar.activation(decay_exp[:, half * RB:(half + 1) * RB, :].rearrange("p b t -> p (b t)"),
                                                tr[:, half * RT:(half + 1) * RT], ACT.Exp,
                                                bias=col(core, "time_decay", half))
                last.then_inc(decay_expd, 1)
                act.wait_ge(decay_expd, s + 1)
                nc.scalar.activation(wT[:, u, :, 1:S], decay_exp[:, :, 0:S - 1], ACT.Exp, scale=-1.0).then_inc(w_ready, 1)

            def square(s):
                act.wait_ge(o_stored, s + 1)
                if later(s):
                    act.wait_ge(var_stored, s)
                nc.scalar.activation(o_sq[:, :], core.o[:, ds(s, CH * C)], ACT.Square).then_inc(sq_ready, 1)

            def projections(s, u, squares):
                copy(s, u, NW)
                if later(squares):
                    square(squares - 1)
                copy(s, u, NK)
                copy(s, u, NR)
                decay(s, u)
                copy(s, u, NV)

            def body(s, u, more, more2):
                copy(s, u, NG)
                if more:
                    mixer(s + 1)
                if more:
                    projections(s + 1, 1 - u, s)
                elif later(s):
                    square(s - 1)
                if more2:
                    copy_in(s + 2)

            copy_in(0)
            mixer(0)
            projections(0, 0, 0)
            copy_in(1)
            bodies(act, body)
            square(RUNS - 1)

        @block.vector
        def _(dve):
            def normalise(s):
                if later(s):
                    dve.wait_ge(xnT_ready, s)
                for c in range(CH):
                    t = s * CH + c
                    last = nc.vector.tensor_scalar(xn[:, c, :], core.x[:, ds(t, C)], core.rstd[:, ds(t, 1)],
                                                   core.neg_mean[:, ds(t, 1)], ALU.mult, ALU.add)
                last.then_inc(xn_ready, 1)

            def shift(s):
                if later(s):
                    dve.wait_ge(xm_ready, s * NMIX)
                nc.vector.tensor_copy(xa[:, :, :, 0], core.state_rows[:, 1, :, ds(s, RB)]).then_inc(first_slot, 1)
                dve.wait_ge(xa_ready, s + 1)
                dve.wait_ge(first_slot, s + 1)
                nc.vector.tensor_tensor(sx[:, :, :, :].rearrange("p h b t -> p (h b) t"),
                                        xa[:, :, :, 0:S].rearrange("p h b t -> p (h b) t"),
                                        xa[:, :, :, 1:S + 1].rearrange("p h b t -> p (h b) t"),
                                        ALU.subtract).then_inc(sx_ready, 1)
                dve.wait_ge(sx_ready, s + 1)
                if later(s):
                    dve.wait_ge(mixer_ready, s)
                for half in range(HALVES):
                    last = nc.vector.scalar_tensor_tensor(
                        out=xin[:, half, :].rearrange("p (b t) -> p b t", t=S), in0=sx[:, half, :, :],
                        scalar=col(core, "maa_x", half), in1=xa[:, half, :, 1:S + 1], op0=ALU.mult, op1=ALU.add)
                last.then_inc(xin_ready, 1)

            def mix(s, m):
                dve.wait_ge(mix_ready, s * NMIX + m + 1)
                if later(s) or m >= 2:
                    dve.wait_ge(xm_ready, s * NMIX + m - 1)
                for half in range(HALVES):
                    last = nc.vector.scalar_tensor_tensor(
                        out=mixed[:, m % 2, half, :], in0=mix_banks[m % 2][:, half * RT:(half + 1) * RT],
                        scalar=col(core, "maa_stack", MIX[m] * HALVES + half),
                        in1=sx[:, half, :, :].rearrange("p b t -> p (b t)"), op0=ALU.add, op1=ALU.mult)
                last.then_inc(mixed_ready, 1)

            def gate(s):
                dve.wait_ge(gate_ready, s + 1)
                nc.vector.scalar_tensor_tensor(out=core.gate[:, ds(s, HALVES * RT)], in0=gate_tanh[:, :], scalar=1.0,
                                               in1=proj_banks[NG % 2], op0=ALU.add, op1=ALU.mult).then_inc(gate_done, 1)

            def make_bonus(s, u):
                dve.wait_ge(copied, s * 3 + 2)
                if later(s):
                    dve.wait_ge(bonus_sum_ready, s)
                for half in range(HALVES):
                    last = nc.vector.scalar_tensor_tensor(
                        out=bonus[:, half, :], in0=rT[:, u, half, :], scalar=col(core, "u", half),
                        in1=kT[:, u, half, :, :].rearrange("p b t -> p (b t)"), op0=ALU.mult, op1=ALU.mult)
                last.then_inc(bonus_ready, 1)

            def recur(s, u, n):
                half, j0 = group(n)
                g = s * GROUPS_R + n
                dve.wait_ge(vj_ready, g + 1)
                if later(s):
                    dve.wait_ge(summed, s * SUMS + n * JG // JQ + 1 - SUMS)
                if n == 0:
                    dve.wait_ge(copied, s * 3 + 3)
                    dve.wait_ge(w_ready, s + 1)
                nc.vector.tensor_copy(st[:, n, :, :, 0], core.state0[:, half * RS + j0:half * RS + j0 + JG, ds(s, RB)])
                nc.vector.tensor_tensor(
                    st[:, n, :, :, 1:S], v_bank.rearrange("p (j b t) -> p j b t", j=JG, t=S)[:, :, :, 0:S - 1],
                    kT[:, u, half, :, 0:S - 1].unsqueeze(1).to_broadcast([P, JG, RB, S - 1]),
                    ALU.mult).then_inc(kv_ready, 1)
                dve.wait_ge(kv_ready, g + 1)
                for jj in range(JG):
                    states = st[:, n, jj, :, :].rearrange("p b t -> p (b t)")
                    last = nc.vector.tensor_tensor_scan(
                        states, wT[:, u, half * RB:(half + 1) * RB, :].rearrange("p b t -> p (b t)"), states, 0.0,
                        ALU.mult, ALU.add)
                last.then_inc(scanned, 1)
                dve.wait_ge(scanned, g + 1)
                states = st[:, n, :, :, :].rearrange("p j b t -> p j (b t)")
                nc.vector.tensor_tensor(states, states, rT[:, u, half, :].unsqueeze(1).to_broadcast([P, JG, RT]),
                                        ALU.mult).then_inc(read_ready, 1)

            def add_bonus(s, u):
                dve.wait_ge(bonus_sum_ready, s + 1)
                nc.vector.tensor_tensor(bonus_v[:, :, :], vT[:, u, :, :],
                                        tr[:, 0:RT].unsqueeze(1).to_broadcast([P, HALVES, RT]),
                                        ALU.mult).then_inc(o_bonus, 1)

            def add_up(s):
                dve.wait_ge(o_bonus, s + 1)
                dve.wait_ge(summed, s * SUMS + SUMS)
                if later(s):
                    dve.wait_ge(oT_ready, s)
                nc.vector.tensor_tensor(o[:, :], o_bank, bonus_v[:, :, :].rearrange("p h t -> p (h t)"),
                                        ALU.add).then_inc(o_ready, 1)

            def centre(s):
                dve.wait_ge(oT_ready, s + 1)
                nc.vector.tensor_reduce(out=mean[:, :].rearrange("p (c h) -> p c h", c=CH),
                                        in_=small.rearrange("p (c j h) -> p c h j", c=CH, j=RS),
                                        op=ALU.add, axis=AX.X).then_inc(mean_ready, 1)
                dve.wait_ge(mean_ready, s + 1)
                nc.vector.tensor_scalar(mean[:, :], mean[:, :], 1.0 / RS, None, ALU.mult).then_inc(mean_scaled, 1)
                dve.wait_ge(mean_scaled, s + 1)
                nc.vector.tensor_tensor(
                    core.o[:, ds(s, CH * C)].rearrange("p (c j h) -> p c j h", c=CH, j=RS),
                    small.rearrange("p (c j h) -> p c j h", c=CH, j=RS),
                    mean[:, :].rearrange("p (c h) -> p c h", c=CH).unsqueeze(2).to_broadcast([P, CH, RS, RH]),
                    ALU.subtract).then_inc(o_stored, 1)

            def sum_squares(s):
                dve.wait_ge(sq_ready, s + 1)
                nc.vector.tensor_reduce(out=core.var[:, ds(s, CH * RH)].rearrange("p (c h) -> p c h", c=CH),
                                        in_=o_sq[:, :].rearrange("p (c j h) -> p c h j", c=CH, j=RS),
                                        op=ALU.add, axis=AX.X).then_inc(var_stored, 1)

            def body(s, u, more, more2):
                if later(s):
                    add_up(s - 1)
                for n in range(GROUPS_R):
                    recur(s, u, n)
                    if n == 0 and more:
                        shift(s + 1)
                    if n == 2:
                        add_bonus(s, u)
                    if n in (2, 3, 4, 5, 6) and more:
                        mix(s + 1, n - 2)
                    if n == 1:
                        gate(s)
                    if n == 3 and later(s):
                        centre(s - 1)
                    if n == 6 and later(s):
                        sum_squares(s - 1)
                    if n == 5 and more2:
                        normalise(s + 2)
                if more:
                    make_bonus(s + 1, 1 - u)

            nc.vector.memset(wT[:, :, :, 0], 0.0)
            normalise(0)
            shift(0)
            for m in range(NMIX):
                mix(0, m)
            make_bonus(0, 0)
            normalise(1)
            bodies(dve, body)
            add_up(RUNS - 1)
            centre(RUNS - 1)
            sum_squares(RUNS - 1)


def run_pairs(eng, body):
    body(0, 0)
    body(1, 1)
    with eng.Fori(1, RUNS // 2 - 2) as i:
        body(2 * i, 0)
        body(2 * i + 1, 1)
    for s in range(RUNS - 4, RUNS):
        body(s, s % 2)


def run_there(s):
    return not isinstance(s, int) or s < RUNS


def gate_phase(core):
    nc = core.nc
    with ExitStack() as ctx:
        def sb(name, shape):
            return ctx.enter_context(nc.sbuf_tensor(f"gate_{name}", shape, FP32))

        rstd = sb("rstd", [P, TILES * RH])
        on = sb("on", [P, 2, CH * C])
        onT = sb("onT", [P, 2, HALVES * RT])
        yT = sb("yT", [P, 2, HALVES * RT])
        tr, proj = core.banks[0:2], core.banks[2:4]
        (std_ready, rstd_ready, on_ready, onT_ready, onT_copied, y_ready, proj_ready, x_ready) = semaphores(
            nc, ctx, *(f"gate_{s}" for s in ("std_ready", "rstd_ready", "on_ready", "onT_ready", "onT_copied",
                                             "y_ready", "proj_ready", "x_ready")))
        block = ctx.enter_context(nc.Block())

        @block.tensor
        def _(pe):
            def transpose(s, u):
                pe.wait_ge(on_ready, s + 1)
                if later(s - 1):
                    pe.wait_ge(onT_copied, s - 1)
                for half in range(HALVES):
                    for c in range(CH):
                        a = half * RT + c * P
                        last = nc.tensor.transpose(tr[u][:, a:a + P], on[:, u, c * C + half * P:c * C + (half + 1) * P],
                                                   core.ident[:, :])
                last.then_inc(onT_ready, 1)

            def project(s, u):
                pe.wait_ge(y_ready, s + 1)
                if later(s - 1):
                    pe.wait_ge(x_ready, s - 1)
                for c in range(CH):
                    for kb in range(HALVES):
                        a = kb * RT + c * P
                        last = nc.tensor.matmul(proj[u][:, c * C:(c + 1) * C], yT[:, u, a:a + P], core.w["WoT"][:, kb, :],
                                                start=(kb == 0), stop=(kb == HALVES - 1))
                last.then_inc(proj_ready, 1)

            def body(s, u):
                if run_there(s + 2):
                    transpose(s + 2, u)
                project(s, u)

            transpose(0, 0)
            transpose(1, 1)
            run_pairs(pe, body)

        @block.scalar
        def _(act):
            def copy(s, u):
                act.wait_ge(onT_ready, s + 1)
                if later(s - 1):
                    act.wait_ge(y_ready, s - 1)
                for half in range(HALVES):
                    last = nc.scalar.activation(onT[:, u, half * RT:(half + 1) * RT],
                                                tr[u][:, half * RT:(half + 1) * RT],
                                                ACT.Identity, scale=col(core, "gn_w", half), bias=col(core, "gn_b", half))
                last.then_inc(onT_copied, 1)

            nc.scalar.activation(rstd[:, :], core.var[:, :], ACT.Sqrt, scale=1.0 / RS,
                                 bias=core.eps[:, :]).then_inc(std_ready, 1)
            run_pairs(act, copy)

        @block.vector
        def _(dve):
            def scale(s, u):
                if later(s - 1):
                    dve.wait_ge(onT_ready, s - 1)
                heads = rstd[:, ds(s, CH * RH)].rearrange("p (c h) -> p c h", c=CH)
                nc.vector.tensor_tensor(on[:, u, :].rearrange("p (c j h) -> p c j h", c=CH, j=RS),
                                        core.o[:, ds(s, CH * C)].rearrange("p (c j h) -> p c j h", c=CH, j=RS),
                                        heads.unsqueeze(2).to_broadcast([P, CH, RS, RH]), ALU.mult).then_inc(on_ready, 1)

            def gate(s, u):
                dve.wait_ge(onT_copied, s + 1)
                if later(s - 1):
                    dve.wait_ge(proj_ready, s - 1)
                nc.vector.scalar_tensor_tensor(out=yT[:, u, :], in0=onT[:, u, :], scalar=0.5,
                                               in1=core.gate[:, ds(s, HALVES * RT)], op0=ALU.mult,
                                               op1=ALU.mult).then_inc(y_ready, 1)

            def add_residual(s, u):
                dve.wait_ge(proj_ready, s + 1)
                xs = core.x[:, ds(s, CH * C)]
                nc.vector.tensor_tensor(xs, proj[u], xs, ALU.add).then_inc(x_ready, 1)

            def make_stats(s):
                dve.wait_ge(x_ready, s + 1)
                for c in range(CH):
                    t = s * CH + c
                    nc.vector.bn_stats(core.stats[:, ds(t, 6)], core.x[:, ds(t, C)])

            def body(s, u):
                if later(s):
                    add_residual(s - 1, 1 - u)
                if run_there(s + 1):
                    gate(s + 1, 1 - u)
                if run_there(s + 3):
                    scale(s + 3, 1 - u)
                if later(s):
                    make_stats(s - 1)

            dve.wait_ge(std_ready, 1)
            nc.vector.reciprocal(rstd[:, :], rstd[:, :]).then_inc(rstd_ready, 1)
            dve.wait_ge(rstd_ready, 1)
            scale(0, 0)
            scale(1, 1)
            scale(2, 0)
            gate(0, 0)
            run_pairs(dve, body)
            add_residual(RUNS - 1, 1)
            make_stats(RUNS - 1)


def channel_phase(core, out):
    nc = core.nc
    w = core.w
    with ExitStack() as ctx:
        def sb(name, shape):
            return ctx.enter_context(nc.sbuf_tensor(f"ch_{name}", shape, FP32))

        xn = sb("xn", [P, 2, CH, C])
        xc = sb("xc", [P, 2, HALVES, RB, S + 1])
        sx = sb("sx", [P, HALVES, RB, S])
        xk, xr = sb("xk", [P, 2, HALVES, RT]), sb("xr", [P, 2, HALVES, RT])
        relu = sb("relu", [P, 2, HALVES * RT])
        kk = sb("kk", [P, 2, HALVES * RT])
        rr = sb("rr", [P, 2, CH * C])
        tr, key, recept, value = (core.banks[2 * i:2 * i + 2] for i in range(4))
        names = ("xn_ready xnT_ready xc_ready first_slot sx_ready mixed_ready key_ready relu_ready kk_ready recept_ready "
                 "rr_ready value_ready rv_ready out_ready stored").split()
        (xn_ready, xnT_ready, xc_ready, first_slot, sx_ready, mixed_ready, key_ready, relu_ready, kk_ready, recept_ready,
         rr_ready, value_ready, rv_ready, out_ready, stored) = semaphores(nc, ctx, *(f"ch_{n}" for n in names))
        block = ctx.enter_context(nc.Block())

        @block.sync
        def _(sp):
            with sp.Fori(0, RUNS) as s:
                sp.wait_ge(out_ready, s + 1)
                sp.dma_start(out[:, ds(s, CH * C)], core.x[:, ds(s, CH * C)]).then_inc(stored, 16)
            sp.wait_ge(stored, 16 * RUNS)

        @block.gpsimd
        def _(pool):
            def square(s, u):
                pool.wait_ge(relu_ready, s + 1)
                if later(s):
                    pool.wait_ge(kk_ready, s)
                if later(s - 1):
                    pool.wait_ge(value_ready, s - 1)
                nc.gpsimd.tensor_tensor(kk[:, u, :], relu[:, u, :], relu[:, u, :], ALU.mult).then_inc(kk_ready, 1)

            run_pairs(pool, square)

        @block.tensor
        def _(pe):
            def transpose(s, u):
                pe.wait_ge(xn_ready, s + 1)
                if later(s - 1):
                    pe.wait_ge(xc_ready, s - 1)
                for half in range(HALVES):
                    for c in range(CH):
                        a = half * RT + c * P
                        last = nc.tensor.transpose(tr[u][:, a:a + P], xn[:, u, c, half * P:(half + 1) * P],
                                                   core.ident[:, :])
                last.then_inc(xnT_ready, 1)

            def keys(s, u):
                pe.wait_ge(mixed_ready, s + 1)
                if later(s - 1):
                    pe.wait_ge(relu_ready, s - 1)
                for half in range(HALVES):
                    for kb in range(HALVES):
                        last = nc.tensor.matmul(key[u][:, half * RT:(half + 1) * RT],
                                                w["WfkT"][:, kb, half * P:(half + 1) * P], xk[:, u, kb, :],
                                                start=(kb == 0), stop=(kb == HALVES - 1))
                last.then_inc(key_ready, 1)

            def receptances(s, u):
                if later(s - 1):
                    pe.wait_ge(rr_ready, s - 1)
                for c in range(CH):
                    for kb in range(HALVES):
                        last = nc.tensor.matmul(recept[u][:, c * C:(c + 1) * C], xr[:, u, kb, c * P:(c + 1) * P],
                                                w["WfrT"][:, kb, :], start=(kb == 0), stop=(kb == HALVES - 1))
                last.then_inc(recept_ready, 1)

            def values(s, u):
                pe.wait_ge(kk_ready, s + 1)
                if later(s - 1):
                    pe.wait_ge(rv_ready, s - 1)
                for c in range(CH):
                    for kb in range(HALVES):
                        a = kb * RT + c * P
                        last = nc.tensor.matmul(value[u][:, c * C:(c + 1) * C], kk[:, u, a:a + P],
                                                w["WfvT"][:, kb, :], start=(kb == 0), stop=(kb == HALVES - 1))
                last.then_inc(value_ready, 1)

            def body(s, u):
                if run_there(s + 2):
                    transpose(s + 2, u)
                if run_there(s + 1):
                    keys(s + 1, 1 - u)
                values(s, u)
                if run_there(s + 1):
                    receptances(s + 1, 1 - u)

            transpose(0, 0)
            transpose(1, 1)
            keys(0, 0)
            receptances(0, 0)
            run_pairs(pe, body)

        @block.scalar
        def _(act):
            def copy_in(s, u):
                act.wait_ge(xnT_ready, s + 1)
                if later(s - 1):
                    act.wait_ge(mixed_ready, s - 1)
                for half in range(HALVES):
                    last = nc.scalar.activation(xc[:, u, half, :, 1:S + 1],
                                                tr[u][:, half * RT:(half + 1) * RT].rearrange("p (b t) -> p b t", t=S),
                                                ACT.Identity, scale=col(core, "r_ln2_w", half),
                                                bias=col(core, "r_ln2_b", half))
                last.then_inc(xc_ready, 1)

            def nonlinear(s, u):
                act.wait_ge(key_ready, s + 1)
                if later(s - 1):
                    act.wait_ge(kk_ready, s - 1)
                nc.scalar.activation(relu[:, u, :], key[u], ACT.Relu).then_inc(relu_ready, 1)
                act.wait_ge(recept_ready, s + 1)
                if later(s - 1):
                    act.wait_ge(out_ready, s - 1)
                nc.scalar.activation(rr[:, u, :], recept[u], ACT.Sigmoid).then_inc(rr_ready, 1)

            def body(s, u):
                if run_there(s + 2):
                    copy_in(s + 2, u)
                if run_there(s + 1):
                    nonlinear(s + 1, 1 - u)

            copy_in(0, 0)
            copy_in(1, 1)
            nonlinear(0, 0)
            run_pairs(act, body)

        @block.vector
        def _(dve):
            def normalise(s, u):
                if later(s - 1):
                    dve.wait_ge(xnT_ready, s - 1)
                for c in range(CH):
                    t = s * CH + c
                    last = nc.vector.tensor_scalar(xn[:, u, c, :], core.x[:, ds(t, C)], core.rstd[:, ds(t, 1)],
                                                   core.neg_mean[:, ds(t, 1)], ALU.mult, ALU.add)
                last.then_inc(xn_ready, 1)

            def shift(s, u):
                nc.vector.tensor_copy(xc[:, u, :, :, 0], core.state_rows[:, 0, :, ds(s, RB)]).then_inc(first_slot, 1)
                dve.wait_ge(xc_ready, s + 1)
                dve.wait_ge(first_slot, s + 1)
                nc.vector.tensor_tensor(sx[:, :, :, :].rearrange("p h b t -> p (h b) t"),
                                        xc[:, u, :, :, 0:S].rearrange("p h b t -> p (h b) t"),
                                        xc[:, u, :, :, 1:S + 1].rearrange("p h b t -> p (h b) t"),
                                        ALU.subtract).then_inc(sx_ready, 1)
                dve.wait_ge(sx_ready, s + 1)
                if later(s - 1):
                    dve.wait_ge(key_ready, s - 1)
                    dve.wait_ge(recept_ready, s - 1)
                for half in range(HALVES):
                    for dst, name in ((xk, "ffn_maa_k"), (xr, "ffn_maa_r")):
                        last = nc.vector.scalar_tensor_tensor(
                            out=dst[:, u, half, :].rearrange("p (b t) -> p b t", t=S), in0=sx[:, half, :, :],
                            scalar=col(core, name, half), in1=xc[:, u, half, :, 1:S + 1], op0=ALU.mult, op1=ALU.add)
                last.then_inc(mixed_ready, 1)

            def finish(s, u):
                dve.wait_ge(value_ready, s + 1)
                dve.wait_ge(rr_ready, s + 1)
                nc.vector.tensor_tensor(rr[:, u, :], value[u], rr[:, u, :], ALU.mult).then_inc(rv_ready, 1)
                dve.wait_ge(rv_ready, s + 1)
                xs = core.x[:, ds(s, CH * C)]
                nc.vector.tensor_tensor(xs, rr[:, u, :], xs, ALU.add).then_inc(out_ready, 1)

            def body(s, u):
                if later(s):
                    finish(s - 1, 1 - u)
                if run_there(s + 2):
                    shift(s + 2, u)
                if run_there(s + 3):
                    normalise(s + 3, 1 - u)

            normalise(0, 0)
            normalise(1, 1)
            shift(0, 0)
            normalise(2, 0)
            shift(1, 1)
            run_pairs(dve, body)
            finish(RUNS - 1, 1)


FIRST_WEIGHTS = {"w_qkv": (2, 3 * C), "w_ao": (2, C), "w_q": (2, C), "w_kv": (2, 2 * C), "w_co": (2, C),
                 "w1": (2, F1), "w2": (8, C)}
SECOND_WEIGHTS = {"maa_w1": (2, NMIX * DM), "td_w1": (2, DD), "WrT": (2, C), "WkT": (2, C), "WvT": (2, C),
                  "WgT": (2, C), "WoT": (2, C), "WfkT": (2, C), "WfrT": (2, C), "WfvT": (2, C)}


def build(nc, dram, out):
    core = Core()
    core.nc, core.dram = nc, dram
    with ExitStack() as ctx:
        def sb(name, shape, scope=ctx):
            return scope.enter_context(nc.sbuf_tensor(name, shape, FP32))

        def weights(table, scope):
            for k, (kb, n) in table.items():
                core.weights[k] = sb(k, [P, kb * n], scope)
                core.w[k] = core.weights[k][:, :].rearrange("p (k n) -> p k n", k=kb)

        core.weights, core.w = {}, {}
        core.x = sb("x", [P, TILES * C])
        core.cols = sb("cols", [P, NCOLS])
        core.ident = sb("ident", [P, P])
        core.stats = sb("stats", [P, TILES * 6])
        core.norm_tmp = sb("norm_tmp", [P, 3, TILES])
        core.neg_mean = sb("neg_mean", [P, TILES])
        core.rstd = sb("rstd", [P, TILES])
        core.eps = sb("eps", [P, 1])
        core.psum = ctx.enter_context(nc.psum_tensor("psum", [P, 8 * 512], FP32))
        core.banks = [core.psum[:, i * 512:(i + 1) * 512] for i in range(8)]

        with ExitStack() as first:
            core.rows = sb("rows", [P, 3, C], first)
            core.parity = sb("parity", [P, 2], first)
            core.q_bias = sb("q_bias", [P, 2, HALVES], first)
            core.k_heads = sb("k_heads", [P, HALVES * BPT, PAIRS, S], first)
            core.self_mask = sb("self_mask", [P, S], first)
            core.self_bias = sb("self_bias", [P, S], first)
            core.cross_mask = sb("cross_mask", [P, TILES * S], first)
            core.cross_bias = sb("cross_bias", [P, TILES * S], first)
            core.vpad = sb("vpad", [P, PAIRS, P], first)
            weights(FIRST_WEIGHTS, first)
            load_phase(core, dram)
            norm_phase(core, "norm1")
            attention_phase(core, False)
            norm_phase(core, "norm2")
            attention_phase(core, True)
            norm_phase(core, "norm3")
            gelu_phase(core)

        core.head_sum = sb("head_sum", [P, HALVES, P])
        core.spread = sb("spread", [P, RS, P])
        core.maa_w2a, core.maa_w2b = sb("maa_w2a", [P, C]), sb("maa_w2b", [DM, C])
        core.td_w2 = sb("td_w2", [DD, C])
        core.state_rows = sb("state_rows", [P, 2, HALVES, B])
        core.state0 = sb("state0", [P, HALVES * RS, B])
        core.o = sb("o", [P, TILES * C])
        core.gate = sb("gate", [P, TILES * C])
        core.var = sb("var", [P, TILES * RH])
        weights(SECOND_WEIGHTS, ctx)
        load_second_phase(core, dram)
        norm_phase(core, "norm4")
        recurrence_phase(core)
        gate_phase(core)
        norm_phase(core, "norm5")
        channel_phase(core, out)


def lay_out(inputs):
    a = {k: np.asarray(v) for k, v in inputs.items()}
    L0, L1 = "L0_xattn_", "L1_xattn_"

    def per_channel(v):
        return v.reshape(-1, P).T

    def by_value_column(v):
        return v.reshape(RH, RS, -1).swapaxes(0, 1).reshape(v.shape)

    def rows(w):
        return np.ascontiguousarray(w.reshape(-1, P, w.shape[1]).transpose(1, 0, 2).reshape(P, -1))

    b_qkv, b_kv = a[L0 + "b_qkv"], a[L0 + "b_kv"]
    vectors = {"ln1_s": a[L0 + "ln1_s"], "ln1_b": a[L0 + "ln1_b"], "b_q_self": b_qkv[:C], "b_k_self": b_qkv[C:2 * C],
               "b_v_self": b_qkv[2 * C:], "ln2_s": a[L0 + "ln2_s"], "ln2_b": a[L0 + "ln2_b"],
               "b_q_cross": a[L0 + "b_q"], "b_k_cross": b_kv[:C], "b_v_cross": b_kv[C:], "ln3_s": a[L0 + "ln3_s"],
               "ln3_b": a[L0 + "ln3_b"], "b1": a[L0 + "b1"], "r_ln1_w": a[L1 + "ln1_w"], "r_ln1_b": a[L1 + "ln1_b"],
               "r_ln2_w": a[L1 + "ln2_w"], "r_ln2_b": a[L1 + "ln2_b"], "maa_x": a[L1 + "maa_x"],
               "maa_stack": a[L1 + "maa_stack"].reshape(-1), "time_decay": a[L1 + "time_decay"],
               "u": a[L1 + "u"].reshape(-1), "gn_w": by_value_column(a[L1 + "gn_w"]),
               "gn_b": by_value_column(a[L1 + "gn_b"]),
               "ffn_maa_k": a[L1 + "ffn_maa_k"], "ffn_maa_r": a[L1 + "ffn_maa_r"]}
    ctx = a["ctx_2048"]
    p = np.arange(P)
    out = {
        "x": rows(a["x"].reshape(B * S, C)),
        "cols": np.ascontiguousarray(np.concatenate([per_channel(vectors[k]) for k in COLS], axis=1)),
        "rows": np.ascontiguousarray(np.stack([a[L0 + "b_ao"], a[L0 + "b_co"], a[L0 + "b2"]])),
        "enc": np.ascontiguousarray(ctx.reshape(B * S, HALVES, P).transpose(2, 1, 0)),
        "cross_mask": rows(a["mask_Bx1xSxS2_ff1"].reshape(B * S, S)),
        "self_mask": np.ascontiguousarray(np.concatenate([a["mask_1x1xSxS2_fc1"].reshape(S, S)] * 2)),
        "ident": np.eye(P, dtype=np.float32),
        "parity": np.ascontiguousarray(((p[:, None] // HD) % 2 == np.arange(2)[None, :]).astype(np.float32)),
    }
    to_rows = [p[None, :] % RH == half * HPH + p[:, None] // RS for half in range(HALVES)]
    out["head_sum"] = np.ascontiguousarray(np.stack(to_rows, axis=1).astype(np.float32))
    out["spread"] = np.ascontiguousarray(np.stack(
        [(to_rows[half].T & (p[:, None] // RH == jl)).astype(np.float32) for half in range(HALVES) for jl in range(JQ)],
        axis=1))
    out["maa_w2"] = np.ascontiguousarray(a[L1 + "maa_w2"].reshape(NMIX * DM, C))
    out["td_w2"] = np.ascontiguousarray(a[L1 + "td_w2"])
    out["state_rows"] = np.ascontiguousarray(ctx[:, 0:2, :].reshape(B, 2, HALVES, P).transpose(3, 1, 2, 0))
    out["state0"] = np.ascontiguousarray(
        ctx[:, 2:2 + RS, :].reshape(B, HALVES, P, RS).transpose(2, 1, 3, 0).reshape(P, HALVES * RS, B))
    for k in FIRST_WEIGHTS:
        out[k] = rows(a[L0 + k])
    for k in SECOND_WEIGHTS:
        w = a[L1 + k[:-1]] if k[0] == "W" else a[L1 + k]
        if k in ("WvT", "WgT"):
            w = by_value_column(w)
        out[k] = rows(by_value_column(w.T) if k == "WoT" else w.T) if k[0] == "W" else rows(w)
    return out


def kernel(**inputs):
    import concourse.bacc as bacc
    from concourse.bass_utils import run_bass_kernel_spmd

    nc = bacc.Bacc("TRN2", target_bir_lowering=False, num_devices=1)
    arrays = lay_out(inputs)
    dram = {k: nc.dram_tensor(f"in_{k}", v.shape, mybir.dt.from_np(v.dtype), kind="ExternalInput").ap()
            for k, v in arrays.items()}
    out = nc.dram_tensor("out", [P, TILES * C], FP32, kind="ExternalOutput").ap()
    build(nc, dram, out)
    result = run_bass_kernel_spmd(nc, [{f"in_{k}": v for k, v in arrays.items()}], core_ids=[0]).results[0]["out"]
    return np.ascontiguousarray(result.reshape(P, TILES, C).transpose(1, 0, 2).reshape(B, S, C))
```

```python
import concourse.bass as bass
from concourse import mybir
from contextlib import ExitStack
import numpy as np

FP32 = mybir.dt.float32
ALU = mybir.AluOpType
ACT = mybir.ActivationFunctionType
AX = mybir.AxisListType

B, S, C = 64, 64, 256
P = 128
HALVES = C // P
TILES = B * S // P
BPT = P // S
NH, HD = 16, 16
PAIRS = NH // 2
HALF_PAIRS = PAIRS // HALVES
UNROLLED = 4
POOL_GROUPS, ACT_GROUPS = (0, 1, 2), (3,)
PW = 2 * HD + 2
F1 = 4 * C
EPS = 1e-5
MASKED = 10000.0
RH, RS = 32, 8
HPH = RH // HALVES
DM, DD, NMIX = 32, 64, 5

COLS = {}
for _name, _n in (("ln1_s", 2), ("ln1_b", 2), ("b_q_self", 2), ("b_k_self", 2), ("b_v_self", 2),
                  ("ln2_s", 2), ("ln2_b", 2), ("b_q_cross", 2), ("b_k_cross", 2), ("b_v_cross", 2),
                  ("ln3_s", 2), ("ln3_b", 2), ("b1", 8), ("r_ln1_w", 2), ("r_ln1_b", 2),
                  ("r_ln2_w", 2), ("r_ln2_b", 2), ("maa_x", 2), ("maa_stack", 2 * NMIX),
                  ("time_decay", 2), ("u", 2), ("gn_w", 2), ("gn_b", 2), ("ffn_maa_k", 2),
                  ("ffn_maa_r", 2)):
    COLS[_name] = (sum(n for _, n in COLS.values()), _n)
NCOLS = sum(n for _, n in COLS.values())


def ds(t, n):
    return bass.ds(t * n, n)


def later(n):
    return not isinstance(n, int) or n > 0


class Core:
    pass


def semaphores(nc, ctx, *names):
    return [ctx.enter_context(nc.semaphore(n)) for n in names]


def col(core, name, i):
    return core.cols[:, COLS[name][0] + i:COLS[name][0] + i + 1]


def load_phase(core, dram):
    nc = core.nc
    whole = {name: (core.weights[name][:, :], dram[name]) for name in (*FIRST_WEIGHTS, *SECOND_WEIGHTS)}
    bias_rows = [(core.rows[:, n, :], dram["rows"][n:n + 1, :].partition_broadcast(P)) for n in range(3)]
    loads = {
        "self": [(core.cols[:, :], dram["cols"]), (core.ident[:, :], dram["ident"]), whole["w_qkv"],
                 (core.parity[:, :], dram["parity"]), (core.self_mask[:, :], dram["self_mask"]), *bias_rows,
                 whole["w_ao"]],
        "cross": [(core.cross_mask[:, :], dram["cross_mask"]), whole["w_q"], whole["w_kv"], whole["w_co"]],
        "gelu": [whole["w1"], whole["w2"]],
        "recurrent": [(core.head_sum[:, :, :], dram["head_sum"]), (core.spread[:, :, :], dram["spread"]),
                      (core.maa_w2a[:, :], dram["maa_w2"][0:P, :]), (core.state_rows[:, :, :, :], dram["state_rows"]),
                      (core.state0[:, :, :], dram["state0"]),
                      *[(core.maa_w2b[c * DD:c * DD + DM, c, :], dram["maa_w2"][P:P + DM, :]) for c in range(CH)],
                      *[(core.td_w2[c * DD:(c + 1) * DD, c, :], dram["td_w2"]) for c in range(CH)],
                      *[whole[name] for name in SECOND_WEIGHTS]],
    }
    core.loads = loads
    core.load_counts = {phase: 16 * len(group) for phase, group in loads.items()}
    with ExitStack() as ctx:
        parts = 4
        [prepared] = semaphores(nc, ctx, "prepared")
        x_loaded = semaphores(nc, ctx, *(f"x_part{i}_loaded" for i in range(parts)))
        block = ctx.enter_context(nc.Block())
        n = TILES // parts

        @block.sync
        def _(sp):
            for i in range(parts):
                cols = slice(i * n * C, (i + 1) * n * C)
                sp.dma_start(core.x[:, cols], dram["x"][:, cols]).then_inc(x_loaded[i], 16)

        @block.scalar
        def _(act):
            for dst, src in loads["self"]:
                act.dma_start(dst, src).then_inc(core.loaded["self"], 16)

        @block.gpsimd
        def _(pool):
            nc.gpsimd.memset(core.vpad[:, :, :], 0.0).then_inc(prepared, 1)
            nc.gpsimd.memset(core.eps[:, :], EPS).then_inc(prepared, 1)
            nc.gpsimd.memset(core.k_heads[:, :, :, :], 0.0).then_inc(prepared, 1)
            nc.gpsimd.memset(core.maa_w2b[:, :, :], 0.0).then_inc(prepared, 1)
            nc.gpsimd.memset(core.td_w2[:, :, :], 0.0).then_inc(prepared, 1)
            pool.wait_ge(prepared, 5)
            for e in range(2):
                for b in range(BPT):
                    a = b * PW + 2 * HD + e
                    nc.gpsimd.memset(core.vpad[e * S:(e + 1) * S, :, a:a + 1], 1.0).then_inc(prepared, 1)
            pool.wait_ge(prepared, 9)

        @block.vector
        def _(dve):
            for i in range(parts):
                dve.wait_ge(x_loaded[i], 16)
                with dve.Fori(i * n // 4, (i + 1) * n // 4) as r:
                    for j in range(4):
                        nc.vector.bn_stats(core.stats[:, ds(4 * r + j, 6)], core.x[:, ds(4 * r + j, C)])


def load_later(core, sp):
    for phase in ("cross", "gelu", "recurrent"):
        for dst, src in core.loads[phase]:
            sp.dma_start(dst, src).then_inc(core.loaded[phase], 16)


def norm_phase(core, name, phase=None):
    nc = core.nc
    with ExitStack() as ctx:
        step, var_ready, std_ready = semaphores(nc, ctx, f"{name}_step", f"{name}_var_ready", f"{name}_std_ready")
        block = ctx.enter_context(nc.Block())
        st = core.stats[:, :].rearrange("p (t s) -> p t s", s=6)
        mean_even, m2_even, mean_odd, m2_odd = (st[:, :, i] for i in (1, 2, 4, 5))
        a, b, c = (core.norm_tmp[:, i, :] for i in range(3))

        if phase:
            @block.sync
            def _(sp):
                sp.wait_ge(core.loaded[phase], core.load_counts[phase])

        @block.vector
        def _(dve):
            nc.vector.tensor_tensor(a, m2_even, m2_odd, ALU.add)
            nc.vector.tensor_tensor(b, mean_even, mean_odd, ALU.subtract)
            nc.vector.tensor_tensor(core.neg_mean[:, :], mean_even, mean_odd, ALU.add).then_inc(step, 1)
            dve.wait_ge(step, 1)
            nc.vector.tensor_tensor(b, b, b, ALU.mult).then_inc(step, 1)
            dve.wait_ge(step, 2)
            nc.vector.tensor_scalar(b, b, 0.25, None, ALU.mult).then_inc(step, 1)
            dve.wait_ge(step, 3)
            nc.vector.scalar_tensor_tensor(out=c, in0=a, scalar=1.0 / C, in1=b, op0=ALU.mult,
                                           op1=ALU.add).then_inc(var_ready, 1)
            dve.wait_ge(std_ready, 1)
            nc.vector.reciprocal(core.rstd[:, :], a).then_inc(step, 1)
            dve.wait_ge(step, 4)
            nc.vector.scalar_tensor_tensor(out=core.neg_mean[:, :], in0=core.neg_mean[:, :], scalar=-0.5,
                                           in1=core.rstd[:, :], op0=ALU.mult, op1=ALU.mult)

        @block.scalar
        def _(act):
            act.wait_ge(var_ready, 1)
            nc.scalar.activation(a, c, ACT.Sqrt, bias=core.eps[:, :]).then_inc(std_ready, 1)


def attention_phase(core, cross):
    nc = core.nc
    kind = "cross" if cross else "self"
    n = int(cross)
    ln_s, ln_b = ("ln2_s", "ln2_b") if cross else ("ln1_s", "ln1_b")
    wq, q0 = (core.w["w_q"], 0) if cross else (core.w["w_qkv"], 0)
    wk, k0 = (core.w["w_kv"], 0) if cross else (core.w["w_qkv"], C)
    wv, v0 = (core.w["w_kv"], C) if cross else (core.w["w_qkv"], 2 * C)
    wo = core.w["w_co"] if cross else core.w["w_ao"]
    with ExitStack() as ctx:
        def sb(name, shape):
            return ctx.enter_context(nc.sbuf_tensor(f"{kind}_{name}", shape, FP32))

        xn = sb("xn", [P, C])
        lnT = sb("lnT", [P, HALVES, P])
        qT = sb("qT", [P, HALVES, P])
        kT = sb("kT", [P, HALVES * BPT, S])
        k_heads = core.k_heads
        z = sb("z", [P, NH, S])
        probs = sb("probs", [P, NH * S])
        zT = sb("zT", [P, PAIRS, P])
        row_max = sb("row_max", [P, NH])
        recip = sb("recip", [P, NH])
        heads = sb("heads", [P, C])
        headsT = sb("headsT", [P, HALVES, P])
        encT = sb("encT", [P, HALVES, P]) if cross else None
        kvT = encT if cross else lnT

        tr, qk, vv, proj = (core.banks[i] for i in (0, 1, 2, 7))
        tr, trh = tr[:, 0:C], tr[:, C:2 * C]
        scores = core.psum[:, 3 * 512:5 * 512].rearrange("p (h k) -> p h k", k=S)
        outs = core.psum[:, 3 * 512:5 * 512].rearrange("p (r n) -> p r n", n=P)
        pT = core.psum[:, 5 * 512:7 * 512]

        names = ("xn_ready xnT_ready ln_ready qk_ready v_ready q_copied v_copied scores_ready masked biased max_ready "
                 "shifted probs_ready probsT_ready probsT_copied out_ready recip_ready heads_ready headsT_ready "
                 "headsT_copied proj_ready x_ready bias_added enc_loaded k_copied k_spread_pool k_spread_act").split()
        [prepared] = semaphores(nc, ctx, f"{kind}_prepared")
        (xn_ready, xnT_ready, ln_ready, qk_ready, v_ready, q_copied, v_copied, scores_ready, masked, biased, max_ready,
         shifted, probs_ready, probsT_ready, probsT_copied, out_ready, recip_ready, heads_ready, headsT_ready,
         headsT_copied, proj_ready, x_ready, bias_added, enc_loaded, k_copied, k_spread_pool,
         k_spread_act) = semaphores(nc, ctx, *(f"{kind}_{s}" for s in names))
        block = ctx.enter_context(nc.Block())

        def there(t):
            return not isinstance(t, int) or t < TILES

        if cross:
            @block.sync
            def _(sp):
                def load(t):
                    sp.dma_start(encT[:, :, :], core.dram["enc"][:, :, ds(t, P)]).then_inc(enc_loaded, 16)

                load(0)
                with sp.Fori(1, TILES) as t:
                    sp.wait_ge(v_ready, t)
                    load(t)
        else:
            @block.sync
            def _(sp):
                load_later(core, sp)

        def spread_keys(eng, groups):
            for g in groups:
                rows = slice(32 * g, 32 * (g + 1))
                last = eng.tensor_tensor(
                    k_heads[rows, :, 2 * g:2 * g + 2, :],
                    kT[rows, :, :].unsqueeze(2).to_broadcast([32, HALVES * BPT, 2, S]),
                    core.parity[rows, :].unsqueeze(1).unsqueeze(3).to_broadcast([32, HALVES * BPT, 2, S]), ALU.mult)
            return last

        @block.gpsimd
        def _(pool):
            def add_bias(t):
                pool.wait_ge(xn_ready, t + 1)
                if later(t):
                    pool.wait_ge(k_spread_pool, t)
                xt = core.x[:, ds(t, C)]
                nc.gpsimd.tensor_tensor(xt, xt, core.rows[:, n, :], ALU.add).then_inc(bias_added, 1)

            def spread(t):
                pool.wait_ge(bias_added, t + 1)
                pool.wait_ge(k_copied, t + 1)
                spread_keys(nc.gpsimd, POOL_GROUPS).then_inc(k_spread_pool, 1)

            add_bias(0)
            spread(0)
            with pool.Fori(1, TILES) as t:
                add_bias(t)
                spread(t)

        @block.tensor
        def _(pe):
            def transpose_in(t):
                pe.wait_ge(xn_ready, t + 1)
                if later(t):
                    pe.wait_ge(ln_ready, t)
                if later(t - 3):
                    pe.wait_ge(headsT_copied, t - 3)
                for half in range(HALVES):
                    last = nc.tensor.transpose(tr[:, half * P:(half + 1) * P], xn[:, half * P:(half + 1) * P],
                                               core.ident[:, :])
                last.then_inc(xnT_ready, 1)

            def project_qk(t):
                pe.wait_ge(ln_ready, t + 1)
                if cross:
                    pe.wait_ge(enc_loaded, 16 * t + 16)
                for dst, w, c0, src in ((0, wq, q0, lnT), (HALVES, wk, k0, kvT)):
                    for half in range(HALVES):
                        for kb in range(HALVES):
                            last = nc.tensor.matmul(
                                qk[:, (dst + half) * P:(dst + half + 1) * P],
                                w[:, kb, c0 + half * P:c0 + (half + 1) * P], src[:, kb, :],
                                start=(kb == 0), stop=(kb == HALVES - 1))
                last.then_inc(qk_ready, 1)

            def project_v(t):
                if later(t):
                    pe.wait_ge(v_copied, t)
                for kb in range(HALVES):
                    last = nc.tensor.matmul(vv[:, 0:C], kvT[:, kb, :], wv[:, kb, v0:v0 + C],
                                            start=(kb == 0), stop=(kb == HALVES - 1))
                last.then_inc(v_ready, 1)

            def score(t):
                pe.wait_ge(q_copied, t + 1)
                pe.wait_ge(k_spread_pool, t + 1)
                pe.wait_ge(k_spread_act, t + 1)
                if later(t):
                    pe.wait_ge(masked, t)
                if later(t - 1):
                    pe.wait_ge(heads_ready, t - 1)
                for half in range(HALVES):
                    for b in range(BPT):
                        last = nc.tensor.matmul(
                            scores[b * S:(b + 1) * S, half * PAIRS:(half + 1) * PAIRS, :],
                            qT[:, half, b * S:(b + 1) * S], k_heads[:, half * BPT + b, :, :], start=True, stop=True)
                    last.then_inc(scores_ready, 1)

            def transpose_probs(t):
                if later(t):
                    pe.wait_ge(probsT_copied, t)
                for pair in range(PAIRS):
                    if pair % HALF_PAIRS == 0:
                        pe.wait_ge(probs_ready, HALVES * t + pair // HALF_PAIRS + 1)
                    last = nc.tensor.transpose(pT[:, pair * P:(pair + 1) * P], probs[:, pair * P:(pair + 1) * P],
                                               core.ident[:, :])
                last.then_inc(probsT_ready, 1)

            def attend(t):
                pe.wait_ge(probsT_copied, t + 1)
                pe.wait_ge(v_copied, t + 1)
                if there(t + 1):
                    pe.wait_ge(masked, t + 2)
                for pair in range(PAIRS):
                    for b in range(BPT):
                        rows = slice(b * S, (b + 1) * S)
                        last = nc.tensor.matmul(outs[rows, pair, 0:PW], zT[:, pair, rows],
                                                core.vpad[:, pair, b * PW:(b + 1) * PW], start=True, stop=True)
                last.then_inc(out_ready, 1)

            def transpose_heads(t):
                pe.wait_ge(heads_ready, t + 1)
                if later(t):
                    pe.wait_ge(headsT_copied, t)
                for half in range(HALVES):
                    last = nc.tensor.transpose(trh[:, half * P:(half + 1) * P], heads[:, half * P:(half + 1) * P],
                                               core.ident[:, :])
                last.then_inc(headsT_ready, 1)

            def project_out(t):
                pe.wait_ge(headsT_copied, t + 1)
                if later(t):
                    pe.wait_ge(x_ready, t)
                for kb in range(HALVES):
                    last = nc.tensor.matmul(proj[:, 0:C], headsT[:, kb, :], wo[:, kb, :],
                                            start=(kb == 0), stop=(kb == HALVES - 1))
                last.then_inc(proj_ready, 1)

            def body(t):
                if there(t + 1):
                    score(t + 1)
                if there(t + 2):
                    project_qk(t + 2)
                attend(t)
                if later(t):
                    project_out(t - 1)
                if there(t + 3):
                    transpose_in(t + 3)
                if there(t + 2):
                    project_v(t + 2)
                if there(t + 1):
                    transpose_probs(t + 1)
                transpose_heads(t)

            transpose_in(0)
            project_qk(0)
            project_v(0)
            transpose_in(1)
            score(0)
            project_qk(1)
            project_v(1)
            transpose_in(2)
            transpose_probs(0)
            body(0)
            with pe.Fori(0, (TILES - 4) // UNROLLED) as i:
                for j in range(UNROLLED):
                    body(UNROLLED * i + 1 + j)
            for t in range(TILES - 3, TILES):
                body(t)
            project_out(TILES - 1)

        @block.scalar
        def _(act):
            def normalise(t):
                if later(t):
                    act.wait_ge(xnT_ready, t)
                nc.scalar.activation(xn[:, :], core.x[:, ds(t, C)], ACT.Identity, scale=core.rstd[:, ds(t, 1)],
                                     bias=core.neg_mean[:, ds(t, 1)]).then_inc(xn_ready, 1)

            def copy_ln(t):
                act.wait_ge(xnT_ready, t + 1)
                if later(t):
                    act.wait_ge(v_ready, t)
                if later(t - 2):
                    act.wait_ge(headsT_ready, t - 2)
                for half in range(HALVES):
                    last = nc.scalar.activation(lnT[:, half, :], tr[:, half * P:(half + 1) * P], ACT.Identity,
                                                scale=col(core, ln_s, half), bias=col(core, ln_b, half))
                last.then_inc(ln_ready, 1)

            def copy_qk(t):
                act.wait_ge(qk_ready, t + 1)
                if later(t):
                    act.wait_ge(scores_ready, HALVES * t)
                    act.wait_ge(k_spread_pool, t)
                for half in range(HALVES):
                    last = nc.scalar.activation(
                        kT[:, half * BPT:(half + 1) * BPT, :].rearrange("p b k -> p (b k)"),
                        qk[:, (HALVES + half) * P:(HALVES + half + 1) * P], ACT.Identity,
                        bias=col(core, f"b_k_{kind}", half))
                last.then_inc(k_copied, 1)
                for half in range(HALVES):
                    last = nc.scalar.activation(qT[:, half, :], qk[:, half * P:(half + 1) * P], ACT.Identity,
                                                scale=HD ** -0.5, bias=core.q_bias[:, n, half:half + 1])
                last.then_inc(q_copied, 1)

            def spread(t):
                act.wait_ge(k_copied, t + 1)
                for g in ACT_GROUPS:
                    rows = slice(32 * g, 32 * (g + 1))
                    for e in range(2):
                        last = nc.scalar.activation(k_heads[rows, :, 2 * g + e, :], kT[rows, :, :], ACT.Copy,
                                                    scale=core.parity[rows, e:e + 1])
                last.then_inc(k_spread_act, 1)

            def copy_values(t):
                act.wait_ge(v_ready, t + 1)
                if later(t):
                    act.wait_ge(out_ready, t)
                for e in range(2):
                    for b in range(BPT):
                        a = b * PW + e * HD
                        last = nc.scalar.activation(
                            core.vpad[e * S:(e + 1) * S, :, a:a + HD],
                            vv[b * S:(b + 1) * S, 0:C].rearrange("p (r e d) -> p r e d", r=PAIRS, e=2)[:, :, e, :],
                            ACT.Copy)
                last.then_inc(v_copied, 1)

            def exps(t):
                if later(t):
                    act.wait_ge(probsT_ready, t)
                for half in range(HALVES):
                    act.wait_ge(shifted, HALVES * t + half + 1)
                    its_heads = slice(half * PAIRS, (half + 1) * PAIRS)
                    nc.scalar.activation(probs[:, half * PAIRS * S:(half + 1) * PAIRS * S],
                                         z[:, its_heads, :].rearrange("p h k -> p (h k)"), ACT.Exp).then_inc(probs_ready, 1)

            def copy_probs(t):
                act.wait_ge(probsT_ready, t + 1)
                if later(t):
                    act.wait_ge(out_ready, t)
                for j in range(2):
                    last = nc.scalar.activation(zT[:, j * PAIRS // 2:(j + 1) * PAIRS // 2, :],
                                                pT[:, j * 512:(j + 1) * 512], ACT.Copy)
                last.then_inc(probsT_copied, 1)

            def copy_heads(t):
                act.wait_ge(headsT_ready, t + 1)
                if later(t):
                    act.wait_ge(proj_ready, t)
                for half in range(HALVES):
                    last = nc.scalar.activation(headsT[:, half, :], trh[:, half * P:(half + 1) * P], ACT.Identity,
                                                bias=col(core, f"b_v_{kind}", half))
                last.then_inc(headsT_copied, 1)

            def body(t):
                copy_probs(t)
                if there(t + 2):
                    copy_ln(t + 2)
                if later(t):
                    copy_heads(t - 1)
                if there(t + 3):
                    normalise(t + 3)
                if there(t + 2):
                    copy_qk(t + 2)
                if there(t + 1):
                    copy_values(t + 1)
                if there(t + 1):
                    exps(t + 1)
                if there(t + 2):
                    spread(t + 2)

            normalise(0)
            copy_ln(0)
            normalise(1)
            act.wait_ge(prepared, 1)
            copy_qk(0)
            spread(0)
            copy_values(0)
            copy_ln(1)
            normalise(2)
            copy_qk(1)
            spread(1)
            exps(0)
            body(0)
            with act.Fori(1, TILES - 3) as t:
                body(t)
            for t in range(TILES - 3, TILES):
                body(t)
            copy_heads(TILES - 1)

        @block.vector
        def _(dve):
            def apply_mask(t):
                mask = core.cross_mask[:, ds(t, S)] if cross else core.self_mask[:, :]
                if later(t):
                    dve.wait_ge(probs_ready, HALVES * t)
                for half in range(HALVES):
                    dve.wait_ge(scores_ready, HALVES * t + half + 1)
                    its_heads = slice(half * PAIRS, (half + 1) * PAIRS)
                    last = nc.vector.tensor_tensor(z[:, its_heads, :], scores[:, its_heads, :],
                                                   mask.unsqueeze(1).to_broadcast([P, PAIRS, S]), ALU.mult)
                last.then_inc(masked, 1)

            def subtract_max(t):
                bias = core.cross_bias[:, ds(t, S)] if cross else core.self_bias[:, :]
                dve.wait_ge(masked, t + 1)
                nc.vector.tensor_tensor(z[:, :, :], z[:, :, :], bias.unsqueeze(1).to_broadcast([P, NH, S]),
                                        ALU.add).then_inc(biased, 1)
                dve.wait_ge(biased, t + 1)
                nc.vector.tensor_reduce(out=row_max[:, :], in_=z[:, :, :], op=ALU.max, axis=AX.X).then_inc(max_ready, 1)
                dve.wait_ge(max_ready, t + 1)
                for half in range(HALVES):
                    its_heads = slice(half * PAIRS, (half + 1) * PAIRS)
                    nc.vector.tensor_tensor(z[:, its_heads, :], z[:, its_heads, :],
                                            row_max[:, its_heads].unsqueeze(2).to_broadcast([P, PAIRS, S]),
                                            ALU.subtract).then_inc(shifted, 1)

            def divide(t):
                dve.wait_ge(out_ready, t + 1)
                nc.vector.reciprocal(recip[:, :].rearrange("p (r e) -> p r e", e=2),
                                     outs[:, :, 2 * HD:PW]).then_inc(recip_ready, 1)
                dve.wait_ge(recip_ready, t + 1)
                if later(t):
                    dve.wait_ge(headsT_ready, t)
                nc.vector.tensor_tensor(
                    heads[:, :].rearrange("p (r e d) -> p r e d", e=2, d=HD),
                    outs[:, :, 0:2 * HD].rearrange("p r (e d) -> p r e d", e=2),
                    recip[:, :].rearrange("p (r e) -> p r e", e=2).unsqueeze(3).to_broadcast([P, PAIRS, 2, HD]),
                    ALU.mult).then_inc(heads_ready, 1)

            def add_residual(t):
                xt = core.x[:, ds(t, C)]
                dve.wait_ge(proj_ready, t + 1)
                dve.wait_ge(bias_added, t + 1)
                nc.vector.tensor_tensor(xt, proj[:, 0:C], xt, ALU.add).then_inc(x_ready, 1)
                dve.wait_ge(x_ready, t + 1)
                nc.vector.bn_stats(core.stats[:, ds(t, 6)], xt)

            def body(t):
                if there(t + 1):
                    apply_mask(t + 1)
                    subtract_max(t + 1)
                divide(t)
                if later(t):
                    add_residual(t - 1)

            b_q = COLS[f"b_q_{kind}"][0]
            nc.vector.tensor_scalar_mul(core.q_bias[:, n, :], core.cols[:, b_q:b_q + 2], HD ** -0.5).then_inc(prepared, 1)
            mask, bias = (core.cross_mask, core.cross_bias) if cross else (core.self_mask, core.self_bias)
            nc.vector.tensor_scalar(bias[:, :], mask[:, :], -1.0, MASKED, ALU.add, ALU.mult).then_inc(prepared, 1)
            dve.wait_ge(prepared, 2)
            apply_mask(0)
            subtract_max(0)
            body(0)
            with dve.Fori(1, TILES - 1) as t:
                body(t)
            body(TILES - 1)
            add_residual(TILES - 1)


def gelu_phase(core):
    nc = core.nc
    n4 = 4
    runs, hidden = TILES // n4, F1 // P
    w1, w2 = core.w["w1"], core.w["w2"]
    with ExitStack() as ctx:
        def sb(name, shape):
            return ctx.enter_context(nc.sbuf_tensor(f"gelu_{name}", shape, FP32))

        xn = sb("xn", [P, n4, C])
        lnT = sb("lnT", [P, HALVES, n4 * P])
        hT = sb("hT", [P, hidden, n4 * P])
        tr = core.banks[0:2]
        up_banks = core.banks[2:5]
        down_banks = core.banks[5:7]
        names = ("xn_ready", "xnT_ready", "ln_ready", "up_ready", "gelu_ready", "down_ready", "x_ready", "bias_added")
        (xn_ready, xnT_ready, ln_ready, up_ready, gelu_ready, down_ready, x_ready,
         bias_added) = semaphores(nc, ctx, *(f"gelu_{s}" for s in names))
        block = ctx.enter_context(nc.Block())

        @block.gpsimd
        def _(pool):
            with pool.Fori(0, runs) as s:
                pool.wait_ge(xn_ready, s + 1)
                xs = core.x[:, ds(s, n4 * C)].rearrange("p (j c) -> p j c", j=n4)
                nc.gpsimd.tensor_tensor(xs, xs, core.rows[:, 2, :].unsqueeze(1).to_broadcast([P, n4, C]),
                                        ALU.add).then_inc(bias_added, 1)

        @block.tensor
        def _(pe):
            def transpose(s):
                pe.wait_ge(xn_ready, s + 1)
                if later(s):
                    pe.wait_ge(ln_ready, s)
                for half in range(HALVES):
                    for j in range(n4):
                        last = nc.tensor.transpose(tr[half][:, j * P:(j + 1) * P],
                                                   xn[:, j, half * P:(half + 1) * P], core.ident[:, :])
                last.then_inc(xnT_ready, 1)

            def up(s):
                pe.wait_ge(ln_ready, s + 1)
                for h in range(hidden):
                    if h >= len(up_banks) or later(s):
                        pe.wait_ge(gelu_ready, s * hidden + h + 1 - len(up_banks))
                    for kb in range(HALVES):
                        last = nc.tensor.matmul(up_banks[h % len(up_banks)], w1[:, kb, h * P:(h + 1) * P],
                                                lnT[:, kb, :], start=(kb == 0), stop=(kb == HALVES - 1))
                    last.then_inc(up_ready, 1)

            def down(s):
                pe.wait_ge(gelu_ready, s * hidden + hidden)
                if later(s):
                    pe.wait_ge(x_ready, s * n4)
                for j in range(n4):
                    for h in range(hidden):
                        last = nc.tensor.matmul(down_banks[j // 2][:, (j % 2) * C:(j % 2 + 1) * C],
                                                hT[:, h, j * P:(j + 1) * P], w2[:, h, :],
                                                start=(h == 0), stop=(h == hidden - 1))
                    if j % 2:
                        last.then_inc(down_ready, 1)

            transpose(0)
            up(0)
            transpose(1)
            down(0)
            with pe.Fori(1, runs - 1) as s:
                up(s)
                transpose(s + 1)
                down(s)
            up(runs - 1)
            down(runs - 1)

        @block.scalar
        def _(act):
            def copy_in(s):
                act.wait_ge(xnT_ready, s + 1)
                for half in range(HALVES):
                    last = nc.scalar.activation(lnT[:, half, :], tr[half], ACT.Identity,
                                                scale=col(core, "ln3_s", half), bias=col(core, "ln3_b", half))
                last.then_inc(ln_ready, 1)

            def gelus(s):
                if later(s):
                    act.wait_ge(down_ready, 2 * s)
                for h in range(hidden):
                    act.wait_ge(up_ready, s * hidden + h + 1)
                    nc.scalar.activation(hT[:, h, :], up_banks[h % len(up_banks)], ACT.Gelu_apprx_tanh,
                                         bias=col(core, "b1", h)).then_inc(gelu_ready, 1)

            copy_in(0)
            gelus(0)
            copy_in(1)
            with act.Fori(1, runs - 1) as s:
                gelus(s)
                copy_in(s + 1)
            gelus(runs - 1)

        @block.vector
        def _(dve):
            def normalise(s):
                if later(s):
                    dve.wait_ge(xnT_ready, s)
                for j in range(n4):
                    t = s * n4 + j
                    last = nc.vector.tensor_scalar(xn[:, j, :], core.x[:, ds(t, C)], core.rstd[:, ds(t, 1)],
                                                   core.neg_mean[:, ds(t, 1)], ALU.mult, ALU.add)
                last.then_inc(xn_ready, 1)

            def add_residual(s):
                for j in range(n4):
                    t = s * n4 + j
                    if j % 2 == 0:
                        dve.wait_ge(down_ready, 2 * s + j // 2 + 1)
                    if j == 0:
                        dve.wait_ge(bias_added, s + 1)
                    xt = core.x[:, ds(t, C)]
                    nc.vector.tensor_tensor(xt, down_banks[j // 2][:, (j % 2) * C:(j % 2 + 1) * C], xt,
                                            ALU.add).then_inc(x_ready, 1)
                for j in range(n4):
                    t = s * n4 + j
                    dve.wait_ge(x_ready, t + 1)
                    nc.vector.bn_stats(core.stats[:, ds(t, 6)], core.x[:, ds(t, C)])

            normalise(0)
            normalise(1)
            add_residual(0)
            with dve.Fori(1, runs - 1) as s:
                normalise(s + 1)
                add_residual(s)
            add_residual(runs - 1)


MIX = (1, 0, 3, 2, 4)
NW, NK, NR, NV, NG = range(NMIX)
CH = 2
RT = CH * P
RB = RT // S
RUNS = B * S // RT
JG = 2
GROUPS_R = HALVES * RS // JG
JQ = P // RH
POOL_SUM = 1
SUMS = GROUPS_R * JG // JQ


def group(n):
    q, part = divmod(n, JQ // JG)
    return q % HALVES, q // HALVES * JQ + part * JG


def recurrence_phase(core):
    nc = core.nc
    w = core.w
    with ExitStack() as ctx:
        def sb(name, shape):
            return ctx.enter_context(nc.sbuf_tensor(f"rec_{name}", shape, FP32))

        xn = sb("xn", [P, CH, C])
        xa = sb("xa", [P, HALVES, RB, S + 1])
        sx = sb("sx", [P, HALVES, RB, S])
        xin = sb("xin", [P, HALVES, RT])
        mixer_a = sb("mixer_a", [P, RT])
        mixer_b = sb("mixer_b", [P, P])
        mixed = sb("mixed", [P, 2, HALVES, RT])
        xm = sb("xm", [P, 2, HALVES, RT])
        decay_in = sb("decay_in", [P, P])
        decay_exp = sb("decay_exp", [P, HALVES * RB, S])
        gate_tanh = sb("gate_tanh", [P, HALVES * RT])
        kT = sb("kT", [P, 2, HALVES, RB, S])
        rT = sb("rT", [P, 2, HALVES, RT])
        vT = sb("vT", [P, 2, HALVES, RT])
        wT = sb("wT", [P, 2, HALVES * RB, S])
        bonus = sb("bonus", [P, HALVES, RT])
        u_sum = sb("u_sum", [P, HALVES, P])
        bonus_v = sb("bonus_v", [P, HALVES, RT])
        st = sb("st", [P, GROUPS_R, JG, RB, S])
        o = sb("o", [P, HALVES * RT])
        o_sq = sb("o_sq", [P, CH * C])
        mean = sb("mean", [P, CH * RH])

        tr, small = core.banks[0], core.banks[1]
        mix_banks, proj_banks = core.banks[2:4], core.banks[4:6]
        v_bank, o_bank = core.banks[6], core.banks[7]

        names = ("xn_ready xnT_ready xa_ready u_ready sx_ready xin_ready mixer_ready mixer_tanh mix_ready mixed_ready "
                 "xm_ready decay_ready decay_tanh proj_ready copied gate_ready gate_done decay_expd w_ready oT_ready "
                 "bonus_ready bonus_sum_ready vj_ready kv_ready scanned read_ready pool_read_ready summed "
                 "o_bonus o_ready mean_ready o_stored sq_ready var_stored").split()
        [mixer_cleared] = semaphores(nc, ctx, "rec_mixer_cleared")
        sem = dict(zip(names, semaphores(nc, ctx, *(f"rec_{n}" for n in names))))
        (xn_ready, xnT_ready, xa_ready, u_ready, sx_ready, xin_ready, mixer_ready, mixer_tanh, mix_ready, mixed_ready,
         xm_ready, decay_ready, decay_tanh, proj_ready, copied, gate_ready, gate_done, decay_expd, w_ready, oT_ready,
         bonus_ready, bonus_sum_ready, vj_ready, kv_ready, scanned, read_ready, pool_read_ready, summed,
         o_bonus, o_ready, mean_ready, o_stored, sq_ready, var_stored) = (sem[n] for n in names)
        block = ctx.enter_context(nc.Block())

        def bodies(eng, body):
            body(0, 0, True, True)
            body(1, 1, True, True)
            with eng.Fori(1, RUNS // 2 - 1) as i:
                body(2 * i, 0, True, True)
                body(2 * i + 1, 1, True, True)
            body(RUNS - 2, 0, True, False)
            body(RUNS - 1, 1, False, False)

        @block.gpsimd
        def _(pool):
            def step_back(s):
                pool.wait_ge(xa_ready, s + 1)
                if later(s):
                    pool.wait_ge(mixed_ready, s * NMIX)
                nc.gpsimd.tensor_tensor(sx[:, :, :, :].rearrange("p h b t -> p (h b) t"),
                                        xa[:, :, :, 0:S].rearrange("p h b t -> p (h b) t"),
                                        xa[:, :, :, 1:S + 1].rearrange("p h b t -> p (h b) t"),
                                        ALU.subtract).then_inc(sx_ready, 1)

            def make_bonus(s, u):
                pool.wait_ge(copied, s * 3 + 2)
                if later(s):
                    pool.wait_ge(bonus_sum_ready, s)
                nc.gpsimd.tensor_tensor(bonus[:, :, :], rT[:, u, :, :],
                                        kT[:, u, :, :, :].rearrange("p h b t -> p h (b t)"),
                                        ALU.mult).then_inc(bonus_ready, 1)

            def mix(s, m):
                pool.wait_ge(mixed_ready, s * NMIX + m + 1)
                if m >= 2:
                    pool.wait_ge(proj_ready, s * NMIX + m - 1)
                nc.gpsimd.tensor_tensor(
                    xm[:, m % 2, :, :].rearrange("p h (b t) -> p (h b) t", t=S),
                    mixed[:, m % 2, :, :].rearrange("p h (b t) -> p (h b) t", t=S),
                    xa[:, :, :, 1:S + 1].rearrange("p h b t -> p (h b) t"), ALU.add).then_inc(xm_ready, 1)

            def read(s, u, n):
                pool.wait_ge(scanned, s * GROUPS_R + n + 1)
                half, _ = group(n)
                states = st[:, n, :, :, :].rearrange("p j b t -> p j (b t)")
                nc.gpsimd.tensor_tensor(states, states, rT[:, u, half, :].unsqueeze(1).to_broadcast([P, JG, RT]),
                                        ALU.mult).then_inc(pool_read_ready, 1)

            def body(s, u, more, _):
                if more:
                    step_back(s + 1)
                make_bonus(s, u)
                for n in range(GROUPS_R):
                    if n * JG // JQ == POOL_SUM:
                        read(s, u, n)
                    if n in (2, 3, 4, 5, 6) and more:
                        mix(s + 1, n - 2)

            step_back(0)
            for m in range(NMIX):
                mix(0, m)
            bodies(pool, body)

        @block.tensor
        def _(pe):
            def transpose(s):
                pe.wait_ge(xn_ready, s + 1)
                if later(s):
                    pe.wait_ge(decay_expd, s)
                for half in range(HALVES):
                    for c in range(CH):
                        a = half * RT + c * P
                        last = nc.tensor.transpose(tr[:, a:a + P], xn[:, c, half * P:(half + 1) * P], core.ident[:, :])
                last.then_inc(xnT_ready, 1)

            def mixer(s):
                pe.wait_ge(xin_ready, s + 1)
                if later(s - 2):
                    pe.wait_ge(o_stored, s - 2)
                for kb in range(HALVES):
                    nc.tensor.matmul(small[:, 0:RT], w["maa_w1"][:, kb, 0:P], xin[:, kb, :],
                                     start=(kb == 0), stop=(kb == HALVES - 1))
                for kb in range(HALVES):
                    for c in range(CH):
                        last = nc.tensor.matmul(small[c * DD:c * DD + DM, RT:RT + P], w["maa_w1"][:, kb, P:P + DM],
                                                xin[:, kb, c * P:(c + 1) * P], start=(kb == 0), stop=(kb == HALVES - 1))
                last.then_inc(mixer_ready, 1)

            def mix(s, m):
                if m == 0:
                    pe.wait_ge(mixer_tanh, s + 1)
                if later(s) or m >= 2:
                    pe.wait_ge(mixed_ready, s * NMIX + m - 1)
                f = MIX[m]
                for half in range(HALVES):
                    out = mix_banks[m % 2][:, half * RT:(half + 1) * RT]
                    if f < 4:
                        rows = slice(f * DM, (f + 1) * DM)
                        last = nc.tensor.matmul(out, core.maa_w2a[rows, half * P:(half + 1) * P], mixer_a[rows, :],
                                                start=True, stop=True)
                        continue
                    for c in range(CH):
                        last = nc.tensor.matmul(out[:, c * P:(c + 1) * P], core.maa_w2b[:, c, half * P:(half + 1) * P],
                                                mixer_b[:, :], start=True, stop=True)
                last.then_inc(mix_ready, 1)

            def project(s, m):
                pe.wait_ge(xm_ready, s * NMIX + m + 1)
                if m == NW:
                    pe.wait_ge(xa_ready, s + 1)
                    if later(s):
                        pe.wait_ge(o_bonus, s)
                    for kb in range(HALVES):
                        for c in range(CH):
                            last = nc.tensor.matmul(tr[c * DD:(c + 1) * DD, 0:P], w["td_w1"][:, kb, :],
                                                    xm[:, m % 2, kb, c * P:(c + 1) * P],
                                                    start=(kb == 0), stop=(kb == HALVES - 1))
                    last.then_inc(proj_ready, 1)
                    return
                name = {NK: "WkT", NR: "WrT", NV: "WvT", NG: "WgT"}[m]
                bank = proj_banks[m % 2]
                if later(s) and m == NK:
                    pe.wait_ge(copied, s * 3)
                if later(s) and m == NR:
                    pe.wait_ge(gate_done, s)
                if m >= 3:
                    pe.wait_ge(copied, s * 3 + m - 2)
                for half in range(HALVES):
                    for kb in range(HALVES):
                        last = nc.tensor.matmul(bank[:, half * RT:(half + 1) * RT], w[name][:, kb, half * P:(half + 1) * P],
                                                xm[:, m % 2, kb, :], start=(kb == 0), stop=(kb == HALVES - 1))
                last.then_inc(proj_ready, 1)

            def decay(s):
                pe.wait_ge(decay_tanh, s + 1)
                for half in range(HALVES):
                    for c in range(CH):
                        a = half * RT + c * P
                        last = nc.tensor.matmul(tr[:, a:a + P], core.td_w2[:, c, half * P:(half + 1) * P],
                                                decay_in[:, :], start=True, stop=True)
                last.then_inc(decay_ready, 1)

            def bonus_sums(s, more):
                pe.wait_ge(bonus_ready, s + 1)
                pe.wait_ge(u_ready, 1)
                if more:
                    pe.wait_ge(xa_ready, s + 2)
                else:
                    pe.wait_ge(decay_expd, s + 1)
                for half in range(HALVES):
                    last = nc.tensor.matmul(tr[:, 0:RT], u_sum[:, half, :], bonus[:, half, :],
                                            start=(half == 0), stop=(half == HALVES - 1))
                last.then_inc(bonus_sum_ready, 1)

            def transpose_out(s, tanhs):
                pe.wait_ge(o_ready, s + 1)
                pe.wait_ge(mixer_tanh, tanhs)
                for c in range(CH):
                    for jq in range(HALVES):
                        a = c * C + jq * P
                        last = nc.tensor.transpose(small[:, a:a + P], o[:, jq * RT + c * P:jq * RT + (c + 1) * P],
                                                   core.ident[:, :])
                last.then_inc(oT_ready, 1)

            def spread(s, u, n):
                half, j0 = group(n)
                if n == 0:
                    pe.wait_ge(copied, s * 3 + 3)
                if later(s) or n:
                    pe.wait_ge(kv_ready, s * GROUPS_R + n)
                for jj in range(JG):
                    jq, jl = divmod(j0 + jj, JQ)
                    last = nc.tensor.matmul(v_bank[:, jj * RT:(jj + 1) * RT], core.spread[:, half * JQ + jl, :],
                                            vT[:, u, jq, :], start=True, stop=True)
                last.then_inc(vj_ready, 1)

            def sum_heads(s, q):
                half, jq = q % HALVES, q // HALVES
                per_sum = JQ // JG
                if q == POOL_SUM:
                    pe.wait_ge(pool_read_ready, (s + 1) * per_sum)
                else:
                    pe.wait_ge(read_ready, s * (GROUPS_R - per_sum) + (q + 1 - int(q > POOL_SUM)) * per_sum)
                if q == 0 and later(s):
                    pe.wait_ge(o_ready, s)
                for jl in range(JQ):
                    rows = slice(jl * RH, (jl + 1) * RH)
                    states = st[:, q * JQ // JG + jl // JG, jl % JG, :, :].rearrange("p b t -> p (b t)")
                    last = nc.tensor.matmul(o_bank[rows, jq * RT:(jq + 1) * RT], core.head_sum[:, half, 0:RH], states,
                                            start=(half == 0), stop=(half == HALVES - 1))
                last.then_inc(summed, 1)

            def body(s, u, more, more2):
                for n in range(GROUPS_R):
                    if n == 0 and later(s):
                        sum_heads(s - 1, SUMS - 1)
                    spread(s, u, n)
                    if n == 0:
                        project(s, NG)
                    if n == 1:
                        bonus_sums(s, more)
                        if more:
                            mixer(s + 1)
                    if n == 3 and later(s):
                        transpose_out(s - 1, s + 2 if more else s + 1)
                    if n in (2, 3) and more:
                        mix(s + 1, n - 2)
                    if n in (2, 6):
                        sum_heads(s, n // 2 - 1)
                    if n in (4, 5, 6) and more:
                        mix(s + 1, n - 2)
                    if n >= 4 and more:
                        project(s + 1, n - 4)
                    if n == 4:
                        sum_heads(s, POOL_SUM)
                    if n == 6 and more:
                        decay(s + 1)
                    if n == 7 and more2:
                        transpose(s + 2)

            transpose(0)
            mixer(0)
            for m in range(NMIX):
                mix(0, m)
                if m:
                    project(0, m - 1)
                if m == NMIX - 1:
                    decay(0)
            transpose(1)
            bodies(pe, body)
            sum_heads(RUNS - 1, SUMS - 1)
            transpose_out(RUNS - 1, RUNS)

        @block.scalar
        def _(act):
            def normalise(s):
                if later(s):
                    act.wait_ge(xnT_ready, s)
                for c in range(CH):
                    t = s * CH + c
                    last = nc.scalar.activation(xn[:, c, :], core.x[:, ds(t, C)], ACT.Identity,
                                                scale=core.rstd[:, ds(t, 1)], bias=core.neg_mean[:, ds(t, 1)])
                last.then_inc(xn_ready, 1)

            def copy_in(s):
                act.wait_ge(xnT_ready, s + 1)
                if later(s):
                    act.wait_ge(xm_ready, s * NMIX)
                for half in range(HALVES):
                    last = nc.scalar.activation(xa[:, half, :, 1:S + 1],
                                                tr[:, half * RT:(half + 1) * RT].rearrange("p (b t) -> p b t", t=S),
                                                ACT.Identity, scale=col(core, "r_ln1_w", half),
                                                bias=col(core, "r_ln1_b", half))
                last = nc.scalar.activation(xa[:, :, :, 0], core.state_rows[:, 1, :, ds(s, RB)], ACT.Copy)
                last.then_inc(xa_ready, 1)

            def mixer(s):
                act.wait_ge(mixer_ready, s + 1)
                nc.scalar.activation(mixer_a[:, :], small[:, 0:RT], ACT.Tanh)
                for c in range(CH):
                    rows = slice(c * DD, c * DD + DM)
                    last = nc.scalar.activation(mixer_b[rows, :], small[rows, RT:RT + P], ACT.Tanh)
                last.then_inc(mixer_tanh, 1)

            def copy(s, u, m):
                act.wait_ge(proj_ready, s * NMIX + m + 1)
                bank = proj_banks[m % 2]
                if m == NW:
                    nc.scalar.activation(decay_in[:, :], tr[:, 0:P], ACT.Tanh).then_inc(decay_tanh, 1)
                elif m == NG:
                    nc.scalar.activation(gate_tanh[:, :], bank, ACT.Tanh, scale=0.5).then_inc(gate_ready, 1)
                elif m == NK:
                    nc.scalar.activation(kT[:, u, :, :, :].rearrange("p h b t -> p (h b t)"), bank,
                                         ACT.Copy).then_inc(copied, 1)
                else:
                    dst = rT if m == NR else vT
                    nc.scalar.activation(dst[:, u, :, :].rearrange("p h t -> p (h t)"), bank, ACT.Copy).then_inc(copied, 1)

            def decay(s, u):
                act.wait_ge(decay_ready, s + 1)
                for half in range(HALVES):
                    last = nc.scalar.activation(decay_exp[:, half * RB:(half + 1) * RB, :].rearrange("p b t -> p (b t)"),
                                                tr[:, half * RT:(half + 1) * RT], ACT.Exp,
                                                bias=col(core, "time_decay", half))
                last.then_inc(decay_expd, 1)
                act.wait_ge(decay_expd, s + 1)
                nc.scalar.activation(wT[:, u, :, 1:S], decay_exp[:, :, 0:S - 1], ACT.Exp, scale=-1.0).then_inc(w_ready, 1)

            def square(s):
                act.wait_ge(o_stored, s + 1)
                if later(s):
                    act.wait_ge(var_stored, s)
                nc.scalar.activation(o_sq[:, :], core.o[:, ds(s, CH * C)], ACT.Square).then_inc(sq_ready, 1)

            def projections(s, u, squares):
                copy(s, u, NW)
                if later(squares - 1):
                    square(squares - 2)
                copy(s, u, NK)
                copy(s, u, NR)
                decay(s, u)
                copy(s, u, NV)

            def body(s, u, more, more2):
                copy(s, u, NG)
                if more:
                    mixer(s + 1)
                if more2:
                    normalise(s + 2)
                if more:
                    projections(s + 1, 1 - u, s)
                elif later(s - 1):
                    square(s - 2)
                if more2:
                    copy_in(s + 2)

            normalise(0)
            copy_in(0)
            normalise(1)
            act.wait_ge(mixer_cleared, 1)
            mixer(0)
            projections(0, 0, 0)
            copy_in(1)
            bodies(act, body)
            square(RUNS - 2)
            square(RUNS - 1)

        @block.vector
        def _(dve):
            def mixer_input(s):
                dve.wait_ge(sx_ready, s + 1)
                if later(s):
                    dve.wait_ge(mixer_ready, s)
                for half in range(HALVES):
                    last = nc.vector.scalar_tensor_tensor(
                        out=xin[:, half, :].rearrange("p (b t) -> p b t", t=S), in0=sx[:, half, :, :],
                        scalar=col(core, "maa_x", half), in1=xa[:, half, :, 1:S + 1], op0=ALU.mult, op1=ALU.add)
                last.then_inc(xin_ready, 1)

            def mix(s, m):
                dve.wait_ge(mix_ready, s * NMIX + m + 1)
                if later(s) or m >= 2:
                    dve.wait_ge(xm_ready, s * NMIX + m - 1)
                for half in range(HALVES):
                    last = nc.vector.scalar_tensor_tensor(
                        out=mixed[:, m % 2, half, :], in0=mix_banks[m % 2][:, half * RT:(half + 1) * RT],
                        scalar=col(core, "maa_stack", MIX[m] * HALVES + half),
                        in1=sx[:, half, :, :].rearrange("p b t -> p (b t)"), op0=ALU.add, op1=ALU.mult)
                last.then_inc(mixed_ready, 1)

            def gate(s):
                dve.wait_ge(gate_ready, s + 1)
                nc.vector.scalar_tensor_tensor(out=core.gate[:, ds(s, HALVES * RT)], in0=gate_tanh[:, :], scalar=1.0,
                                               in1=proj_banks[NG % 2], op0=ALU.add, op1=ALU.mult).then_inc(gate_done, 1)

            def recur(s, u, n):
                half, j0 = group(n)
                g = s * GROUPS_R + n
                dve.wait_ge(vj_ready, g + 1)
                if later(s):
                    dve.wait_ge(summed, s * SUMS + n * JG // JQ + 1 - SUMS)
                if n == 0:
                    dve.wait_ge(copied, s * 3 + 3)
                    dve.wait_ge(w_ready, s + 1)
                nc.vector.tensor_copy(st[:, n, :, :, 0], core.state0[:, half * RS + j0:half * RS + j0 + JG, ds(s, RB)])
                nc.vector.tensor_tensor(
                    st[:, n, :, :, 1:S], v_bank.rearrange("p (j b t) -> p j b t", j=JG, t=S)[:, :, :, 0:S - 1],
                    kT[:, u, half, :, 0:S - 1].unsqueeze(1).to_broadcast([P, JG, RB, S - 1]),
                    ALU.mult).then_inc(kv_ready, 1)
                dve.wait_ge(kv_ready, g + 1)
                decays = wT[:, u, half * RB:(half + 1) * RB, :].rearrange("p b t -> p (b t)")
                for jj in range(JG):
                    states = st[:, n, jj, :, :].rearrange("p b t -> p (b t)")
                    last = nc.vector.tensor_tensor_scan(states, decays, states, 0.0, ALU.mult, ALU.add)
                last.then_inc(scanned, 1)
                if n * JG // JQ == POOL_SUM:
                    return
                dve.wait_ge(scanned, g + 1)
                states = st[:, n, :, :, :].rearrange("p j b t -> p j (b t)")
                nc.vector.tensor_tensor(states, states, rT[:, u, half, :].unsqueeze(1).to_broadcast([P, JG, RT]),
                                        ALU.mult).then_inc(read_ready, 1)

            def add_bonus(s, u):
                dve.wait_ge(bonus_sum_ready, s + 1)
                nc.vector.tensor_tensor(bonus_v[:, :, :], vT[:, u, :, :],
                                        tr[:, 0:RT].unsqueeze(1).to_broadcast([P, HALVES, RT]),
                                        ALU.mult).then_inc(o_bonus, 1)

            def add_up(s):
                dve.wait_ge(o_bonus, s + 1)
                dve.wait_ge(summed, s * SUMS + SUMS)
                if later(s):
                    dve.wait_ge(oT_ready, s)
                nc.vector.tensor_tensor(o[:, :], o_bank, bonus_v[:, :, :].rearrange("p h t -> p (h t)"),
                                        ALU.add).then_inc(o_ready, 1)

            def centre(s):
                dve.wait_ge(oT_ready, s + 1)
                nc.vector.tensor_reduce(out=mean[:, :].rearrange("p (c h) -> p c h", c=CH),
                                        in_=small.rearrange("p (c j h) -> p c h j", c=CH, j=RS),
                                        op=ALU.add, axis=AX.X).then_inc(mean_ready, 1)
                dve.wait_ge(mean_ready, s + 1)
                for c in range(CH):
                    last = nc.vector.scalar_tensor_tensor(
                        out=core.o[:, ds(s * CH + c, C)].rearrange("p (j h) -> p j h", j=RS),
                        in0=mean[:, c * RH:(c + 1) * RH].unsqueeze(1).to_broadcast([P, RS, RH]), scalar=-1.0 / RS,
                        in1=small[:, c * C:(c + 1) * C].rearrange("p (j h) -> p j h", j=RS), op0=ALU.mult, op1=ALU.add)
                last.then_inc(o_stored, 1)

            def sum_squares(s):
                dve.wait_ge(sq_ready, s + 1)
                nc.vector.tensor_reduce(out=core.var[:, ds(s, CH * RH)].rearrange("p (c h) -> p c h", c=CH),
                                        in_=o_sq[:, :].rearrange("p (c j h) -> p c h j", c=CH, j=RS),
                                        op=ALU.add, axis=AX.X).then_inc(var_stored, 1)

            def body(s, u, more, more2):
                if later(s):
                    add_up(s - 1)
                for n in range(GROUPS_R):
                    recur(s, u, n)
                    if n == 0 and more:
                        mixer_input(s + 1)
                    if n == 2:
                        add_bonus(s, u)
                    if n in (2, 3, 4, 5, 6) and more:
                        mix(s + 1, n - 2)
                    if n == 1:
                        gate(s)
                    if n == 6 and later(s - 1):
                        sum_squares(s - 2)
                    if n == 7 and later(s):
                        centre(s - 1)

            nc.vector.memset(mixer_b[:, :], 0.0).then_inc(mixer_cleared, 1)
            nc.vector.memset(wT[:, :, :, 0], 0.0)
            for half in range(HALVES):
                last = nc.vector.tensor_scalar(u_sum[:, half, :], core.head_sum[:, half, :], col(core, "u", half), None,
                                               ALU.mult)
            last.then_inc(u_ready, 1)
            mixer_input(0)
            for m in range(NMIX):
                mix(0, m)
            bodies(dve, body)
            add_up(RUNS - 1)
            sum_squares(RUNS - 2)
            centre(RUNS - 1)
            sum_squares(RUNS - 1)


def run_pairs(eng, body):
    body(0, 0)
    body(1, 1)
    with eng.Fori(1, RUNS // 2 - 2) as i:
        body(2 * i, 0)
        body(2 * i + 1, 1)
    for s in range(RUNS - 4, RUNS):
        body(s, s % 2)


def run_there(s):
    return not isinstance(s, int) or s < RUNS


def gate_phase(core):
    nc = core.nc
    with ExitStack() as ctx:
        def sb(name, shape):
            return ctx.enter_context(nc.sbuf_tensor(f"gate_{name}", shape, FP32))

        rstd = sb("rstd", [P, TILES * RH])
        on = sb("on", [P, 2, CH * C])
        onT = sb("onT", [P, 2, HALVES * RT])
        yT = sb("yT", [P, 2, HALVES * RT])
        tr, proj = core.banks[0:2], core.banks[2:4]
        (std_ready, rstd_ready, on_ready, onT_ready, onT_copied, y_ready, proj_ready, x_ready) = semaphores(
            nc, ctx, *(f"gate_{s}" for s in ("std_ready", "rstd_ready", "on_ready", "onT_ready", "onT_copied",
                                             "y_ready", "proj_ready", "x_ready")))
        block = ctx.enter_context(nc.Block())

        @block.gpsimd
        def _(pool):
            def scale(s, u):
                pool.wait_ge(rstd_ready, s + 1)
                if later(s - 1):
                    pool.wait_ge(onT_ready, s - 1)
                heads = rstd[:, ds(s, CH * RH)].rearrange("p (c h) -> p c h", c=CH)
                nc.gpsimd.tensor_tensor(on[:, u, :].rearrange("p (c j h) -> p c j h", c=CH, j=RS),
                                        core.o[:, ds(s, CH * C)].rearrange("p (c j h) -> p c j h", c=CH, j=RS),
                                        heads.unsqueeze(2).to_broadcast([P, CH, RS, RH]), ALU.mult).then_inc(on_ready, 1)

            run_pairs(pool, scale)

        @block.tensor
        def _(pe):
            def transpose(s, u):
                pe.wait_ge(on_ready, s + 1)
                if later(s - 1):
                    pe.wait_ge(onT_copied, s - 1)
                for half in range(HALVES):
                    for c in range(CH):
                        a = half * RT + c * P
                        last = nc.tensor.transpose(tr[u][:, a:a + P], on[:, u, c * C + half * P:c * C + (half + 1) * P],
                                                   core.ident[:, :])
                last.then_inc(onT_ready, 1)

            def project(s, u):
                pe.wait_ge(y_ready, s + 1)
                if later(s - 1):
                    pe.wait_ge(x_ready, s - 1)
                for c in range(CH):
                    for kb in range(HALVES):
                        a = kb * RT + c * P
                        last = nc.tensor.matmul(proj[u][:, c * C:(c + 1) * C], yT[:, u, a:a + P], core.w["WoT"][:, kb, :],
                                                start=(kb == 0), stop=(kb == HALVES - 1))
                last.then_inc(proj_ready, 1)

            def body(s, u):
                if run_there(s + 2):
                    transpose(s + 2, u)
                project(s, u)

            transpose(0, 0)
            transpose(1, 1)
            run_pairs(pe, body)

        @block.scalar
        def _(act):
            def copy(s, u):
                act.wait_ge(onT_ready, s + 1)
                if later(s - 1):
                    act.wait_ge(y_ready, s - 1)
                for half in range(HALVES):
                    last = nc.scalar.activation(onT[:, u, half * RT:(half + 1) * RT],
                                                tr[u][:, half * RT:(half + 1) * RT],
                                                ACT.Identity, scale=col(core, "gn_w", half), bias=col(core, "gn_b", half))
                last.then_inc(onT_copied, 1)

            nc.scalar.activation(rstd[:, :], core.var[:, :], ACT.Sqrt, scale=1.0 / RS,
                                 bias=core.eps[:, :]).then_inc(std_ready, 1)
            run_pairs(act, copy)

        @block.vector
        def _(dve):
            def invert(s):
                std = rstd[:, ds(s, CH * RH)]
                nc.vector.reciprocal(std, std).then_inc(rstd_ready, 1)

            def gate(s, u):
                dve.wait_ge(onT_copied, s + 1)
                if later(s - 1):
                    dve.wait_ge(proj_ready, s - 1)
                nc.vector.scalar_tensor_tensor(out=yT[:, u, :], in0=onT[:, u, :], scalar=0.5,
                                               in1=core.gate[:, ds(s, HALVES * RT)], op0=ALU.mult,
                                               op1=ALU.mult).then_inc(y_ready, 1)

            def add_residual(s, u):
                dve.wait_ge(proj_ready, s + 1)
                xs = core.x[:, ds(s, CH * C)]
                nc.vector.tensor_tensor(xs, proj[u], xs, ALU.add).then_inc(x_ready, 1)

            def make_stats(s):
                dve.wait_ge(x_ready, s + 1)
                for c in range(CH):
                    t = s * CH + c
                    nc.vector.bn_stats(core.stats[:, ds(t, 6)], core.x[:, ds(t, C)])

            def body(s, u):
                if later(s):
                    add_residual(s - 1, 1 - u)
                if run_there(s + 1):
                    gate(s + 1, 1 - u)
                if run_there(s + 4):
                    invert(s + 4)
                if later(s):
                    make_stats(s - 1)

            dve.wait_ge(std_ready, 1)
            for s in range(4):
                invert(s)
            gate(0, 0)
            run_pairs(dve, body)
            add_residual(RUNS - 1, 1)
            make_stats(RUNS - 1)


def channel_phase(core, out):
    nc = core.nc
    w = core.w
    with ExitStack() as ctx:
        def sb(name, shape):
            return ctx.enter_context(nc.sbuf_tensor(f"ch_{name}", shape, FP32))

        xn = sb("xn", [P, 2, CH, C])
        xc = sb("xc", [P, 2, HALVES, RB, S + 1])
        sx = sb("sx", [P, HALVES, RB, S])
        xk, xr = sb("xk", [P, 2, HALVES, RT]), sb("xr", [P, 2, HALVES, RT])
        relu = sb("relu", [P, 2, HALVES * RT])
        kk = sb("kk", [P, 2, HALVES * RT])
        rr = sb("rr", [P, 2, CH * C])
        tr, key, recept, value = (core.banks[2 * i:2 * i + 2] for i in range(4))
        names = ("xn_ready xnT_ready xc_ready first_slot sx_ready mixed_ready key_ready relu_ready kk_ready recept_ready "
                 "rr_ready value_ready rv_ready out_ready stored").split()
        (xn_ready, xnT_ready, xc_ready, first_slot, sx_ready, mixed_ready, key_ready, relu_ready, kk_ready, recept_ready,
         rr_ready, value_ready, rv_ready, out_ready, stored) = semaphores(nc, ctx, *(f"ch_{n}" for n in names))
        block = ctx.enter_context(nc.Block())

        @block.sync
        def _(sp):
            with sp.Fori(0, RUNS) as s:
                sp.wait_ge(out_ready, s + 1)
                sp.dma_start(out[:, ds(s, CH * C)], core.x[:, ds(s, CH * C)]).then_inc(stored, 16)
            sp.wait_ge(stored, 16 * RUNS)

        @block.gpsimd
        def _(pool):
            def square(s, u):
                pool.wait_ge(relu_ready, s + 1)
                if later(s):
                    pool.wait_ge(kk_ready, s)
                if later(s - 1):
                    pool.wait_ge(value_ready, s - 1)
                nc.gpsimd.tensor_tensor(kk[:, u, :], relu[:, u, :], relu[:, u, :], ALU.mult).then_inc(kk_ready, 1)

            run_pairs(pool, square)

        @block.tensor
        def _(pe):
            def transpose(s, u):
                pe.wait_ge(xn_ready, s + 1)
                if later(s - 1):
                    pe.wait_ge(xc_ready, s - 1)
                for half in range(HALVES):
                    for c in range(CH):
                        a = half * RT + c * P
                        last = nc.tensor.transpose(tr[u][:, a:a + P], xn[:, u, c, half * P:(half + 1) * P],
                                                   core.ident[:, :])
                last.then_inc(xnT_ready, 1)

            def keys(s, u):
                pe.wait_ge(mixed_ready, s + 1)
                if later(s - 1):
                    pe.wait_ge(relu_ready, s - 1)
                for half in range(HALVES):
                    for kb in range(HALVES):
                        last = nc.tensor.matmul(key[u][:, half * RT:(half + 1) * RT],
                                                w["WfkT"][:, kb, half * P:(half + 1) * P], xk[:, u, kb, :],
                                                start=(kb == 0), stop=(kb == HALVES - 1))
                last.then_inc(key_ready, 1)

            def receptances(s, u):
                if later(s - 1):
                    pe.wait_ge(rr_ready, s - 1)
                for c in range(CH):
                    for kb in range(HALVES):
                        last = nc.tensor.matmul(recept[u][:, c * C:(c + 1) * C], xr[:, u, kb, c * P:(c + 1) * P],
                                                w["WfrT"][:, kb, :], start=(kb == 0), stop=(kb == HALVES - 1))
                last.then_inc(recept_ready, 1)

            def values(s, u):
                pe.wait_ge(kk_ready, s + 1)
                if later(s - 1):
                    pe.wait_ge(rv_ready, s - 1)
                for c in range(CH):
                    for kb in range(HALVES):
                        a = kb * RT + c * P
                        last = nc.tensor.matmul(value[u][:, c * C:(c + 1) * C], kk[:, u, a:a + P],
                                                w["WfvT"][:, kb, :], start=(kb == 0), stop=(kb == HALVES - 1))
                last.then_inc(value_ready, 1)

            def body(s, u):
                if run_there(s + 2):
                    transpose(s + 2, u)
                if run_there(s + 1):
                    keys(s + 1, 1 - u)
                values(s, u)
                if run_there(s + 1):
                    receptances(s + 1, 1 - u)

            transpose(0, 0)
            transpose(1, 1)
            keys(0, 0)
            receptances(0, 0)
            run_pairs(pe, body)

        @block.scalar
        def _(act):
            def copy_in(s, u):
                act.wait_ge(xnT_ready, s + 1)
                if later(s - 1):
                    act.wait_ge(mixed_ready, s - 1)
                for half in range(HALVES):
                    last = nc.scalar.activation(xc[:, u, half, :, 1:S + 1],
                                                tr[u][:, half * RT:(half + 1) * RT].rearrange("p (b t) -> p b t", t=S),
                                                ACT.Identity, scale=col(core, "r_ln2_w", half),
                                                bias=col(core, "r_ln2_b", half))
                last.then_inc(xc_ready, 1)

            def nonlinear(s, u):
                act.wait_ge(key_ready, s + 1)
                if later(s - 1):
                    act.wait_ge(kk_ready, s - 1)
                nc.scalar.activation(relu[:, u, :], key[u], ACT.Relu).then_inc(relu_ready, 1)
                act.wait_ge(recept_ready, s + 1)
                if later(s - 1):
                    act.wait_ge(out_ready, s - 1)
                nc.scalar.activation(rr[:, u, :], recept[u], ACT.Sigmoid).then_inc(rr_ready, 1)

            def body(s, u):
                if run_there(s + 2):
                    copy_in(s + 2, u)
                if run_there(s + 1):
                    nonlinear(s + 1, 1 - u)

            copy_in(0, 0)
            copy_in(1, 1)
            nonlinear(0, 0)
            run_pairs(act, body)

        @block.vector
        def _(dve):
            def normalise(s, u):
                if later(s - 1):
                    dve.wait_ge(xnT_ready, s - 1)
                for c in range(CH):
                    t = s * CH + c
                    last = nc.vector.tensor_scalar(xn[:, u, c, :], core.x[:, ds(t, C)], core.rstd[:, ds(t, 1)],
                                                   core.neg_mean[:, ds(t, 1)], ALU.mult, ALU.add)
                last.then_inc(xn_ready, 1)

            def shift(s, u):
                nc.vector.tensor_copy(xc[:, u, :, :, 0], core.state_rows[:, 0, :, ds(s, RB)]).then_inc(first_slot, 1)
                dve.wait_ge(xc_ready, s + 1)
                dve.wait_ge(first_slot, s + 1)
                nc.vector.tensor_tensor(sx[:, :, :, :].rearrange("p h b t -> p (h b) t"),
                                        xc[:, u, :, :, 0:S].rearrange("p h b t -> p (h b) t"),
                                        xc[:, u, :, :, 1:S + 1].rearrange("p h b t -> p (h b) t"),
                                        ALU.subtract).then_inc(sx_ready, 1)
                dve.wait_ge(sx_ready, s + 1)
                if later(s - 1):
                    dve.wait_ge(key_ready, s - 1)
                    dve.wait_ge(recept_ready, s - 1)
                for half in range(HALVES):
                    for dst, name in ((xk, "ffn_maa_k"), (xr, "ffn_maa_r")):
                        last = nc.vector.scalar_tensor_tensor(
                            out=dst[:, u, half, :].rearrange("p (b t) -> p b t", t=S), in0=sx[:, half, :, :],
                            scalar=col(core, name, half), in1=xc[:, u, half, :, 1:S + 1], op0=ALU.mult, op1=ALU.add)
                last.then_inc(mixed_ready, 1)

            def finish(s, u):
                dve.wait_ge(value_ready, s + 1)
                dve.wait_ge(rr_ready, s + 1)
                nc.vector.tensor_tensor(rr[:, u, :], value[u], rr[:, u, :], ALU.mult).then_inc(rv_ready, 1)
                dve.wait_ge(rv_ready, s + 1)
                xs = core.x[:, ds(s, CH * C)]
                nc.vector.tensor_tensor(xs, rr[:, u, :], xs, ALU.add).then_inc(out_ready, 1)

            def body(s, u):
                if later(s):
                    finish(s - 1, 1 - u)
                if run_there(s + 2):
                    shift(s + 2, u)
                if run_there(s + 3):
                    normalise(s + 3, 1 - u)

            normalise(0, 0)
            normalise(1, 1)
            shift(0, 0)
            normalise(2, 0)
            shift(1, 1)
            run_pairs(dve, body)
            finish(RUNS - 1, 1)


FIRST_WEIGHTS = {"w_qkv": (2, 3 * C), "w_ao": (2, C), "w_q": (2, C), "w_kv": (2, 2 * C), "w_co": (2, C),
                 "w1": (2, F1), "w2": (8, C)}
SECOND_WEIGHTS = {"maa_w1": (2, NMIX * DM), "td_w1": (2, DD), "WrT": (2, C), "WkT": (2, C), "WvT": (2, C),
                  "WgT": (2, C), "WoT": (2, C), "WfkT": (2, C), "WfrT": (2, C), "WfvT": (2, C)}


def build(nc, dram, out):
    core = Core()
    core.nc, core.dram = nc, dram
    with ExitStack() as ctx:
        def sb(name, shape, scope=ctx):
            return scope.enter_context(nc.sbuf_tensor(name, shape, FP32))

        def weights(table, scope):
            for k, (kb, n) in table.items():
                core.weights[k] = sb(k, [P, kb * n], scope)
                core.w[k] = core.weights[k][:, :].rearrange("p (k n) -> p k n", k=kb)

        core.weights, core.w = {}, {}
        core.x = sb("x", [P, TILES * C])
        core.cols = sb("cols", [P, NCOLS])
        core.ident = sb("ident", [P, P])
        core.stats = sb("stats", [P, TILES * 6])
        core.norm_tmp = sb("norm_tmp", [P, 3, TILES])
        core.neg_mean = sb("neg_mean", [P, TILES])
        core.rstd = sb("rstd", [P, TILES])
        core.eps = sb("eps", [P, 1])
        core.psum = ctx.enter_context(nc.psum_tensor("psum", [P, 8 * 512], FP32))
        core.banks = [core.psum[:, i * 512:(i + 1) * 512] for i in range(8)]

        core.head_sum = sb("head_sum", [P, HALVES, P])
        core.spread = sb("spread", [P, RS, P])
        core.maa_w2a, core.maa_w2b = sb("maa_w2a", [P, C]), sb("maa_w2b", [P, CH, C])
        core.td_w2 = sb("td_w2", [P, CH, C])
        core.state_rows = sb("state_rows", [P, 2, HALVES, B])
        core.state0 = sb("state0", [P, HALVES * RS, B])
        weights(SECOND_WEIGHTS, ctx)
        phases = ("self", "cross", "gelu", "recurrent")
        core.loaded = dict(zip(phases, semaphores(nc, ctx, *(f"{phase}_weights_loaded" for phase in phases))))

        with ExitStack() as first:
            core.rows = sb("rows", [P, 3, C], first)
            core.parity = sb("parity", [P, 2], first)
            core.q_bias = sb("q_bias", [P, 2, HALVES], first)
            core.k_heads = sb("k_heads", [P, HALVES * BPT, PAIRS, S], first)
            core.self_mask = sb("self_mask", [P, S], first)
            core.self_bias = sb("self_bias", [P, S], first)
            core.cross_mask = sb("cross_mask", [P, TILES * S], first)
            core.cross_bias = sb("cross_bias", [P, TILES * S], first)
            core.vpad = sb("vpad", [P, PAIRS, BPT * PW], first)
            weights(FIRST_WEIGHTS, first)
            load_phase(core, dram)
            norm_phase(core, "norm1", "self")
            attention_phase(core, False)
            norm_phase(core, "norm2", "cross")
            attention_phase(core, True)
            norm_phase(core, "norm3", "gelu")
            gelu_phase(core)

        core.o = sb("o", [P, TILES * C])
        core.gate = sb("gate", [P, TILES * C])
        core.var = sb("var", [P, TILES * RH])
        norm_phase(core, "norm4", "recurrent")
        recurrence_phase(core)
        gate_phase(core)
        norm_phase(core, "norm5")
        channel_phase(core, out)


def lay_out(inputs):
    a = {k: np.asarray(v) for k, v in inputs.items()}
    L0, L1 = "L0_xattn_", "L1_xattn_"

    def per_channel(v):
        return v.reshape(-1, P).T

    def by_value_column(v):
        return v.reshape(RH, RS, -1).swapaxes(0, 1).reshape(v.shape)

    def rows(w):
        return np.ascontiguousarray(w.reshape(-1, P, w.shape[1]).transpose(1, 0, 2).reshape(P, -1))

    b_qkv, b_kv = a[L0 + "b_qkv"], a[L0 + "b_kv"]
    vectors = {"ln1_s": a[L0 + "ln1_s"], "ln1_b": a[L0 + "ln1_b"], "b_q_self": b_qkv[:C], "b_k_self": b_qkv[C:2 * C],
               "b_v_self": b_qkv[2 * C:], "ln2_s": a[L0 + "ln2_s"], "ln2_b": a[L0 + "ln2_b"],
               "b_q_cross": a[L0 + "b_q"], "b_k_cross": b_kv[:C], "b_v_cross": b_kv[C:], "ln3_s": a[L0 + "ln3_s"],
               "ln3_b": a[L0 + "ln3_b"], "b1": a[L0 + "b1"], "r_ln1_w": a[L1 + "ln1_w"], "r_ln1_b": a[L1 + "ln1_b"],
               "r_ln2_w": a[L1 + "ln2_w"], "r_ln2_b": a[L1 + "ln2_b"], "maa_x": a[L1 + "maa_x"],
               "maa_stack": a[L1 + "maa_stack"].reshape(-1), "time_decay": a[L1 + "time_decay"],
               "u": a[L1 + "u"].reshape(-1), "gn_w": by_value_column(a[L1 + "gn_w"]),
               "gn_b": by_value_column(a[L1 + "gn_b"]),
               "ffn_maa_k": a[L1 + "ffn_maa_k"], "ffn_maa_r": a[L1 + "ffn_maa_r"]}
    ctx = a["ctx_2048"]
    p = np.arange(P)
    out = {
        "x": rows(a["x"].reshape(B * S, C)),
        "cols": np.ascontiguousarray(np.concatenate([per_channel(vectors[k]) for k in COLS], axis=1)),
        "rows": np.ascontiguousarray(np.stack([a[L0 + "b_ao"], a[L0 + "b_co"], a[L0 + "b2"]])),
        "enc": np.ascontiguousarray(ctx.reshape(B * S, HALVES, P).transpose(2, 1, 0)),
        "cross_mask": rows(a["mask_Bx1xSxS2_ff1"].reshape(B * S, S)),
        "self_mask": np.ascontiguousarray(np.concatenate([a["mask_1x1xSxS2_fc1"].reshape(S, S)] * 2)),
        "ident": np.eye(P, dtype=np.float32),
        "parity": np.ascontiguousarray(((p[:, None] // HD) % 2 == np.arange(2)[None, :]).astype(np.float32)),
    }
    to_rows = [p[None, :] % RH == half * HPH + p[:, None] // RS for half in range(HALVES)]
    out["head_sum"] = np.ascontiguousarray(np.stack(to_rows, axis=1).astype(np.float32))
    out["spread"] = np.ascontiguousarray(np.stack(
        [(to_rows[half].T & (p[:, None] // RH == jl)).astype(np.float32) for half in range(HALVES) for jl in range(JQ)],
        axis=1))
    out["maa_w2"] = np.ascontiguousarray(a[L1 + "maa_w2"].reshape(NMIX * DM, C))
    out["td_w2"] = np.ascontiguousarray(a[L1 + "td_w2"])
    out["state_rows"] = np.ascontiguousarray(ctx[:, 0:2, :].reshape(B, 2, HALVES, P).transpose(3, 1, 2, 0))
    out["state0"] = np.ascontiguousarray(
        ctx[:, 2:2 + RS, :].reshape(B, HALVES, P, RS).transpose(2, 1, 3, 0).reshape(P, HALVES * RS, B))
    for k in FIRST_WEIGHTS:
        out[k] = rows(a[L0 + k])
    for k in SECOND_WEIGHTS:
        w = a[L1 + k[:-1]] if k[0] == "W" else a[L1 + k]
        if k in ("WvT", "WgT"):
            w = by_value_column(w)
        out[k] = rows(by_value_column(w.T) if k == "WoT" else w.T) if k[0] == "W" else rows(w)
    return out


def kernel(**inputs):
    import concourse.bacc as bacc
    from concourse.bass_utils import run_bass_kernel_spmd

    nc = bacc.Bacc("TRN2", target_bir_lowering=False, num_devices=1)
    arrays = lay_out(inputs)
    dram = {k: nc.dram_tensor(f"in_{k}", v.shape, mybir.dt.from_np(v.dtype), kind="ExternalInput").ap()
            for k, v in arrays.items()}
    out = nc.dram_tensor("out", [P, TILES * C], FP32, kind="ExternalOutput").ap()
    build(nc, dram, out)
    result = run_bass_kernel_spmd(nc, [{f"in_{k}": v for k, v in arrays.items()}], core_ids=[0]).results[0]["out"]
    return np.ascontiguousarray(result.reshape(P, TILES, C).transpose(1, 0, 2).reshape(B, S, C))
```
